# Optimizing a Trainium2 kernel written in Bass

```python
import numpy as np
import jax
import jax.numpy as jnp

def _softmax(x, axis=-1):
    return jax.nn.softmax(x, axis=axis)

def _gelu(x):
    return jax.nn.gelu(x, approximate=True)

def _silu(x):
    return jax.nn.silu(x)

def _sigmoid(x):
    return jax.nn.sigmoid(x)

def _layernorm(x, axis=-1, eps=1e-05):
    m = jnp.mean(x, axis=axis, keepdims=True)
    v = jnp.var(x, axis=axis, keepdims=True)
    return (x - m) / jnp.sqrt(v + eps)

def _scatter_add(tgt, idx, src, axis=0):
    return tgt.at[idx].add(src)

def _segment_sum(src, seg, n):
    return jax.ops.segment_sum(src, seg, n)
kernel_name = 'mk_metaformer_d2_conv_nchw768_r4_c6d681'

def setup_inputs(seed: int=0):
    np.random.seed(seed)
    _w = jnp.asarray

    def _rec_inputs():
        import jax
        import jax.numpy as jnp
        _gk = jax.random.key(seed)
        x = -0.0001538 + 1 * jax.random.normal(jax.random.fold_in(_gk, 1), (8, 192, 32, 32), jnp.float32)
        return x
    x = _rec_inputs()

    def _L0_conv_setup():
        import jax, jax.numpy as jnp
        import numpy as np
        B, C, H, W = (8, 192, 32, 32)
        CO, KS = (192, 3)

        def _conv(x, w, b):
            y = jax.lax.conv_general_dilated(x, w, (1, 1), [(1, 1), (1, 1)], dimension_numbers=('NCHW', 'OIHW', 'NCHW'))
            return y + b[None, :, None, None]

        def _deform_conv(x, offset, mask, w, b):
            b_, c_, h_, w_ = x.shape
            co, _, kh, kw = w.shape
            K = kh * kw
            off = offset.reshape(b_, K, 2, h_, w_)
            ky = (jnp.arange(K) // kw).astype(x.dtype)
            kx = (jnp.arange(K) % kw).astype(x.dtype)
            py = off[:, :, 0] + (jnp.arange(h_, dtype=x.dtype) - 1.0)[None, None, :, None] + ky[None, :, None, None]
            px = off[:, :, 1] + (jnp.arange(w_, dtype=x.dtype) - 1.0)[None, None, None, :] + kx[None, :, None, None]
            y0 = jnp.floor(py)
            x0 = jnp.floor(px)
            wy1 = py - y0
            wx1 = px - x0
            y0i = y0.astype(jnp.int32)
            x0i = x0.astype(jnp.int32)

            def corner(yi, xi, wt):
                valid = (yi >= 0) & (yi < h_) & (xi >= 0) & (xi < w_)
                yc = jnp.clip(yi, 0, h_ - 1)
                xc = jnp.clip(xi, 0, w_ - 1)
                g = jax.vmap(lambda im, yy, xx: im[:, yy, xx])(x, yc, xc)
                return g * (wt * valid)[:, None]
            p = corner(y0i, x0i, (1.0 - wy1) * (1.0 - wx1) * mask) + corner(y0i, x0i + 1, (1.0 - wy1) * wx1 * mask) + corner(y0i + 1, x0i, wy1 * (1.0 - wx1) * mask) + corner(y0i + 1, x0i + 1, wy1 * wx1 * mask)
            out = jnp.einsum('bckhw,ock->bohw', p, w.reshape(co, c_, K))
            return out + b[None, :, None, None]
        key = jax.random.key(seed)
        ks = jax.random.split(key, 6)
        x = jax.random.normal(ks[0], (B, C, H, W), jnp.float32)
        proj_w = jax.random.normal(ks[1], (CO, C, KS, KS), jnp.float32) * 0.02
        proj_b = jnp.zeros((CO,), jnp.float32)
        off_w = jax.random.normal(ks[2], (2 * KS * KS, C, KS, KS), jnp.float32) * 0.01
        off_b = jax.random.normal(ks[3], (2 * KS * KS,), jnp.float32) * 0.01
        mask_w = jax.random.normal(ks[4], (KS * KS, C, KS, KS), jnp.float32) * 0.01
        mask_b = jax.random.normal(ks[5], (KS * KS,), jnp.float32) * 0.01
        gamma = jnp.ones((CO,), jnp.float32)
        beta = jnp.zeros((CO,), jnp.float32)
        return {'x': x, 'proj_w': proj_w, 'proj_b': proj_b, 'off_w': off_w, 'off_b': off_b, 'mask_w': mask_w, 'mask_b': mask_b, 'gamma': gamma, 'beta': beta}
    _L0_conv_all = _L0_conv_setup()
    _L0_conv_in = {k: v for k, v in _L0_conv_all.items() if k in ('proj_w', 'proj_b', 'off_w', 'off_b', 'mask_w', 'mask_b', 'gamma', 'beta')}
    del _L0_conv_all

    def _L0_ffn_setup():
        import jax, jax.numpy as jnp
        import numpy as np
        N_EMBD = 192
        EXPERT_SIZES = [(8, 128), (8, 256)]
        TOP_K = 8
        NORM_TOPK_PROB = True
        EXPERT_WIDTHS = []
        for cnt, w in EXPERT_SIZES:
            EXPERT_WIDTHS += [w] * cnt
        EXPERT_OFFSETS = np.concatenate([[0], np.cumsum(EXPERT_WIDTHS)]).astype(np.int64)
        NUM_EXPERTS = len(EXPERT_WIDTHS)
        TOTAL_WIDTH = int(EXPERT_OFFSETS[-1])
        key = jax.random.key(seed)
        k1, k2, k3, k4 = jax.random.split(key, 4)
        x = jax.random.normal(k1, (1, 512, N_EMBD), dtype=jnp.float32)
        router_w = jax.random.normal(k2, (NUM_EXPERTS, N_EMBD), dtype=jnp.float32) * 0.02
        w1 = jnp.clip(jax.random.normal(k3, (N_EMBD, TOTAL_WIDTH), dtype=jnp.float32) * 0.02, -0.06, 0.06)
        w2 = jnp.clip(jax.random.normal(k4, (TOTAL_WIDTH, N_EMBD), dtype=jnp.float32) * 0.02, -0.06, 0.06)
        return {'x': x, 'router_w': router_w, 'w1': w1, 'w2': w2}
    _L0_ffn_all = _L0_ffn_setup()
    _L0_ffn_in = {k: v for k, v in _L0_ffn_all.items() if k in ('router_w', 'w1', 'w2')}
    del _L0_ffn_all

    def _L1_conv_setup():
        import jax, jax.numpy as jnp
        import numpy as np
        DIM = 192
        HEADS = 12
        B, C, H, W = (32, DIM, 32, 32)
        key = jax.random.key(seed)
        k1, k2, k3, k4 = jax.random.split(key, 4)
        x = jax.random.normal(k1, (B, C, H, W), dtype=jnp.float32)
        scale = 1.0 / np.sqrt(DIM)
        qkv_w = jax.random.normal(k2, (DIM, DIM), dtype=jnp.float32) * scale
        temp = jnp.ones((HEADS, 1), dtype=jnp.float32)
        out_w = jax.random.normal(k3, (DIM, DIM), dtype=jnp.float32) * scale
        out_b = jax.random.normal(k4, (DIM,), dtype=jnp.float32) * 0.01
        return {'x': x, 'qkv_w': qkv_w, 'temp': temp, 'out_w': out_w, 'out_b': out_b}
    _L1_conv_all = _L1_conv_setup()
    _L1_conv_in = {k: v for k, v in _L1_conv_all.items() if k in ('qkv_w', 'temp', 'out_w', 'out_b')}
    del _L1_conv_all

    def _L1_ffn_setup():
        import jax, jax.numpy as jnp
        import numpy as np
        B, S, D = (4, 256, 192)
        E = 8
        H = 192
        HS = 768
        TOPK_ROUTED = 2
        key = jax.random.key(seed)
        ks = jax.random.split(key, 10)
        w = lambda k, shape: jax.random.normal(k, shape, dtype=jnp.float32) * 0.02
        return {'x': jax.random.normal(ks[0], (B, S, D), dtype=jnp.float32), 'router_w': w(ks[1], (D, E)), 'w_gate': w(ks[2], (E, D, H)), 'w_up': w(ks[3], (E, D, H)), 'w_down': w(ks[4], (E, H, D)), 'ws_gate': w(ks[5], (D, HS)), 'ws_up': w(ks[6], (D, HS)), 'ws_down': w(ks[7], (HS, D)), 'sg_w': w(ks[8], (D, 1)), 'sg_b': jnp.zeros((1,), jnp.float32)}
    _L1_ffn_all = _L1_ffn_setup()
    _L1_ffn_in = {k: v for k, v in _L1_ffn_all.items() if k in ('router_w', 'w_gate', 'w_up', 'w_down', 'ws_gate', 'ws_up', 'ws_down', 'sg_w', 'sg_b')}
    del _L1_ffn_all
    return {'x': x, 'L0_conv_proj_w': _L0_conv_in['proj_w'], 'L0_conv_proj_b': _L0_conv_in['proj_b'], 'L0_conv_off_w': _L0_conv_in['off_w'], 'L0_conv_off_b': _L0_conv_in['off_b'], 'L0_conv_mask_w': _L0_conv_in['mask_w'], 'L0_conv_mask_b': _L0_conv_in['mask_b'], 'L0_conv_gamma': _L0_conv_in['gamma'], 'L0_conv_beta': _L0_conv_in['beta'], 'L0_ffn_router_w': _L0_ffn_in['router_w'], 'L0_ffn_w1': _L0_ffn_in['w1'], 'L0_ffn_w2': _L0_ffn_in['w2'], 'L1_conv_qkv_w': _L1_conv_in['qkv_w'], 'L1_conv_temp': _L1_conv_in['temp'], 'L1_conv_out_w': _L1_conv_in['out_w'], 'L1_conv_out_b': _L1_conv_in['out_b'], 'L1_ffn_router_w': _L1_ffn_in['router_w'], 'L1_ffn_w_gate': _L1_ffn_in['w_gate'], 'L1_ffn_w_up': _L1_ffn_in['w_up'], 'L1_ffn_w_down': _L1_ffn_in['w_down'], 'L1_ffn_ws_gate': _L1_ffn_in['ws_gate'], 'L1_ffn_ws_up': _L1_ffn_in['ws_up'], 'L1_ffn_ws_down': _L1_ffn_in['ws_down'], 'L1_ffn_sg_w': _L1_ffn_in['sg_w'], 'L1_ffn_sg_b': _L1_ffn_in['sg_b']}

def reference(x, L0_conv_proj_w, L0_conv_proj_b, L0_conv_off_w, L0_conv_off_b, L0_conv_mask_w, L0_conv_mask_b, L0_conv_gamma, L0_conv_beta, L0_ffn_router_w, L0_ffn_w1, L0_ffn_w2, L1_conv_qkv_w, L1_conv_temp, L1_conv_out_w, L1_conv_out_b, L1_ffn_router_w, L1_ffn_w_gate, L1_ffn_w_up, L1_ffn_w_down, L1_ffn_ws_gate, L1_ffn_ws_up, L1_ffn_ws_down, L1_ffn_sg_w, L1_ffn_sg_b):
    import jax
    import jax.numpy as jnp

    def _L0_conv_ref(x, proj_w, proj_b, off_w, off_b, mask_w, mask_b, gamma, beta):
        import jax, jax.numpy as jnp
        import numpy as np
        B, C, H, W = (8, 192, 32, 32)
        CO, KS = (192, 3)

        def _conv(x, w, b):
            y = jax.lax.conv_general_dilated(x, w, (1, 1), [(1, 1), (1, 1)], dimension_numbers=('NCHW', 'OIHW', 'NCHW'))
            return y + b[None, :, None, None]

        def _deform_conv(x, offset, mask, w, b):
            b_, c_, h_, w_ = x.shape
            co, _, kh, kw = w.shape
            K = kh * kw
            off = offset.reshape(b_, K, 2, h_, w_)
            ky = (jnp.arange(K) // kw).astype(x.dtype)
            kx = (jnp.arange(K) % kw).astype(x.dtype)
            py = off[:, :, 0] + (jnp.arange(h_, dtype=x.dtype) - 1.0)[None, None, :, None] + ky[None, :, None, None]
            px = off[:, :, 1] + (jnp.arange(w_, dtype=x.dtype) - 1.0)[None, None, None, :] + kx[None, :, None, None]
            y0 = jnp.floor(py)
            x0 = jnp.floor(px)
            wy1 = py - y0
            wx1 = px - x0
            y0i = y0.astype(jnp.int32)
            x0i = x0.astype(jnp.int32)

            def corner(yi, xi, wt):
                valid = (yi >= 0) & (yi < h_) & (xi >= 0) & (xi < w_)
                yc = jnp.clip(yi, 0, h_ - 1)
                xc = jnp.clip(xi, 0, w_ - 1)
                g = jax.vmap(lambda im, yy, xx: im[:, yy, xx])(x, yc, xc)
                return g * (wt * valid)[:, None]
            p = corner(y0i, x0i, (1.0 - wy1) * (1.0 - wx1) * mask) + corner(y0i, x0i + 1, (1.0 - wy1) * wx1 * mask) + corner(y0i + 1, x0i, wy1 * (1.0 - wx1) * mask) + corner(y0i + 1, x0i + 1, wy1 * wx1 * mask)
            out = jnp.einsum('bckhw,ock->bohw', p, w.reshape(co, c_, K))
            return out + b[None, :, None, None]
        h, w = (x.shape[-2], x.shape[-1])
        max_off = float(min(h, w) // 4)
        offset = jnp.clip(_conv(x, off_w, off_b), -max_off, max_off)
        mask = 2.0 * jax.nn.sigmoid(_conv(x, mask_w, mask_b))
        y = _deform_conv(x, offset, mask, proj_w, proj_b)
        mean = y.mean(axis=(0, 2, 3))
        var = y.var(axis=(0, 2, 3))
        yn = (y - mean[None, :, None, None]) * jax.lax.rsqrt(var + 1e-05)[None, :, None, None]
        yn = yn * gamma[None, :, None, None] + beta[None, :, None, None]
        return jax.nn.gelu(yn, approximate=False)

    def _L0_ffn_ref(x, router_w, w1, w2):
        import jax, jax.numpy as jnp
        import numpy as np
        N_EMBD = 192
        EXPERT_SIZES = [(8, 128), (8, 256)]
        TOP_K = 8
        NORM_TOPK_PROB = True
        EXPERT_WIDTHS = []
        for cnt, w in EXPERT_SIZES:
            EXPERT_WIDTHS += [w] * cnt
        EXPERT_OFFSETS = np.concatenate([[0], np.cumsum(EXPERT_WIDTHS)]).astype(np.int64)
        NUM_EXPERTS = len(EXPERT_WIDTHS)
        TOTAL_WIDTH = int(EXPERT_OFFSETS[-1])
        B, S, D = x.shape
        xt = x.reshape(-1, D)
        T = xt.shape[0]
        logits = jnp.einsum('td,ed->te', xt, router_w)
        probs = jax.nn.softmax(logits, axis=-1)
        topk_w, topk_idx = jax.lax.top_k(probs, TOP_K)
        if NORM_TOPK_PROB:
            topk_w = topk_w / jnp.sum(topk_w, axis=-1, keepdims=True)
        comb = jnp.zeros((T, NUM_EXPERTS), dtype=xt.dtype)
        comb = comb.at[jnp.arange(T)[:, None], topk_idx].add(topk_w)
        out = jnp.zeros_like(xt)
        for e in range(NUM_EXPERTS):
            off = int(EXPERT_OFFSETS[e])
            wd = EXPERT_WIDTHS[e]
            h = jax.nn.gelu(xt @ w1[:, off:off + wd])
            out = out + comb[:, e:e + 1] * (h @ w2[off:off + wd, :])
        return out.reshape(B, S, D)

    def _L1_conv_ref(x, qkv_w, temp, out_w, out_b):
        import jax, jax.numpy as jnp
        import numpy as np
        DIM = 192
        HEADS = 12
        B, C, H, W = (32, DIM, 32, 32)
        b, c, hh, ww = x.shape
        n = hh * ww
        d = c // HEADS
        xt = x.reshape(b, c, n).transpose(0, 2, 1)
        w = jnp.einsum('bnc,oc->bno', xt, qkv_w).reshape(b, n, HEADS, d).transpose(0, 2, 1, 3)
        norm = jnp.sqrt(jnp.sum(w * w, axis=-2, keepdims=True))
        w_normed = w / jnp.maximum(norm, 1e-12)
        s = jnp.sum(w_normed * w_normed, axis=-1)
        Pi = jax.nn.softmax(s * temp[None, :, :], axis=1)
        Pi_n = Pi / (jnp.sum(Pi, axis=-1, keepdims=True) + 1e-08)
        dots = jnp.einsum('bhn,bhnd->bhd', Pi_n, w * w)[:, :, None, :]
        attn = 1.0 / (1.0 + dots)
        out = -(w * Pi[..., None]) * attn
        out = out.transpose(0, 2, 1, 3).reshape(b, n, c)
        out = jnp.einsum('bnc,oc->bno', out, out_w) + out_b
        return out.transpose(0, 2, 1).reshape(b, c, hh, ww)

    def _L1_ffn_ref(x, router_w, w_gate, w_up, w_down, ws_gate, ws_up, ws_down, sg_w, sg_b):
        import jax, jax.numpy as jnp
        import numpy as np
        B, S, D = (4, 256, 192)
        E = 8
        H = 192
        HS = 768
        TOPK_ROUTED = 2
        probs = jax.nn.softmax(x @ router_w, axis=-1)
        gates, idx = jax.lax.top_k(probs, TOPK_ROUTED)
        gates = gates / jnp.sum(gates, axis=-1, keepdims=True)
        n_exp = router_w.shape[1]
        dense_g = jnp.sum(jax.nn.one_hot(idx, n_exp, dtype=x.dtype) * gates[..., None], axis=-2)
        g = jax.nn.silu(jnp.einsum('bsd,edh->bseh', x, w_gate))
        u = jnp.einsum('bsd,edh->bseh', x, w_up)
        expert_out = jnp.einsum('bseh,ehd->bsed', g * u, w_down)
        routed = jnp.einsum('bse,bsed->bsd', dense_g, expert_out)
        shared = jax.nn.silu(x @ ws_gate) * (x @ ws_up) @ ws_down
        alpha = jax.nn.sigmoid(x @ sg_w + sg_b)
        return alpha * shared + (1.0 - alpha) * routed

    def _gn(v, G=32, eps=1e-05):
        B_, C_, H_, W_ = v.shape
        g = v.reshape(B_, G, C_ // G, H_, W_)
        m = jnp.mean(g, axis=(2, 3, 4), keepdims=True)
        s = jnp.var(g, axis=(2, 3, 4), keepdims=True)
        return ((g - m) / jnp.sqrt(s + eps)).reshape(v.shape)

    def _ln_c(v, eps=1e-06):
        m = jnp.mean(v, axis=1, keepdims=True)
        s = jnp.var(v, axis=1, keepdims=True)
        return (v - m) / jnp.sqrt(s + eps)

    def _ln_t(v, eps=1e-05):
        m = jnp.mean(v, axis=-1, keepdims=True)
        s = jnp.var(v, axis=-1, keepdims=True)
        return (v - m) / jnp.sqrt(s + eps)

    def _to_tokens(v):
        B_, C_, H_, W_ = v.shape
        return v.reshape(B_, C_, H_ * W_).transpose(0, 2, 1)

    def _from_tokens(t, like):
        B_, C_, H_, W_ = like.shape
        return t.transpose(0, 2, 1).reshape(B_, C_, H_, W_)
    x = x + _L0_conv_ref(_ln_c(x), L0_conv_proj_w, L0_conv_proj_b, L0_conv_off_w, L0_conv_off_b, L0_conv_mask_w, L0_conv_mask_b, L0_conv_gamma, L0_conv_beta)
    t = _to_tokens(x)
    t = t + _L0_ffn_ref(_ln_t(t), L0_ffn_router_w, L0_ffn_w1, L0_ffn_w2)
    x = _from_tokens(t, x)
    x = x + _L1_conv_ref(_ln_c(x), L1_conv_qkv_w, L1_conv_temp, L1_conv_out_w, L1_conv_out_b)
    t = _to_tokens(x)
    t = t + _L1_ffn_ref(_ln_t(t), L1_ffn_router_w, L1_ffn_w_gate, L1_ffn_w_up, L1_ffn_w_down, L1_ffn_ws_gate, L1_ffn_ws_up, L1_ffn_ws_down, L1_ffn_sg_w, L1_ffn_sg_b)
    x = _from_tokens(t, x)
    return x

_drawn_inputs = setup_inputs


def setup_inputs(seed=0):
    import zlib

    import numpy as np

    out = dict(_drawn_inputs(seed))
    spreads = {'L0_conv_proj_b': (0.0, 0.8),
     'L0_conv_gamma': (1.0, 0.2),
     'L0_conv_beta': (0.0, 0.1),
     'L1_conv_temp': (1.0, 0.6)}
    factors = {'L0_conv_off_b': 3.265,
     'L0_ffn_router_w': 6.647,
     'L0_ffn_w1': 4.836,
     'L0_ffn_w2': 4.73,
     'L1_conv_out_b': 7.287,
     'L1_ffn_router_w': 8.0,
     'L1_ffn_w_gate': 8.0,
     'L1_ffn_w_up': 8.0,
     'L1_ffn_w_down': 8.0,
     'L1_ffn_ws_gate': 6.274,
     'L1_ffn_ws_up': 6.218,
     'L1_ffn_ws_down': 6.219,
     'L1_ffn_sg_w': 8.0}
    for name, (base, spread) in spreads.items():
        noise = np.random.default_rng([zlib.crc32(name.encode()), seed]).standard_normal(out[name].shape)
        drawn = base * np.exp(spread * noise) if base else spread * noise
        out[name] = jnp.asarray(drawn.astype(out[name].dtype))
    for name, factor in factors.items():
        out[name] = (out[name] * factor).astype(out[name].dtype)
    return out
```

```python
from contextlib import ExitStack

import concourse.bass as bass
from concourse import mybir
import numpy as np

ALU = mybir.AluOpType
ACT = mybir.ActivationFunctionType
AX = mybir.AxisListType
F32 = mybir.dt.float32
F16 = mybir.dt.float16
I32 = mybir.dt.int32

P = 128
NIMG, H, W, C = 8, 32, 32, 192
CA, CB = 128, 64
NTOK = NIMG * H * W
T = NTOK // P
TI = T // NIMG
ROWS = P // W
HP = H + 2
K9 = 9
NOM = 27
FRONT = W + 1
MAXOFF = float(H // 4)
CONV_K = K9 * C
CONV_M = -(-CONV_K // P)
E0, E1 = 16, 8
W0_WIDTHS = [128] * 8 + [256] * 8
HID0 = sum(W0_WIDTHS)
HID1R, HID1S = E1 * 192, 768
HID1 = HID1R + HID1S
CHUNK = 512
TC = CHUNK // P
NCHUNK = NTOK // CHUNK
HEADS, DH = 12, 16
LG = 16


class Count:

    def __init__(self, eng, sem):
        self.eng, self.sem, self.n = eng, sem, 0

    def mark(self, ins):
        ins.then_inc(self.sem, 1)
        self.n = self.n + 1

    def wait(self):
        self.eng.wait_ge(self.sem, self.n)

    def link(self, ins):
        self.mark(ins)
        self.wait()


class Kit:
    def __init__(self, nc, ctx, tag):
        self.nc, self.ctx, self.tag = nc, ctx, tag

    def sb(self, name, shape, dt=F32):
        return self.ctx.enter_context(self.nc.sbuf_tensor(f"{self.tag}_{name}", shape, dt))

    def ps(self, name, shape=(P, 512), dt=F32):
        return self.ctx.enter_context(self.nc.psum_tensor(f"{self.tag}_{name}", list(shape), dt))

    def sem(self, name):
        return self.ctx.enter_context(self.nc.semaphore(f"{self.tag}_{name}"))


def bc(ap, n):
    return ap.unsqueeze(2).to_broadcast([ap.shape[0], ap.shape[1], n])


def at(t, n=1):
    return bass.ds(t, n)


def finish_stats(dve, ch, st, mean, var, tmp, eps):
    me, qe, mo, qo = st[:, :, 1], st[:, :, 2], st[:, :, 4], st[:, :, 5]
    ch.link(dve.tensor_tensor(tmp[:], me, mo, ALU.subtract))
    dve.tensor_tensor(mean[:], me, mo, ALU.add)
    ch.link(dve.tensor_tensor(var[:], qe, qo, ALU.add))
    ch.link(dve.tensor_tensor(tmp[:], tmp[:], tmp[:], ALU.mult))
    dve.tensor_scalar(mean[:], mean[:], 0.5, None, ALU.mult)
    ch.link(dve.tensor_scalar(var[:], var[:], 1.0 / C, float(eps), ALU.mult, ALU.add))
    ch.link(dve.scalar_tensor_tensor(out=var[:], in0=tmp[:], scalar=0.25, in1=var[:],
                                     op0=ALU.mult, op1=ALU.add))


def stage_offsets(nc, io, X, ident, om, table):
    with ExitStack() as ctx:
        k = Kit(nc, ctx, "off")
        st = k.sb("st", [P, T, 6])
        mean, rstd, tmp = k.sb("mean", [P, T]), k.sb("rstd", [P, T]), k.sb("tmp", [P, T])
        RING = 4
        xd = k.sb("xd", [P, RING, 2 * P])
        pad_hi = k.sb("pad_hi", [P, 2, 3, HP, W], F16)
        pad_lo = k.sb("pad_lo", [P, 2, 3, HP, W], F16)
        pad_b = k.sb("pad_b", [P, 2, 3, HP, W], F16)
        wf = k.sb("wf", [P, 2, K9, NOM])
        w_a = k.sb("w_a", [P, K9, 2, NOM], F16)
        w_b = k.sb("w_b", [P, K9, 2, NOM], F16)
        omlo = k.sb("omlo", [P, 2, TI, NOM])
        zero = k.sb("zero", [FRONT, 4 * C])
        ps_t = [k.ps(f"t{i}") for i in range(RING)]
        ps_c = [k.ps(f"c{i}") for i in range(2)]
        s_img = [k.sem(f"image_loaded{b}") for b in range(NIMG)]
        s_w = k.sem("weights_loaded")
        s_const = k.sem("constants_set")
        s_ch, s_stats = k.sem("dve_chain"), k.sem("stats_ready")
        s_var, s_sd, s_xd = k.sem("variance_ready"), k.sem("std_ready"), k.sem("tile_normalised")
        s_tab = [k.sem(f"table_written{i}") for i in range(RING)]
        s_border = k.sem("table_border")
        s_tp, s_hi, s_lo = k.sem("transposed"), k.sem("hi_ready"), k.sem("lo_ready")
        s_shift, s_shift_hi = k.sem("shifted"), k.sem("hi_shifted")
        SHIFTS = ((0, slice(1, W), slice(0, W - 1)), (2, slice(0, W - 1), slice(1, W)))
        s_wsplit = k.sem("weights_split")
        s_conv, s_cfree, s_cl = k.sem("conv_done"), k.sem("conv_psum_free"), k.sem("conv_lo_copied")
        block = ctx.enter_context(nc.Block())

        @block.sync
        def _(sp):
            for b in range(NIMG):
                sp.dma_start(X[:, b * TI:(b + 1) * TI, :], io["x"][b * TI * P:(b + 1) * TI * P, :]
                             .rearrange("(t p) c -> p t c", p=P)).then_inc(s_img[b], 16)
            ow = io["om_w"].rearrange("c (k o) -> c k o", k=K9)
            sp.dma_start(wf[:, 0], ow[0:CA]).then_inc(s_w, 16)
            sp.dma_start(wf[0:CB, 1], ow[CA:C]).then_inc(s_w, 16)
            sp.dma_start(wf[CB:P, 1], ow[CA:C]).then_inc(s_w, 16)
            sp.wait_ge(s_const, 1)
            sp.dma_start(table[NTOK:NTOK + FRONT], zero[:]).then_inc(s_border, 16)
            sp.dma_start(table[0:FRONT], zero[:]).then_inc(s_border, 16)
            sp.wait_ge(s_border, 32)

            with sp.Fori(0, T // RING) as q:
                for r in range(RING):
                    t = q * RING + r
                    sp.wait_ge(s_xd, t + 1)
                    sp.wait_ge(s_const, 1)
                    for n in range(4):
                        row = t * P + FRONT - (n // 2) * W - n % 2
                        sp.dma_start(table[at(row, P), n * C:(n + 1) * C], xd[:, r, 0:C]).then_inc(s_tab[r], 16)
            for r in range(RING):
                sp.wait_ge(s_tab[r], 4 * 16 * (T // RING))

        @block.gpsimd
        def _(pool):
            nc.gpsimd.memset(zero[:], 0.0).then_inc(s_const, 1)
            for pad in (pad_hi, pad_lo, pad_b):
                last = nc.gpsimd.memset(pad[:], 0.0)
            last.then_inc(s_const, 1)

        @block.vector
        def _(dve):
            ch = Count(dve, s_ch)
            for b in range(NIMG):
                dve.wait_ge(s_img[b], 16)
                with dve.Fori(b * TI, (b + 1) * TI) as t:
                    nc.vector.bn_stats(st[:, at(t), :], X[:, at(t), :]).then_inc(s_stats, 1)
            dve.wait_ge(s_stats, T)
            finish_stats(nc.vector, ch, st, mean, rstd, tmp, 1e-6)
            dve.sem_inc(s_var, 1)
            dve.wait_ge(s_w, 48)
            nc.vector.tensor_copy(w_a[:, :, 0, :], wf[:, 0])
            nc.vector.tensor_copy(w_b[:, :, 0, :], wf[:, 1])
            ch.link(nc.vector.memset(w_b[CB:P, :, 1, :], 0.0))
            nc.vector.tensor_tensor(w_a[:, :, 1, :], wf[:, 0], w_a[:, :, 0, :], ALU.subtract)
            nc.vector.tensor_tensor(w_b[0:CB, :, 1, :], wf[0:CB, 1], w_b[0:CB, :, 0, :], ALU.subtract).then_inc(s_wsplit, 1)
            dve.wait_ge(s_sd, 1)
            ch.link(nc.vector.reciprocal(rstd[:], rstd[:]))

            def normalise(t, r, q):
                dve.wait_ge(s_tab[r], 4 * 16 * q)
                m, s = mean[:, at(t)], rstd[:, at(t)]
                nc.vector.tensor_scalar(xd[:, r, 0:C], X[:, at(t), :], m, s, ALU.subtract, ALU.mult)
                nc.vector.tensor_scalar(xd[:, r, C:2 * P], X[:, at(t), CA:C], m, s, ALU.subtract,
                                        ALU.mult).then_inc(s_xd, 1)

            def low(t, u, j):
                dve.wait_ge(s_hi, t + 1)
                rows = slice(1 + j * ROWS, 1 + (j + 1) * ROWS)
                a = ps_t[j % RING][:, 0:P].rearrange("p (r x) -> p r x", x=W)
                b = ps_t[j % RING][CB:P, P:2 * P].rearrange("p (r x) -> p r x", x=W)
                nc.vector.tensor_tensor(pad_lo[:, u, 1, rows], a, pad_hi[:, u, 1, rows], ALU.subtract)
                pb = pad_b[CB:P, u, 1, rows]
                nc.vector.tensor_tensor(pb, b, pb, ALU.subtract).then_inc(s_lo, 1)

            def image(g, u):
                for j in range(TI + 2):
                    if j < TI:
                        normalise(g * TI + j, j % RING, g * (TI // RING) + j // RING)
                    if j >= 2:
                        low(g * TI + j - 2, u, j - 2)
                dve.wait_ge(s_lo, RING + (g + 1) * TI)
                for pad in (pad_lo, pad_b):
                    for kx, dst, src in SHIFTS:
                        last = nc.vector.tensor_copy(pad[:, u, kx, 1:1 + H, dst], pad[:, u, 1, 1:1 + H, src])
                last.then_inc(s_shift, 1)

            def gather_conv(g, u):
                dve.wait_ge(s_cl, g + 1)
                src = ps_c[u][:, 0:TI * 2 * NOM].rearrange("p (t s o) -> p t s o", s=2, o=NOM)[:, :, 0, :]
                nc.vector.tensor_tensor(om[:, at(g * TI, TI), :], src, omlo[:, u], ALU.add).then_inc(s_cfree, 1)

            image(0, 0)
            with dve.Fori(0, NIMG // 2 - 1) as i:
                image(2 * i + 1, 1)
                gather_conv(2 * i, 0)
                image(2 * i + 2, 0)
                gather_conv(2 * i + 1, 1)
            image(NIMG - 1, 1)
            gather_conv(NIMG - 2, 0)
            gather_conv(NIMG - 1, 1)

        @block.scalar
        def _(act):
            act.wait_ge(s_var, 1)
            nc.scalar.activation(rstd[:], rstd[:], ACT.Sqrt).then_inc(s_sd, 1)
            act.wait_ge(s_const, 2)

            def image(g, u):
                act.wait_ge(s_conv, g + 1)
                for j in range(TI):
                    act.wait_ge(s_tp, g * TI + j + 1)
                    rows = slice(1 + j * ROWS, 1 + (j + 1) * ROWS)
                    a = ps_t[j % RING][:, 0:P].rearrange("p (r x) -> p r x", x=W)
                    b = ps_t[j % RING][:, P:2 * P].rearrange("p (r x) -> p r x", x=W)
                    nc.scalar.activation(pad_hi[:, u, 1, rows], a, ACT.Copy)
                    nc.scalar.activation(pad_b[:, u, 1, rows], b, ACT.Copy).then_inc(s_hi, 1)
                act.wait_ge(s_hi, (g + 1) * TI)
                for kx, dst, src in SHIFTS:
                    last = nc.scalar.activation(pad_hi[:, u, kx, 1:1 + H, dst], pad_hi[:, u, 1, 1:1 + H, src], ACT.Copy)
                last.then_inc(s_shift_hi, 1)

            def conv_low(g, u):
                act.wait_ge(s_conv, 2 + g + 1)
                act.wait_ge(s_cfree, g + 1)
                src = ps_c[u][:, 0:TI * 2 * NOM].rearrange("p (t s o) -> p t s o", s=2, o=NOM)[:, :, 1, :]
                nc.scalar.activation(omlo[:, u], src, ACT.Copy).then_inc(s_cl, 1)

            image(0, 0)
            with act.Fori(0, NIMG // 2 - 1) as i:
                image(2 * i + 1, 1)
                conv_low(2 * i, 0)
                image(2 * i + 2, 0)
                conv_low(2 * i + 1, 1)
            image(NIMG - 1, 1)
            conv_low(NIMG - 2, 0)
            conv_low(NIMG - 1, 1)

        @block.tensor
        def _(pe):
            pe.sem_inc(s_lo, RING)
            pe.sem_inc(s_cfree, 2)
            pe.sem_inc(s_conv, 2)
            pe.wait_ge(s_wsplit, 1)

            def image(g, u):
                for j in range(TI):
                    t = g * TI + j
                    pe.wait_ge(s_xd, t + 1)
                    pe.wait_ge(s_lo, t + 1)
                    nc.tensor.transpose(ps_t[j % RING][:, 0:P], xd[:, j % RING, 0:P], ident[:])
                    ins = nc.tensor.transpose(ps_t[j % RING][:, P:2 * P], xd[:, j % RING, P:2 * P], ident[:])
                    ins.then_inc(s_tp, 1)

            def conv(g, u):
                pe.wait_ge(s_shift_hi, g + 1)
                pe.wait_ge(s_shift, g + 1)
                pe.wait_ge(s_cfree, g + 1)
                for j in range(TI):
                    o = j * 2 * NOM
                    for tap in range(K9):
                        ky, kx = tap // 3, tap % 3
                        first = j == 0 and tap == 0
                        for n, (pad, wt, cols) in enumerate(((pad_hi, w_a, 2), (pad_b, w_b, 2), (pad_lo, w_a, 1))):
                            last = nc.tensor.matmul(ps_c[u][:, o:o + cols * NOM], pad[:, u, kx].rearrange("p y x -> p (y x)")
                                                    [:, (j * ROWS + ky) * W:(j * ROWS + ky) * W + P],
                                                    wt[:, tap, 0:cols, :], start=(first and n == 0),
                                                    stop=(tap == K9 - 1 and n == 2), skip_group_check=True)
                last.then_inc(s_conv, 1)

            image(0, 0)
            with pe.Fori(0, NIMG // 2 - 1) as i:
                image(2 * i + 1, 1)
                conv(2 * i, 0)
                image(2 * i + 2, 0)
                conv(2 * i + 1, 1)
            image(NIMG - 1, 1)
            conv(NIMG - 2, 0)
            conv(NIMG - 1, 1)


def stage_corners(nc, io, om, grid, wts, idx):
    with ExitStack() as ctx:
        k = Kit(nc, ctx, "crn")
        N = T * K9
        bias = k.sb("bias", [P, 1, NOM])
        flat = {n: k.sb(n, [P, N]) for n in ("by", "bx", "t", "y0", "y1", "x0", "x1", "m")}
        fl = k.sb("fl", [P, N], I32)
        s_in, s_ch, s_z, s_m = k.sem("loaded"), k.sem("dve_chain"), k.sem("mask_logits"), k.sem("mask_ready")
        block = ctx.enter_context(nc.Block())

        @block.sync
        def _(sp):
            sp.dma_start(bias[:, 0, :], io["om_b"].to_broadcast([P, NOM])).then_inc(s_in, 16)
            sp.dma_start(grid[:], io["grid"]).then_inc(s_in, 16)

        @block.scalar
        def _(act):
            act.wait_ge(s_z, 1)
            nc.scalar.activation(flat["m"][:], flat["m"][:], ACT.Sigmoid).then_inc(s_m, 1)

        @block.vector
        def _(dve):
            v = nc.vector
            ch = Count(dve, s_ch)
            dve.wait_ge(s_in, 32)
            ch.link(v.tensor_tensor(om[:], om[:], bias[:].to_broadcast([P, T, NOM]), ALU.add))
            tk = lambda ap: ap.rearrange("p (t k) -> p t k", k=K9)
            ch.link(v.tensor_copy(tk(flat["m"][:]), om[:, :, 2 * K9:NOM]))
            dve.sem_inc(s_z, 1)
            t = flat["t"][:]
            for d in range(2):
                w0, w1, b = ((flat["y0"], flat["y1"], flat["by"]), (flat["x0"], flat["x1"], flat["bx"]))[d]
                w0, w1, b = w0[:], w1[:], b[:]
                ch.link(v.tensor_scalar(tk(w0), om[:, :, d:2 * K9:2], -MAXOFF, MAXOFF, ALU.max, ALU.min))
                ch.link(v.tensor_tensor(w0, w0, grid[:, d], ALU.add))
                ch.link(v.tensor_copy(fl[:], w0))
                ch.link(v.tensor_copy(b, fl[:]))
                ch.link(v.tensor_tensor(t, b, w0, ALU.is_gt))
                ch.link(v.tensor_tensor(b, b, t, ALU.subtract))
                ch.link(v.tensor_scalar(b, b, 0.0, float(H - 1), ALU.max, ALU.min))
                ch.link(v.tensor_tensor(t, w0, b, ALU.subtract))
                ch.link(v.tensor_scalar(w0, t, -1.0, 1.0, ALU.mult, ALU.add))
                ch.link(v.scalar_tensor_tensor(out=w1, in0=w0, scalar=1.0, in1=t, op0=ALU.add, op1=ALU.min))
                ch.link(v.scalar_tensor_tensor(out=w0, in0=t, scalar=1.0, in1=w0, op0=ALU.add, op1=ALU.min))
                ch.link(v.tensor_scalar(w0, w0, 0.0, None, ALU.max))
                ch.link(v.tensor_scalar(t, b, float(H - 1), None, ALU.is_lt))
                ch.link(v.scalar_tensor_tensor(out=w1, in0=w1, scalar=0.0, in1=t, op0=ALU.max, op1=ALU.mult))
            ch.link(v.scalar_tensor_tensor(out=t, in0=flat["by"][:], scalar=float(W), in1=flat["bx"][:],
                                           op0=ALU.mult, op1=ALU.add))
            ch.link(v.tensor_tensor(t, t, grid[:, 2], ALU.add))
            v.tensor_copy(idx[:].rearrange("p t k -> p (t k)"), t)
            dve.wait_ge(s_m, 1)
            for y in ("y0", "y1"):
                ch.link(v.scalar_tensor_tensor(out=flat[y][:], in0=flat["m"][:], scalar=2.0, in1=flat[y][:],
                                               op0=ALU.mult, op1=ALU.mult))
            for n, (y, x) in enumerate((("y0", "x0"), ("y0", "x1"), ("y1", "x0"), ("y1", "x1"))):
                v.tensor_tensor(wts[:, :, :, n], tk(flat[y][:]), tk(flat[x][:]), ALU.mult)


def stage_deform(nc, io, table, wts, idx, Y, ones, ident, sums):
    with ExitStack() as ctx:
        k = Kit(nc, ctx, "dfm")
        gath = k.sb("gath", [P, 2, K9, 4 * C])
        samp = k.sb("samp", [P, 2, CONV_K])
        sampT = k.sb("sampT", [P, 2, CONV_M * P])
        wconv = k.sb("wconv", [P, CONV_M, C])
        wt = k.sb("wt", [P, 2, K9, 4])
        ix = k.sb("ix", [P, 2, K9], I32)
        ysq = k.sb("ysq", [P, 2, 2, C])
        ps_t = [k.ps(f"t{i}") for i in range(4)]
        ps_y = [k.ps(f"y{i}") for i in range(2)]
        ps_s = k.ps("s")
        s_w = k.sem("weights_loaded")
        s_g = [[k.sem(f"gathered{u}_{n}") for n in range(K9)] for u in range(2)]
        s_ix, s_first, s_samp = k.sem("tile_indices"), k.sem("first_corner"), k.sem("samples_ready")
        s_acc, s_sfree = k.sem("dve_accumulate"), k.sem("samples_free")
        s_turn, s_evac = k.sem("turned"), k.sem("turned_copied")
        s_conv, s_y, s_sum, s_zero, s_sums = k.sem("conv_done"), k.sem("y_ready"), k.sem("y_summed"), k.sem("sum_zeroed"), k.sem("sums")
        block = ctx.enter_context(nc.Block())
        BANKS = 4
        blocks = [list(range(4 * q, min(4 * q + 4, CONV_M))) for q in range(BANKS)]
        rows = lambda m: min(P, CONV_K - m * P)

        @block.sync
        def _(sp):
            full = (CONV_M - 1) * P
            sp.dma_start(wconv[:, 0:CONV_M - 1, :], io["conv_w"][0:full].rearrange("(m p) c -> p m c", p=P)).then_inc(s_w, 16)
            sp.dma_start(wconv[0:CONV_K - full, CONV_M - 1, :], io["conv_w"][full:CONV_K]).then_inc(s_w, 16)

        @block.gpsimd
        def _(pool):
            pool.wait_ge(s_zero, 1)
            with pool.Fori(0, T // 2) as i:
                for u in range(2):
                    t = 2 * i + u
                    pool.wait_ge(s_samp, t + 1)
                    pool.wait_ge(s_zero, 1)
                    nc.gpsimd.tensor_copy(ix[:, u, :], idx[:, at(t), :]).then_inc(s_ix, 1)
                    pool.wait_ge(s_zero, 1)
                    pool.wait_ge(s_ix, t + 1)
                    for n in range(K9):
                        nc.gpsimd.indirect_dma_start(
                            out=gath[:, u, n, :], out_offset=None, in_=table,
                            in_offset=bass.IndirectOffsetOnAxis(ap=ix[:, u, n:n + 1], axis=0)).then_inc(s_g[u][n], 16)

        @block.vector
        def _(dve):
            dve.sem_inc(s_samp, 2)
            nc.vector.memset(ysq[:, 0], 0.0).then_inc(s_zero, 1)

            with dve.Fori(0, T // 2) as i:
                for u in range(2):
                    t = 2 * i + u
                    per = K9 * 3
                    nc.vector.tensor_copy(wt[:, u], wts[:, at(t)]).then_inc(s_acc, 1)
                    dve.wait_ge(s_acc, t * (per + 1) + 1)
                    n_acc = t * (per + 1) + 1
                    for g0 in range(0, K9, 3):
                        dve.wait_ge(s_first, t * K9 + g0 + 3)
                        for c in range(1, 4):
                            if c > 1:
                                dve.wait_ge(s_acc, n_acc - 0)
                            for n in range(g0, g0 + 3):
                                s = samp[:, u, n * C:(n + 1) * C]
                                last = nc.vector.scalar_tensor_tensor(
                                    out=s, in0=gath[:, u, n, c * C:(c + 1) * C], scalar=wt[:, u, n, c:c + 1], in1=s,
                                    op0=ALU.mult, op1=ALU.add)
                                last.then_inc(s_acc, 1)
                                n_acc = n_acc + 1
                    dve.wait_ge(s_acc, n_acc)
                    dve.sem_inc(s_samp, 1)

        @block.scalar
        def _(act):
            act.sem_inc(s_sfree, 2)

            def first_corners(t, u, q):
                act.wait_ge(s_sfree, t + 1)
                act.wait_ge(s_acc, t * (3 * K9 + 1) + 1)
                for n in range(K9):
                    act.wait_ge(s_g[u][n], 16 * (q + 1))
                    nc.scalar.activation(samp[:, u, n * C:(n + 1) * C], gath[:, u, n, 0:C], ACT.Copy,
                                         scale=wt[:, u, n, 0:1]).then_inc(s_first, 1)

            def copy_turned(t, u):
                for q in range(BANKS):
                    act.wait_ge(s_turn, t * BANKS + q + 1)
                    full = [m for m in blocks[q] if rows(m) == P]
                    w = len(full) * P
                    last = nc.scalar.activation(sampT[:, u, 4 * q * P:4 * q * P + w], ps_t[q][:, 0:w], ACT.Copy)
                    for m in blocks[q]:
                        if rows(m) < P:
                            last = nc.scalar.activation(sampT[0:rows(m), u, m * P:(m + 1) * P],
                                                        ps_t[q][0:rows(m), w:w + P], ACT.Copy)
                    last.then_inc(s_evac, 1)

            def keep_y(t, u):
                act.wait_ge(s_conv, t + 1)
                act.wait_ge(s_sum, t + 1)
                nc.scalar.activation(ysq[:, u, 0], ps_y[u][:, 0:C], ACT.Copy)
                nc.scalar.activation(ysq[:, u, 1], ps_y[u][:, 0:C], ACT.Square)
                nc.scalar.activation(Y[:, at(t), :], ps_y[u][:, 0:C], ACT.Copy).then_inc(s_y, 1)

            first_corners(0, 0, 0)
            first_corners(1, 1, 0)
            copy_turned(0, 0)
            with act.Fori(1, T // 2) as i:
                for u in range(2):
                    first_corners(2 * i + u, u, i)
                    copy_turned(2 * i + u - 1, 1 - u)
                    keep_y(2 * i + u - 2, u)
            copy_turned(T - 1, 1)
            keep_y(T - 2, 0)
            keep_y(T - 1, 1)
            act.wait_ge(s_sums, 1)
            nc.scalar.activation(sums[:], ps_s[:, 0:2 * C], ACT.Copy)

        @block.tensor
        def _(pe):
            pe.wait_ge(s_zero, 1)
            nc.tensor.matmul(ps_s[:, 0:2 * C], ones[:], ysq[:, 0].rearrange("p a c -> p (a c)"), start=True, stop=False,
                             skip_group_check=True).then_inc(s_sum, 1)
            pe.sem_inc(s_sum, 1)
            pe.sem_inc(s_evac, BANKS)
            pe.wait_ge(s_w, 32)

            def turn(t, u):
                pe.wait_ge(s_samp, 2 + t + 1)
                for q in range(BANKS):
                    pe.wait_ge(s_evac, t * BANKS + q + 1)
                    for j, m in enumerate(blocks[q]):
                        last = nc.tensor.transpose(ps_t[q][0:rows(m), j * P:(j + 1) * P],
                                                   samp[:, u, m * P:m * P + rows(m)], ident[:])
                    last.then_inc(s_turn, 1)
                pe.wait_ge(s_turn, (t + 1) * BANKS)
                pe.sem_inc(s_sfree, 1)

            def conv(t, u):
                pe.wait_ge(s_evac, BANKS + (t + 1) * BANKS)
                pe.wait_ge(s_y, t + 1)
                for m in range(CONV_M):
                    last = nc.tensor.matmul(ps_y[u][:, 0:C], sampT[0:rows(m), u, m * P:(m + 1) * P],
                                            wconv[0:rows(m), m, :], start=(m == 0), stop=(m == CONV_M - 1))
                last.then_inc(s_conv, 1)

            def add_sums(t, u):
                pe.wait_ge(s_y, 2 + t + 1)
                return nc.tensor.matmul(ps_s[:, 0:2 * C], ones[:], ysq[:, u].rearrange("p a c -> p (a c)"),
                                        start=False, stop=False, skip_group_check=True).then_inc(s_sum, 1)

            pe.sem_inc(s_y, 2)
            turn(0, 0)
            turn(1, 1)
            conv(0, 0)
            with pe.Fori(1, T // 2) as i:
                for u in range(2):
                    turn(2 * i + u, u)
                    conv(2 * i + u - 1, 1 - u)
                    add_sums(2 * i + u - 2, u)
            conv(T - 1, 1)
            add_sums(T - 2, 0)
            add_sums(T - 1, 1)
            pe.wait_ge(s_sum, 2 + T)
            pe.sem_inc(s_sums, 1)


def stage_batchnorm(nc, io, X, Y, sums):
    with ExitStack() as ctx:
        k = Kit(nc, ctx, "bn")
        par = k.sb("par", [P, 3, C])
        mean, var, scale, shift = (k.sb(n, [P, 1, C]) for n in ("mean", "var", "scale", "shift"))
        s_in, s_ch, s_var, s_sd = k.sem("loaded"), k.sem("dve_chain"), k.sem("variance_ready"), k.sem("std_ready")
        s_z, s_gelu = k.sem("normalised"), k.sem("gelu_done")
        block = ctx.enter_context(nc.Block())
        GRP = 8

        @block.sync
        def _(sp):
            for n, name in enumerate(("gamma", "beta", "conv_b")):
                sp.dma_start(par[:, n, :], io[name].to_broadcast([P, C])).then_inc(s_in, 16)

        @block.vector
        def _(dve):
            v, ch = nc.vector, Count(dve, s_ch)
            m, q, sc, sh = mean[:, 0], var[:, 0], scale[:, 0], shift[:, 0]
            dve.wait_ge(s_in, 48)
            ch.link(v.tensor_scalar(m, sums[:, 0:C], 1.0 / NTOK, None, ALU.mult))
            ch.link(v.tensor_scalar(q, sums[:, C:2 * C], 1.0 / NTOK, None, ALU.mult))
            ch.link(v.tensor_tensor(sc, m, m, ALU.mult))
            ch.link(v.tensor_tensor(q, q, sc, ALU.subtract))
            ch.link(v.tensor_scalar(q, q, 0.0, 1e-5, ALU.max, ALU.add))
            dve.sem_inc(s_var, 1)
            ch.link(v.tensor_tensor(sh, m, par[:, 2], ALU.add))
            ch.link(v.tensor_tensor(sh, par[:, 2], sh, ALU.subtract))
            dve.wait_ge(s_sd, 1)
            ch.link(v.reciprocal(q, q))
            ch.link(v.tensor_tensor(sc, q, par[:, 0], ALU.mult))
            ch.link(v.tensor_tensor(sh, sh, sc, ALU.mult))
            ch.link(v.tensor_tensor(sh, sh, par[:, 1], ALU.add))

            def add_back(g):
                dve.wait_ge(s_gelu, g + 1)
                x = X[:, at(g * GRP, GRP), :]
                v.tensor_tensor(x, x, Y[:, at(g * GRP, GRP), :], ALU.add)

            def norm(g):
                y = Y[:, at(g * GRP, GRP), :]
                v.tensor_tensor(y, y, scale[:].to_broadcast([P, GRP, C]), ALU.mult).then_inc(s_z, 1)
                dve.wait_ge(s_z, 2 * g + 1)
                v.tensor_tensor(y, y, shift[:].to_broadcast([P, GRP, C]), ALU.add).then_inc(s_z, 1)

            norm(0)
            with dve.Fori(1, T // GRP) as g:
                norm(g)
                add_back(g - 1)
            add_back(T // GRP - 1)

        @block.scalar
        def _(act):
            act.wait_ge(s_var, 1)
            nc.scalar.activation(var[:, 0], var[:, 0], ACT.Sqrt).then_inc(s_sd, 1)
            with act.Fori(0, T // GRP) as g:
                act.wait_ge(s_z, 2 * g + 2)
                y = Y[:, at(g * GRP, GRP), :]
                nc.scalar.activation(y, y, ACT.Gelu).then_inc(s_gelu, 1)


def stage_route(nc, io, tag, X, xh, xl, xb, comb, ident, eps, router, nexp, topk, shared_bias=None):
    with ExitStack() as ctx:
        k = Kit(nc, ctx, tag)
        RING = 4
        NR = router.shape[1]
        st = k.sb("st", [P, T, 6])
        mean, rstd, tmp = k.sb("mean", [P, T]), k.sb("rstd", [P, T]), k.sb("tmp", [P, T])
        xd = k.sb("xd", [P, RING, 2 * P])
        xf = k.sb("xf", [P, RING, 2 * P])
        ra, rb = k.sb("ra", [P, NR]), k.sb("rb", [CB, NR])
        prob = k.sb("prob", [P, T, LG])
        rest = k.sb("rest", [P, T, LG])
        top = k.sb("top", [P, T, 8])
        red = k.sb("red", [P, T])
        sgb = k.sb("sgb", [P, 1])
        ps_t = [k.ps(f"t{i}") for i in range(RING)]
        ps_l = k.ps("logits", [P, T * LG])
        s_w, s_ch, s_stats = k.sem("router_loaded"), k.sem("dve_chain"), k.sem("stats_ready")
        s_var, s_sd, s_xd = k.sem("variance_ready"), k.sem("std_ready"), k.sem("tile_normalised")
        s_tp, s_hi, s_lo, s_log = k.sem("transposed"), k.sem("hi_ready"), k.sem("lo_ready"), k.sem("logits_ready")
        s_sub, s_exp, s_sgb = k.sem("logits_shifted"), k.sem("exp_done"), k.sem("bias_loaded")
        block = ctx.enter_context(nc.Block())

        @block.sync
        def _(sp):
            sp.dma_start(ra[:], router[0:CA]).then_inc(s_w, 16)
            sp.dma_start(rb[:], router[CA:C]).then_inc(s_w, 16)
            if shared_bias is not None:
                sp.dma_start(sgb[:], shared_bias.to_broadcast([P, 1])).then_inc(s_sgb, 16)

        @block.vector
        def _(dve):
            v, ch = nc.vector, Count(dve, s_ch)
            with dve.Fori(0, T // 8) as g:
                for j in range(8):
                    v.bn_stats(st[:, at(8 * g + j), :], X[:, at(8 * g + j), :]).then_inc(s_stats, 1)
            dve.wait_ge(s_stats, T)
            finish_stats(v, ch, st, mean, rstd, tmp, eps)
            dve.sem_inc(s_var, 1)
            dve.wait_ge(s_sd, 1)
            ch.link(v.reciprocal(rstd[:], rstd[:]))

            def normalise(t, r):
                m, s = mean[:, at(t)], rstd[:, at(t)]
                v.tensor_scalar(xd[:, r, 0:C], X[:, at(t), :], m, s, ALU.subtract, ALU.mult)
                v.tensor_scalar(xd[:, r, C:2 * P], X[:, at(t), CA:C], m, s, ALU.subtract, ALU.mult).then_inc(s_xd, 1)

            def low(t, r):
                dve.wait_ge(s_hi, t + 1)
                cols = at(t * P, P)
                v.tensor_tensor(xl[:, cols], ps_t[r][:, 0:P], xh[:, cols], ALU.subtract)
                v.tensor_tensor(xb[CB:P, cols], ps_t[r][CB:P, P:2 * P], xb[CB:P, cols], ALU.subtract).then_inc(s_lo, 1)

            SKEW = 2
            for t in range(RING):
                normalise(t, t)
                if t >= SKEW:
                    low(t - SKEW, t - SKEW)
            with dve.Fori(1, T // RING) as q:
                for r in range(RING):
                    normalise(RING * q + r, r)
                    low(RING * q + r - SKEW, (r - SKEW) % RING)
            for t in range(T - SKEW, T):
                low(t, t % RING)

            lg = ps_l[:].rearrange("p (t e) -> p t e", e=LG)
            dve.wait_ge(s_log, RING + T)
            ch.link(v.tensor_reduce(red[:], lg[:, :, 0:nexp], AX.X, ALU.max))
            ch.link(v.tensor_tensor(prob[:, :, 0:nexp], lg[:, :, 0:nexp], bc(red[:], nexp), ALU.subtract))
            if shared_bias is not None:
                dve.wait_ge(s_sgb, 16)
                ch.link(v.tensor_scalar(prob[:, :, nexp], lg[:, :, nexp], sgb[:, 0:1], -1.0, ALU.add, ALU.mult))
            dve.sem_inc(s_sub, 1)
            dve.wait_ge(s_exp, 1)
            if topk < 8:
                for j in range(8 - topk):
                    last = v.memset(prob[:, :, nexp + 1 + j:nexp + 2 + j], -2.0 - j)
                ch.link(last)
            width = nexp if topk == 8 else nexp + 1 + 8 - topk
            for t in range(T):
                last = v.max(top[:, t, :], prob[:, t, 0:nexp])
            ch.link(last)
            if topk < 8:
                for j in range(8 - topk):
                    last = v.memset(top[:, :, topk + j:topk + j + 1], -2.0 - j)
                ch.link(last)
            for t in range(T):
                last = v.match_replace(rest[:, t, 0:width], top[:, t, :], prob[:, t, 0:width], -1.0)
            ch.link(last)
            ch.link(v.scalar_tensor_tensor(out=comb[:, :, 0:nexp], in0=rest[:, :, 0:nexp], scalar=0.0,
                                           in1=prob[:, :, 0:nexp], op0=ALU.is_lt, op1=ALU.mult))
            ch.link(v.tensor_reduce(red[:], comb[:, :, 0:nexp], AX.X, ALU.add))
            ch.link(v.reciprocal(red[:], red[:]))
            if shared_bias is not None:
                ch.link(v.tensor_scalar(tmp[:], prob[:, :, nexp], 1.0, None, ALU.add))
                ch.link(v.reciprocal(tmp[:], tmp[:]))
                ch.link(v.tensor_copy(comb[:, :, nexp], tmp[:]))
                ch.link(v.tensor_scalar(tmp[:], tmp[:], -1.0, 1.0, ALU.mult, ALU.add))
                ch.link(v.tensor_tensor(red[:], red[:], tmp[:], ALU.mult))
            v.tensor_tensor(comb[:, :, 0:nexp], comb[:, :, 0:nexp], bc(red[:], nexp), ALU.mult)

        @block.scalar
        def _(act):
            act.wait_ge(s_var, 1)
            nc.scalar.activation(rstd[:], rstd[:], ACT.Sqrt).then_inc(s_sd, 1)
            with act.Fori(0, T // RING) as q:
                for r in range(RING):
                    t = RING * q + r
                    cols = at(t * P, P)
                    act.wait_ge(s_tp, t + 1)
                    act.wait_ge(s_log, t + 1)
                    nc.scalar.activation(xh[:, cols], ps_t[r][:, 0:P], ACT.Copy)
                    nc.scalar.activation(xb[:, cols], ps_t[r][:, P:2 * P], ACT.Copy)
                    nc.scalar.activation(xf[:, r, :], ps_t[r][:, 0:2 * P], ACT.Copy).then_inc(s_hi, 1)
            act.wait_ge(s_sub, 1)
            width = nexp + (shared_bias is not None)
            nc.scalar.activation(prob[:, :, 0:width], prob[:, :, 0:width], ACT.Exp).then_inc(s_exp, 1)

        @block.tensor
        def _(pe):
            pe.sem_inc(s_lo, RING)
            pe.sem_inc(s_log, RING)
            pe.wait_ge(s_w, 32)

            def turn(t, r):
                pe.wait_ge(s_xd, t + 1)
                pe.wait_ge(s_lo, t + 1)
                nc.tensor.transpose(ps_t[r][:, 0:P], xd[:, r, 0:P], ident[:])
                nc.tensor.transpose(ps_t[r][:, P:2 * P], xd[:, r, P:2 * P], ident[:]).then_inc(s_tp, 1)

            def logits(t, r):
                pe.wait_ge(s_hi, t + 1)
                out = ps_l[:, at(t * LG, NR)]
                nc.tensor.matmul(out, xf[:, r, 0:P], ra[:], start=True, stop=False)
                nc.tensor.matmul(out, xf[0:CB, r, P:2 * P], rb[:], start=False, stop=True).then_inc(s_log, 1)

            turn(0, 0)
            for t in range(1, RING):
                turn(t, t)
                logits(t - 1, t - 1)
            with pe.Fori(1, T // RING) as q:
                for r in range(RING):
                    turn(RING * q + r, r)
                    logits(RING * q + r - 1, (r - 1) % RING)
            logits(T - 1, RING - 1)


PIECE = 768


def split_parts(src, p0, hi, lo):
    n = src.shape[0]
    for c in range(0, src.shape[1], PIECE):
        d = min(c + PIECE, src.shape[1])
        yield src[:, c:d], p0, d - c, hi[p0:p0 + n, c:d], None if lo is None else lo[p0:p0 + n, c:d]


def split_up(src, wa_h, wa_l, wbb, wbl):
    yield from split_parts(src[0:CA], 0, wa_h, wa_l)
    yield from split_parts(src[CA:C], 0, wbb, wbl)
    yield from split_parts(src[CA:C], CB, wbb, None)


def split_down(src, hi, lo):
    step = PIECE // C
    for n in range(0, src.shape[0] // P, step):
        m = min(n + step, src.shape[0] // P)
        yield (src[n * P:m * P].rearrange("(n p) c -> p n c", p=P), 0, (m - n) * C,
               hi[:, n:m].rearrange("p n c -> p (n c)"), lo[:, n:m].rearrange("p n c -> p (n c)"))


def stage_split(nc, tag, parts):
    with ExitStack() as ctx:
        k = Kit(nc, ctx, tag)
        NB = 4
        buf = k.sb("buf", [P, NB, PIECE])
        s_in = [k.sem(f"loaded{i}") for i in range(NB)]
        s_hi, s_done = k.sem("hi_made"), k.sem("piece_split")
        block = ctx.enter_context(nc.Block())
        full = [n for n, part in enumerate(parts) if part[4] is not None]

        def piece(n):
            _, p0, w, hi, _ = parts[n]
            return buf[p0:p0 + hi.shape[0], n % NB, 0:w]

        @block.sync
        def _(sp):
            for n, (src, p0, w, hi, lo) in enumerate(parts):
                if n >= NB:
                    sp.wait_ge(s_done, n - NB + 1)
                dst = piece(n)
                if len(src.shape) == 3:
                    dst = dst.rearrange("p (n c) -> p n c", c=C)
                sp.dma_start(dst, src).then_inc(s_in[n % NB], 16)

        @block.scalar
        def _(act):
            for n in full:
                act.wait_ge(s_in[n % NB], 16 * (n // NB + 1))
                nc.scalar.activation(parts[n][3], piece(n), ACT.Copy).then_inc(s_hi, 1)

        @block.vector
        def _(dve):
            for n, (src, p0, w, hi, lo) in enumerate(parts):
                dve.wait_ge(s_in[n % NB], 16 * (n // NB + 1))
                if lo is None:
                    nc.vector.tensor_copy(hi, piece(n)).then_inc(s_done, 1)
                else:
                    dve.wait_ge(s_hi, full.index(n) + 1)
                    nc.vector.tensor_tensor(lo, piece(n), hi, ALU.subtract).then_inc(s_done, 1)


def stage_ffn(nc, tag, X, xh, xl, xb, comb, up, gate, down, groups, func, out=None):
    with ExitStack() as ctx:
        k = Kit(nc, ctx, tag)
        NH = down[0].shape[1]
        NE = len(groups)
        HB = 3
        hf = k.sb("hf", [P, HB, CHUNK])
        hg = k.sb("hg", [P, HB, CHUNK]) if gate else None
        hh = k.sb("hh", [P, HB, CHUNK], F16)
        hl = k.sb("hl", [P, HB, CHUNK], F16)
        acc = k.sb("acc", [P, TC, C])
        cb = k.sb("cb", [P, TC, LG])
        NPS = 2 if gate else 4
        ps_u = [k.ps(f"up{i}") for i in range(NPS)]
        ps_g = [k.ps(f"gate{i}") for i in range(NPS)] if gate else None
        ps_o = [[k.ps(f"out{i}{j}") for j in range(TC // 2)] for i in range(2)]
        s_up, s_gate = k.sem("up_ready"), k.sem("gate_ready")
        s_act, s_hf, s_hh, s_hl = k.sem("activated"), k.sem("hidden_ready"), k.sem("hi_ready"), k.sem("lo_ready")
        s_used, s_acc, s_cb = k.sem("hidden_used"), k.sem("accumulated"), k.sem("comb_copied")
        s_out = k.sem("stored")
        block = ctx.enter_context(nc.Block())
        uses = [[] for _ in range(NH)]
        for e, pieces in enumerate(groups):
            for n, (blk, r0, r1) in enumerate(pieces):
                uses[blk].append((e, r0, r1, n == 0, n == len(pieces) - 1))
        SKEW = 2

        @block.tensor
        def _(pe):
            pe.sem_inc(s_hl, NPS)
            pe.sem_inc(s_acc, 2)

            def product(ps, w, n, cols):
                wa_h, wa_l, wbb, wbl = w
                c = slice(n * P, (n + 1) * P)
                nc.tensor.matmul(ps[:], wa_h[:, c], xh[:, cols], start=True, stop=False)
                nc.tensor.matmul(ps[:], wa_h[:, c], xl[:, cols], start=False, stop=False)
                nc.tensor.matmul(ps[:], wa_l[:, c], xh[:, cols], start=False, stop=False)
                nc.tensor.matmul(ps[:], wbb[:, c], xb[:, cols], start=False, stop=False)
                return nc.tensor.matmul(ps[:], wbl[0:CB, c], xb[0:CB, cols], start=False, stop=True)

            def hidden(i, n):
                cols = at(i * CHUNK, CHUNK)
                pe.wait_ge(s_hl, i * NH + n + 1)
                if gate:
                    product(ps_g[n % NPS], gate, n, cols).then_inc(s_gate, 1)
                product(ps_u[n % NPS], up, n, cols).then_inc(s_up, 1)

            def expert(i, n):
                pe.wait_ge(s_hl, NPS + i * NH + n + 1)
                s = n % HB
                for e, r0, r1, first, end in uses[n]:
                    o = ps_o[e % 2]
                    if first:
                        pe.wait_ge(s_acc, i * NE + e + 1 + (e == 0) * (NE % 2))
                    for j in range(TC):
                        dst = o[j // 2][:, (j % 2) * C:(j % 2 + 1) * C]
                        tok = slice(j * P, (j + 1) * P)
                        for m, (a, b) in enumerate(((hh, down[0]), (hh, down[1]), (hl, down[0]))):
                            last = nc.tensor.matmul(dst, a[r0:r1, s, tok], b[r0:r1, n, :],
                                                    start=(first and m == 0 and j % 2 == 0), stop=(end and m == 2),
                                                    skip_group_check=True)
                last.then_inc(s_used, 1)

            with pe.Fori(0, NCHUNK) as i:
                for n in range(NH + SKEW):
                    if n < NH:
                        hidden(i, n)
                    if n >= SKEW:
                        expert(i, n - SKEW)

        @block.scalar
        def _(act):
            act.sem_inc(s_used, HB)
            if gate:
                act.sem_inc(s_hf, HB)
            with act.Fori(0, NCHUNK) as i:
                for n in range(NH + 1 if gate else NH):
                    b, s = i * NH + n, n % HB
                    if n < NH:
                        act.wait_ge(s_gate if gate else s_up, b + 1)
                        if gate:
                            act.wait_ge(s_hf, b + 1)
                            nc.scalar.activation(hg[:, s], ps_g[n % NPS][:], func).then_inc(s_act, 1)
                        else:
                            act.wait_ge(s_used, b + 1)
                            nc.scalar.activation(hh[:, s], ps_u[n % NPS][:], func)
                            nc.scalar.activation(hf[:, s], ps_u[n % NPS][:], func).then_inc(s_hh, 1)
                    if gate and n >= 1:
                        m, b = n - 1, i * NH + n - 1
                        act.wait_ge(s_hf, HB + b + 1)
                        act.wait_ge(s_used, b + 1)
                        nc.scalar.activation(hh[:, m % HB], hf[:, m % HB], ACT.Copy).then_inc(s_hh, 1)

        @block.vector
        def _(dve):
            v = nc.vector
            with dve.Fori(0, NCHUNK) as i:
                def take(e):
                    dve.wait_ge(s_used, HB + i * NH + groups[e][-1][0] + 1)
                    if e == 0 and out is not None:
                        dve.wait_ge(s_out, 16 * i)
                    dve.wait_ge(s_acc, 2 + i * NE + e)
                    if e == 0:
                        v.tensor_copy(cb[:], comb[:, at(i * TC, TC), :]).then_inc(s_cb, 1)
                        dve.wait_ge(s_cb, i + 1)
                    for j in range(TC):
                        x = X[:, at(i * TC + j), :]
                        last = v.scalar_tensor_tensor(
                            out=x if e == NE - 1 and out is None else acc[:, j],
                            in0=ps_o[e % 2][j // 2][:, (j % 2) * C:(j % 2 + 1) * C], scalar=cb[:, j, e:e + 1],
                            in1=x if e == 0 else acc[:, j], op0=ALU.mult, op1=ALU.add)
                    last.then_inc(s_acc, 1)

                LAG = SKEW + 1
                for n in range(NH + LAG):
                    if gate and n < NH:
                        b, s = i * NH + n, n % HB
                        dve.wait_ge(s_act, b + 1)
                        dve.wait_ge(s_up, b + 1)
                        v.tensor_tensor(hf[:, s], hg[:, s], ps_u[n % NPS][:], ALU.mult).then_inc(s_hf, 1)
                    m = n - 1 if gate else n
                    if 0 <= m < NH:
                        b, s = i * NH + m, m % HB
                        dve.wait_ge(s_hh, b + 1)
                        if not gate:
                            dve.wait_ge(s_used, b + 1)
                        v.tensor_tensor(hl[:, s], hf[:, s], hh[:, s], ALU.subtract).then_inc(s_hl, 1)
                    if n >= LAG:
                        for e, _, _, _, end in uses[n - LAG]:
                            if end:
                                take(e)

        @block.sync
        def _(sp):
            if out is None:
                return
            with sp.Fori(0, NCHUNK) as i:
                sp.wait_ge(s_acc, 2 + (i + 1) * NE)
                sp.dma_start(out[at(i * CHUNK, CHUNK)].rearrange("(t p) c -> p t c", p=P), acc[:]).then_inc(s_out, 16)
            sp.wait_ge(s_out, 16 * NCHUNK)


def stage_attention(nc, io, X, ident, ones):
    with ExitStack() as ctx:
        k = Kit(nc, ctx, "att")
        RING, HALF = 4, CHUNK
        N = H * W
        HT = TI * HEADS
        st = k.sb("st", [P, T, 6])
        mean, rstd, tmp = k.sb("mean", [P, T]), k.sb("rstd", [P, T]), k.sb("tmp", [P, T])
        xd = k.sb("xd", [P, RING, C])
        xt = k.sb("xt", [P, 2, N])
        w = k.sb("w", [P, 2, 2, N])
        w2 = k.sb("w2", [P, 2, 2, N])
        val = k.sb("val", [P, 2, N])
        scr = k.sb("scr", [P, 2, HALF])
        pib = k.sb("pi_channels", [P, 2, 2, HALF])
        wq, wo, wos = k.sb("wq", [P, 2, C]), k.sb("wo", [P, 2, C]), k.sb("wos", [P, 2, C])
        hm, rm = k.sb("headmask", [P, 2, HEADS]), k.sb("rm", [P, 2, HEADS])
        temp = k.sb("temp", [P, 1, HEADS])
        ob = k.sb("ob", [1, C])
        ssq = k.sb("ssq", [P, 2, 2, 2])
        rn = k.sb("rn", [P, 2])
        z, pi = k.sb("z", [P, TI, HEADS]), k.sb("pi", [P, TI, HEADS])
        red = k.sb("red", [P, TI])
        pe_ = k.sb("pi_spread", [P, TI, C])
        dot, psum_pi, att = k.sb("dot", [P, 2, 2]), k.sb("sum_pi", [P, 2, 2]), k.sb("attn", [P, 2, 2])
        ps_t = [k.ps("ta"), k.ps("tb")]
        ps_q = [k.ps("qa"), k.ps("qb")]
        ps_p = [k.ps("pa"), k.ps("pb")]
        ps_s, ps_o = k.ps("s"), k.ps("o")
        ROWSB = (P, CB)
        c0 = (0, CA)
        s_in, s_ch0, s_ch, s_stats = k.sem("loaded"), k.sem("setup_chain"), k.sem("dve_chain"), k.sem("stats_ready")
        s_var, s_sd, s_xd = k.sem("variance_ready"), k.sem("std_ready"), k.sem("tile_normalised")
        s_turn, s_xt, s_q, s_w = k.sem("half_turned"), k.sem("half_copied"), k.sem("qkv_half"), k.sem("w_half_kept")
        s_r, s_s, s_sub, s_exp = k.sem("norms_ready"), k.sem("head_sums"), k.sem("logits_shifted"), k.sem("exp_done")
        s_pe, s_p, s_vh, s_sum = k.sem("pi_spread"), k.sem("pi_turned"), k.sem("values_half"), k.sem("pi_summed")
        s_fold, s_o, s_add = k.sem("weights_scaled"), k.sem("out_pair"), k.sem("pair_added")
        block = ctx.enter_context(nc.Block())

        def images(eng, first, step, last):
            first(0, 0)
            step(1, 1)
            with eng.Fori(1, NIMG // 2) as i:
                step(2 * i, 0)
                step(2 * i + 1, 1)
            last(NIMG - 1, 1)

        @block.sync
        def _(sp):
            for name, dst in (("qkv", wq), ("out_w", wo), ("headmask", hm)):
                for b in range(2):
                    sp.dma_start(dst[0:ROWSB[b], b, :], io[name][c0[b]:c0[b] + ROWSB[b]]).then_inc(s_in, 16)
            sp.dma_start(temp[:, 0, :], io["temp"].to_broadcast([P, HEADS])).then_inc(s_in, 16)
            sp.dma_start(ob[:], io["out_b"]).then_inc(s_in, 16)

        @block.vector
        def _(dve):
            v, c = nc.vector, Count(dve, s_ch0)
            with dve.Fori(0, T // 8) as g:
                for j in range(8):
                    v.bn_stats(st[:, at(8 * g + j), :], X[:, at(8 * g + j), :]).then_inc(s_stats, 1)
            dve.wait_ge(s_stats, T)
            finish_stats(v, c, st, mean, rstd, tmp, 1e-6)
            dve.sem_inc(s_var, 1)
            dve.wait_ge(s_sd, 1)
            c.link(v.reciprocal(rstd[:], rstd[:]))
            dve.wait_ge(s_in, 128)
            LINKS = 21

            def norm(g):
                for j in range(TI):
                    dve.wait_ge(s_turn, 2 * g + j // RING)
                    t = g * TI + j
                    v.tensor_scalar(xd[:, j % RING], X[:, at(t), :], mean[:, at(t)], rstd[:, at(t)],
                                    ALU.subtract, ALU.mult).then_inc(s_xd, 1)

            def head(g, u, ch):
                dve.wait_ge(s_w, 2 * g + 2)
                dve.wait_ge(s_s, g)
                for b in range(2):
                    r = slice(0, ROWSB[b])
                    ch.link(v.tensor_tensor(rn[r, b:b + 1], ssq[r, u, b, 0:1], ssq[r, u, b, 1:2], ALU.add))
                    ch.link(v.tensor_scalar(rn[r, b:b + 1], rn[r, b:b + 1], 1e-24, None, ALU.max))
                    ch.link(v.reciprocal(rn[r, b:b + 1], rn[r, b:b + 1]))
                    ch.link(v.tensor_scalar(rm[r, b], hm[r, b], rn[r, b:b + 1], None, ALU.mult))
                dve.sem_inc(s_r, 1)

            def softmax(g, ch):
                dve.wait_ge(s_s, g + 1)
                lg = ps_s[:, 0:HT].rearrange("p (t h) -> p t h", h=HEADS)
                ch.link(v.tensor_tensor(z[:], lg, temp[:].to_broadcast([P, TI, HEADS]), ALU.mult))
                ch.link(v.tensor_reduce(red[:], z[:], AX.X, ALU.max))
                ch.link(v.tensor_tensor(z[:], z[:], bc(red[:], HEADS), ALU.subtract))
                dve.sem_inc(s_sub, 1)
                dve.wait_ge(s_exp, g + 1)
                ch.link(v.tensor_reduce(red[:], z[:], AX.X, ALU.add))
                ch.link(v.reciprocal(red[:], red[:]))
                ch.link(v.tensor_tensor(pi[:], z[:], bc(red[:], HEADS), ALU.mult))
                dve.wait_ge(s_p, 2 * g)
                v.tensor_copy(pe_[:].rearrange("p t (h d) -> p (t h) d", d=DH),
                              bc(pi[:].rearrange("p t h -> p (t h)"), DH)).then_inc(s_pe, 1)

            def values(g, u, ch):
                dve.wait_ge(s_o, 4 * g)
                for h in range(2):
                    dve.wait_ge(s_sum, 1 + 2 * g + h + 1)
                    cols = slice(h * HALF, (h + 1) * HALF)
                    for b in range(2):
                        r = slice(0, ROWSB[b])
                        v.tensor_tensor(val[r, b, cols], w[r, u, b, cols], pib[r, h, b], ALU.mult)
                        last = v.scalar_tensor_tensor(out=scr[r, b], in0=w2[r, u, b, cols], scalar=1.0, in1=pib[r, h, b],
                                                      op0=ALU.mult, op1=ALU.mult, accum_out=dot[r, b, h:h + 1])
                    last.then_inc(s_vh, 1)
                    dve.wait_ge(s_vh, 2 * g + h + 1)
                a, s = att[:, :, 0], att[:, :, 1]
                ch.link(v.tensor_tensor(a, dot[:, :, 0], dot[:, :, 1], ALU.add))
                ch.link(v.scalar_tensor_tensor(out=s, in0=psum_pi[:, :, 0], scalar=1e-8, in1=psum_pi[:, :, 1],
                                               op0=ALU.add, op1=ALU.add))
                ch.link(v.reciprocal(s, s))
                ch.link(v.tensor_tensor(a, a, s, ALU.mult))
                ch.link(v.tensor_scalar(a, a, 1.0, None, ALU.add))
                ch.link(v.reciprocal(a, a))
                for b in range(2):
                    r = slice(0, ROWSB[b])
                    last = v.tensor_scalar(wos[r, b], wo[r, b], att[r, b, 0:1], -1.0, ALU.mult, ALU.mult)
                ch.link(last)
                dve.sem_inc(s_fold, 1)

            def add(g):
                for r in range(TI // 2):
                    dve.wait_ge(s_o, 4 * g + r + 1)
                    x = X[:, at(g * TI + 2 * r, 2), :]
                    v.tensor_tensor(x, ps_o[:, 0:2 * C].rearrange("p (t c) -> p t c", c=C), x, ALU.add).then_inc(s_add, 1)

            for t_ in (dot, psum_pi):
                last = v.memset(t_[:], 0.0)
            c.link(last)
            dve.sem_inc(s_sum, 1)

            def first(g, u):
                norm(g)

            def step(g, u):
                ch = Count(dve, s_ch)
                ch.n = (g - 1) * LINKS
                head(g - 1, 1 - u, ch)
                norm(g)
                softmax(g - 1, ch)
                values(g - 1, 1 - u, ch)
                add(g - 1)

            def last_(g, u):
                ch = Count(dve, s_ch)
                ch.n = g * LINKS
                head(g, u, ch)
                softmax(g, ch)
                values(g, u, ch)
                add(g)

            images(dve, first, step, last_)

        @block.scalar
        def _(act):
            act.wait_ge(s_var, 1)
            nc.scalar.activation(rstd[:], rstd[:], ACT.Sqrt).then_inc(s_sd, 1)
            act.wait_ge(s_sum, 1)

            def copy_turned(g):
                for h in range(2):
                    act.wait_ge(s_turn, 2 * g + h + 1)
                    act.wait_ge(s_q, 2 * g)
                    for b in range(2):
                        r = slice(0, ROWSB[b])
                        last = nc.scalar.activation(xt[r, b, h * HALF:(h + 1) * HALF], ps_t[b][r, :], ACT.Copy)
                    last.then_inc(s_xt, 1)

            def keep_w(g, u):
                act.wait_ge(s_fold, g + 1)
                for h in range(2):
                    act.wait_ge(s_q, 2 * g + h + 1)
                    cols = slice(h * HALF, (h + 1) * HALF)
                    for b in range(2):
                        r = slice(0, ROWSB[b])
                        nc.scalar.activation(w[r, u, b, cols], ps_q[b][r, :], ACT.Copy)
                        last = nc.scalar.activation(w2[r, u, b, cols], ps_q[b][r, :], ACT.Square,
                                                    accum_out=ssq[r, u, b, h:h + 1])
                    last.then_inc(s_w, 1)

            def exp(g):
                act.wait_ge(s_sub, g + 1)
                nc.scalar.activation(z[:], z[:], ACT.Exp).then_inc(s_exp, 1)

            def sum_pi(g):
                for h in range(2):
                    act.wait_ge(s_p, 2 * g + h + 1)
                    act.wait_ge(s_fold, 2 + g)
                    act.wait_ge(s_sum, 1 + 2 * g + h)
                    for b in range(2):
                        r = slice(0, ROWSB[b])
                        last = nc.scalar.activation(pib[r, h, b], ps_p[b][r, :], ACT.Copy,
                                                    accum_out=psum_pi[r, b, h:h + 1])
                    last.then_inc(s_sum, 1)

            def first(g, u):
                copy_turned(g)
                keep_w(g, u)

            def step(g, u):
                copy_turned(g)
                exp(g - 1)
                keep_w(g, u)
                sum_pi(g - 1)

            def last_(g, u):
                exp(g)
                sum_pi(g)

            images(act, first, step, last_)

        @block.tensor
        def _(pe):
            pe.sem_inc(s_fold, 2)
            pe.wait_ge(s_in, 128)

            def turn_and_project(g):
                for h in range(2):
                    pe.wait_ge(s_xt, 2 * g + h)
                    for j in range(RING):
                        pe.wait_ge(s_xd, g * TI + h * RING + j + 1)
                        for b in range(2):
                            last = nc.tensor.transpose(ps_t[b][0:ROWSB[b], j * P:(j + 1) * P],
                                                       xd[:, j, c0[b]:c0[b] + ROWSB[b]], ident[:])
                    last.then_inc(s_turn, 1)
                for h in range(2):
                    pe.wait_ge(s_xt, 2 * g + h + 1)
                    pe.wait_ge(s_w, 2 * g + h)
                    cols = slice(h * HALF, (h + 1) * HALF)
                    for b in range(2):
                        oc = slice(c0[b], c0[b] + ROWSB[b])
                        nc.tensor.matmul(ps_q[b][0:ROWSB[b], :], wq[:, 0, oc], xt[:, 0, cols], start=True, stop=False)
                        last = nc.tensor.matmul(ps_q[b][0:ROWSB[b], :], wq[0:CB, 1, oc], xt[0:CB, 1, cols],
                                                start=False, stop=True)
                    last.then_inc(s_q, 1)

            def head_sums(g, u):
                pe.wait_ge(s_r, g + 1)
                pe.wait_ge(s_sub, g)
                for j in range(TI):
                    o = ps_s[:, j * HEADS:(j + 1) * HEADS]
                    tok = slice(j * P, (j + 1) * P)
                    nc.tensor.matmul(o, w2[:, u, 0, tok], rm[:, 0], start=True, stop=False)
                    last = nc.tensor.matmul(o, w2[0:CB, u, 1, tok], rm[0:CB, 1], start=False, stop=True)
                last.then_inc(s_s, 1)

            def turn_pi(g):
                pe.wait_ge(s_pe, g + 1)
                for h in range(2):
                    pe.wait_ge(s_sum, 1 + 2 * g + h)
                    for j in range(RING):
                        for b in range(2):
                            last = nc.tensor.transpose(ps_p[b][0:ROWSB[b], j * P:(j + 1) * P],
                                                       pe_[:, h * RING + j, c0[b]:c0[b] + ROWSB[b]], ident[:])
                    last.then_inc(s_p, 1)

            def out_project(g):
                pe.wait_ge(s_fold, 2 + g + 1)
                for r in range(TI // 2):
                    pe.wait_ge(s_add, 4 * g + r)
                    for j in range(2):
                        o = ps_o[:, j * C:(j + 1) * C]
                        tok = slice((2 * r + j) * P, (2 * r + j + 1) * P)
                        nc.tensor.matmul(o, ones[0:1, :], ob[:], start=True, stop=False)
                        nc.tensor.matmul(o, val[:, 0, tok], wos[:, 0], start=False, stop=False)
                        last = nc.tensor.matmul(o, val[0:CB, 1, tok], wos[0:CB, 1], start=False, stop=True)
                    last.then_inc(s_o, 1)

            def first(g, u):
                turn_and_project(g)

            def step(g, u):
                head_sums(g - 1, 1 - u)
                turn_and_project(g)
                turn_pi(g - 1)
                out_project(g - 1)

            def last_(g, u):
                head_sums(g, u)
                turn_pi(g)
                out_project(g)

            images(pe, first, step, last_)


def program(nc, io, out, stages=99, dbg=None):
    table = nc.dram_tensor("corner_table", (NTOK + FRONT, 4 * C), F32, kind="Internal").ap()
    with ExitStack() as ctx:
        k = Kit(nc, ctx, "all")
        X = k.sb("x", [P, T, C])
        Y = k.sb("y", [P, T, C])
        sums = k.sb("sums", [P, 2 * C])
        ident, ones = k.sb("ident", [P, P]), k.sb("ones", [P, P])
        setup_constants(nc, ident, ones)
        with ExitStack() as conv:
            kc = Kit(nc, conv, "conv")
            wts, idx = kc.sb("wts", [P, T, K9, 4]), kc.sb("idx", [P, T, K9], I32)
            with ExitStack() as early:
                ke = Kit(nc, early, "early")
                om = ke.sb("om", [P, T, NOM])
                stage_offsets(nc, io, X, ident, om, table)
                if dbg is not None and stages == 1:
                    return dump(nc, om[:].rearrange("p t o -> p (t o)"), dbg)
                grid = ke.sb("grid", [P, 3, T * K9])
                stage_corners(nc, io, om, grid, wts, idx)
            stage_deform(nc, io, table, wts, idx, Y, ones, ident, sums)
            if dbg is not None and stages == 3:
                return dump(nc, Y[:].rearrange("p t o -> p (t o)"), dbg)
        stage_batchnorm(nc, io, X, Y, sums)
        if dbg is not None and stages == 4:
            return dump(nc, X[:].rearrange("p t o -> p (t o)"), dbg)
        turned = Y[:].rearrange("p t c -> p (t c)").bitcast(F16).rearrange("p (a n) -> p a n", a=3)
        xh, xl, xb = turned[:, 0], turned[:, 1], turned[:, 2]
        comb = k.sb("comb", [P, T, LG])
        stage_route(nc, io, "route0", X, xh, xl, xb, comb, ident, 1e-5, io["router0"], E0, 8)
        with ExitStack() as ffn:
            kf = Kit(nc, ffn, "w0")
            up = [kf.sb(n, [P, HID0], F16) for n in ("ah", "al", "bb")] + [kf.sb("bl", [CB, HID0], F16)]
            down = [kf.sb(n, [P, HID0 // P, C], F16) for n in ("dh", "dl")]
            stage_split(nc, "split0", list(split_up(io["w1_0"], *up)) + list(split_down(io["w2_0"], *down)))
            groups, blk = [], 0
            for w in W0_WIDTHS:
                groups.append([(blk + j, 0, P) for j in range(w // P)])
                blk += w // P
            stage_ffn(nc, "ffn0", X, xh, xl, xb, comb, up, None, down, groups, ACT.Gelu_apprx_tanh)
        if dbg is not None and stages == 5:
            return dump(nc, X[:].rearrange("p t o -> p (t o)"), dbg)
        stage_attention(nc, io, X, ident, ones)
        if dbg is not None and stages == 6:
            return dump(nc, X[:].rearrange("p t o -> p (t o)"), dbg)
        stage_route(nc, io, "route1", X, xh, xl, xb, comb, ident, 1e-5, io["router1"], E1, 2, io["sg_b"])
        with ExitStack() as ffn:
            kf = Kit(nc, ffn, "w1")
            gate, up = ([kf.sb(f"{g}{n}", [P, HID1], F16) for n in ("ah", "al", "bb")] + [kf.sb(f"{g}bl", [CB, HID1], F16)]
                        for g in ("g", "u"))
            down = [kf.sb(n, [P, HID1 // P, C], F16) for n in ("dh", "dl")]
            parts = []
            for w, routed, shared in ((gate, "wg", "wsg"), (up, "wu", "wsu")):
                parts += split_up(io[routed], *(a[:, 0:HID1R] for a in w))
                parts += split_up(io[shared], *(a[:, HID1R:HID1] for a in w))
            nr = HID1R // P
            parts += split_down(io["wd"], *(a[:, 0:nr] for a in down))
            parts += split_down(io["wsd"], *(a[:, nr:HID1 // P] for a in down))
            stage_split(nc, "split1", parts)
            groups = []
            for e in range(0, E1, 2):
                b = e // 2 * 3
                groups += [[(b, 0, P), (b + 1, 0, CB)], [(b + 1, CB, P), (b + 2, 0, P)]]
            groups.append([(b, 0, P) for b in range(nr, HID1 // P)])
            stage_ffn(nc, "ffn1", X, xh, xl, xb, comb, up, gate, down, groups, ACT.Silu, out)


def setup_constants(nc, ident, ones):
    with ExitStack() as ctx:
        k = Kit(nc, ctx, "const")
        s = k.sem("set")
        block = ctx.enter_context(nc.Block())

        @block.gpsimd
        def _(pool):
            nc.gpsimd.memset(ident[:], 0.0).then_inc(s, 1)
            nc.gpsimd.memset(ones[:], 1.0)
            pool.wait_ge(s, 1)
            nc.gpsimd.affine_select(out=ident[:], in_=ident[:], compare_op=ALU.not_equal, fill=1.0, base=0,
                                    pattern=[[-1, P]], channel_multiplier=1).then_inc(s, 1)
            pool.wait_ge(s, 2)


def dump(nc, ap, dbg):
    with ExitStack() as ctx:
        s = Kit(nc, ctx, "dbg").sem("s")
        block = ctx.enter_context(nc.Block())

        @block.sync
        def _(sp):
            sp.dma_start(dbg, ap).then_inc(s, 16)
            sp.wait_ge(s, 16)


def layouts(i):
    f = np.ascontiguousarray
    ar = {k: np.asarray(v) for k, v in i.items()}
    om_w = np.concatenate([ar["L0_conv_off_w"], ar["L0_conv_mask_w"]], 0).reshape(NOM, C, K9).transpose(1, 2, 0)
    p, t, k = np.meshgrid(np.arange(P), np.arange(T), np.arange(K9), indexing="ij")
    grid = np.stack([(t % TI) * ROWS + p // W - 1 + k // 3, p % W - 1 + k % 3,
                     (t // TI) * H * W + FRONT], 1).astype(np.float32)
    return {
        "x": f(ar["x"].reshape(NIMG, C, H * W).transpose(0, 2, 1).reshape(NTOK, C)),
        "om_w": f(om_w.reshape(C, K9 * NOM)),
        "om_b": f(np.concatenate([ar["L0_conv_off_b"], ar["L0_conv_mask_b"]]).reshape(1, NOM)),
        "grid": f(grid.reshape(P, 3, T * K9)),
        "conv_w": f(ar["L0_conv_proj_w"].reshape(C, C, K9).transpose(2, 1, 0).reshape(CONV_K, C)),
        "conv_b": f(ar["L0_conv_proj_b"].reshape(1, C)),
        "gamma": f(ar["L0_conv_gamma"].reshape(1, C)),
        "beta": f(ar["L0_conv_beta"].reshape(1, C)),
        "router0": f(ar["L0_ffn_router_w"].T),
        "w1_0": f(ar["L0_ffn_w1"]),
        "w2_0": f(ar["L0_ffn_w2"]),
        "qkv": f(ar["L1_conv_qkv_w"].T),
        "temp": f(ar["L1_conv_temp"].reshape(1, HEADS)),
        "out_w": f(ar["L1_conv_out_w"].T),
        "out_b": f(ar["L1_conv_out_b"].reshape(1, C)),
        "headmask": f((np.arange(C)[:, None] // DH == np.arange(HEADS)).astype(np.float32)),
        "router1": f(np.concatenate([ar["L1_ffn_router_w"], ar["L1_ffn_sg_w"]], 1)),
        "sg_b": f(ar["L1_ffn_sg_b"].reshape(1, 1)),
        "wg": f(ar["L1_ffn_w_gate"].transpose(1, 0, 2).reshape(C, HID1R)),
        "wu": f(ar["L1_ffn_w_up"].transpose(1, 0, 2).reshape(C, HID1R)),
        "wd": f(ar["L1_ffn_w_down"].reshape(HID1R, C)),
        "wsg": f(ar["L1_ffn_ws_gate"]),
        "wsu": f(ar["L1_ffn_ws_up"]),
        "wsd": f(ar["L1_ffn_ws_down"]),
    }


def kernel(**inputs):
    import concourse.bacc as bacc
    from concourse.bass_utils import run_bass_kernel_spmd

    nc = bacc.Bacc("TRN2", target_bir_lowering=False, num_devices=1)
    arrays = {f"in_{n}": a for n, a in layouts(inputs).items()}
    io = {n[3:]: nc.dram_tensor(n, a.shape, mybir.dt.from_np(a.dtype), kind="ExternalInput").ap()
          for n, a in arrays.items()}
    out = nc.dram_tensor("out", (NTOK, C), F32, kind="ExternalOutput").ap()
    program(nc, io, out)
    got = run_bass_kernel_spmd(nc, [arrays], core_ids=[0]).results[0]["out"]
    return np.ascontiguousarray(got.reshape(NIMG, H * W, C).transpose(0, 2, 1)).reshape(NIMG, C, H, W)
```

```python
from contextlib import ExitStack

import concourse.bass as bass
from concourse import mybir
import numpy as np

ALU = mybir.AluOpType
ACT = mybir.ActivationFunctionType
AX = mybir.AxisListType
F32 = mybir.dt.float32
F16 = mybir.dt.float16
I32 = mybir.dt.int32

P = 128
NIMG, H, W, C = 8, 32, 32, 192
CA, CB = 128, 64
NTOK = NIMG * H * W
T = NTOK // P
TI = T // NIMG
ROWS = P // W
HP = H + 2
K9 = 9
NOM = 27
FRONT = W + 1
MAXOFF = float(H // 4)
CONV_K = K9 * C
CONV_M = -(-CONV_K // P)
E0, E1 = 16, 8
W0_WIDTHS = [128] * 8 + [256] * 8
HID0 = sum(W0_WIDTHS)
HID1R, HID1S = E1 * 192, 768
HID1 = HID1R + HID1S
CHUNK = 512
TC = CHUNK // P
NCHUNK = NTOK // CHUNK
HEADS, DH = 12, 16
LG = 16


class Count:

    def __init__(self, eng, sem):
        self.eng, self.sem, self.n = eng, sem, 0

    def mark(self, ins):
        ins.then_inc(self.sem, 1)
        self.n = self.n + 1

    def wait(self):
        self.eng.wait_ge(self.sem, self.n)

    def link(self, ins):
        self.mark(ins)
        self.wait()


USED = []


def clear_semaphores(nc):
    nc.clear_and_free_semaphores(USED)
    USED.clear()
    nc.all_engine_barrier()


class Kit:

    def __init__(self, nc, ctx, tag):
        self.nc, self.ctx, self.tag = nc, ctx, tag

    def sb(self, name, shape, dt=F32):
        return self.ctx.enter_context(self.nc.sbuf_tensor(f"{self.tag}_{name}", shape, dt))

    def ps(self, name, shape=(P, 512), dt=F32):
        return self.ctx.enter_context(self.nc.psum_tensor(f"{self.tag}_{name}", list(shape), dt))

    def sem(self, name):
        sem = self.nc.alloc_semaphore(f"{self.tag}_{name}")
        USED.append(sem)
        return sem


def bc(ap, n):
    return ap.unsqueeze(2).to_broadcast([ap.shape[0], ap.shape[1], n])


def at(t, n=1):
    return bass.ds(t, n)


def turn_tile(nc, ps, x, ident):
    nc.tensor.transpose(ps[:, 0:P], x[:, 0:P], ident[:])
    nc.tensor.transpose(ps[:, P:2 * P], x[:, C - P:C], ident[:])
    return nc.tensor.transpose(ps[0:CB, P:2 * P], x[:, CA:C], ident[:])


FINISH = 5


def finish_stats(dve, ch, st, mean, var, tmp, eps):
    me, qe, mo, qo = st[:, :, 1], st[:, :, 2], st[:, :, 4], st[:, :, 5]
    ch.link(dve.tensor_tensor(tmp, me, mo, ALU.subtract))
    dve.tensor_tensor(mean, me, mo, ALU.add)
    ch.link(dve.tensor_tensor(var, qe, qo, ALU.add))
    ch.link(dve.tensor_tensor(tmp, tmp, tmp, ALU.mult))
    dve.tensor_scalar(mean, mean, 0.5, None, ALU.mult)
    ch.link(dve.tensor_scalar(var, var, 1.0 / C, float(eps), ALU.mult, ALU.add))
    ch.link(dve.scalar_tensor_tensor(out=var, in0=tmp, scalar=0.25, in1=var,
                                     op0=ALU.mult, op1=ALU.add))


def stage_offsets(nc, io, X, xn, st, ident, om, table):
    with ExitStack() as ctx:
        k = Kit(nc, ctx, "off")
        mean, rstd, tmp = (k.sb(n, [P, 2, TI]) for n in ("mean", "rstd", "tmp"))
        RING = 4
        pad_hi = k.sb("pad_hi", [P, 2, 3, HP, W], F16)
        pad_lo = k.sb("pad_lo", [P, 2, 3, HP, W], F16)
        pad_b = k.sb("pad_b", [P, 2, 3, HP, W], F16)
        wf = k.sb("wf", [P, 2, K9, NOM])
        w_a = k.sb("w_a", [P, K9, 2, NOM], F16)
        w_b = k.sb("w_b", [P, K9, 2, NOM], F16)
        omlo = k.sb("omlo", [P, 2, TI, NOM])
        zero = k.sb("zero", [FRONT, 4 * C])
        ps_t = [k.ps(f"t{i}") for i in range(RING)]
        ps_c = [k.ps(f"c{i}") for i in range(2)]
        s_img = [k.sem(f"image_loaded{u}") for u in range(2)]
        s_w = k.sem("weights_loaded")
        s_const = k.sem("constants_set")
        s_ch, s_split = k.sem("stats_chain"), k.sem("split_chain")
        s_var, s_sd, s_xd = k.sem("variance_ready"), k.sem("std_ready"), k.sem("tile_normalised")
        s_tab = [k.sem(f"table_written{u}") for u in range(2)]
        s_border = k.sem("table_border")
        s_tp, s_hi, s_lo = k.sem("transposed"), k.sem("hi_ready"), k.sem("lo_ready")
        s_shift, s_shift_hi = k.sem("shifted"), k.sem("hi_shifted")
        SHIFTS = ((0, slice(1, W), slice(0, W - 1)), (2, slice(0, W - 1), slice(1, W)))
        s_wsplit = k.sem("weights_split")
        s_conv, s_cfree, s_cl = k.sem("conv_done"), k.sem("conv_psum_free"), k.sem("conv_lo_copied")
        block = ctx.enter_context(nc.Block())

        @block.sync
        def _(sp):
            def load(g, u):
                sp.dma_start(X[:, at(g * TI, TI), :], io["x"][at(g * TI * P, TI * P)]
                             .rearrange("(t p) c -> p t c", p=P)).then_inc(s_img[u], 16)

            def store(g, u):
                sp.wait_ge(s_xd, (g + 1) * TI)
                for n in range(4):
                    row = g * TI * P + FRONT - (n // 2) * W - n % 2
                    sp.dma_start(table[at(row, TI * P), n * C:(n + 1) * C].rearrange("(t p) c -> p t c", p=P),
                                 xn[:, u * TI:(u + 1) * TI, :]).then_inc(s_tab[u], 16)

            load(0, 0)
            load(1, 1)
            ow = io["om_w"].rearrange("c (k o) -> c k o", k=K9)
            sp.dma_start(wf[:, 0], ow[0:CA]).then_inc(s_w, 16)
            sp.dma_start(wf[0:CB, 1], ow[CA:C]).then_inc(s_w, 16)
            sp.dma_start(wf[CB:P, 1], ow[CA:C]).then_inc(s_w, 16)
            sp.wait_ge(s_const, 1)
            sp.dma_start(table[NTOK:NTOK + FRONT], zero[:]).then_inc(s_border, 16)
            sp.dma_start(table[0:FRONT], zero[:]).then_inc(s_border, 16)
            sp.wait_ge(s_border, 32)
            sp.wait_ge(s_img[0], 16)
            load(2, 0)
            with sp.Fori(0, NIMG // 2 - 2) as i:
                for u in range(2):
                    sp.wait_ge(s_img[1 - u], 16 * (i + 1 + u))
                    load(2 * i + u + 3, 1 - u)
                    store(2 * i + u, u)
            sp.wait_ge(s_img[1], 16 * (NIMG // 2 - 1))
            load(NIMG - 1, 1)
            for g in range(NIMG - 4, NIMG):
                store(g, g % 2)
            for tab in s_tab:
                sp.wait_ge(tab, 1 + 4 * 16 * (NIMG // 2))

        @block.gpsimd
        def _(pool):
            nc.gpsimd.memset(zero[:], 0.0).then_inc(s_const, 1)
            for pad in (pad_hi, pad_lo, pad_b):
                last = nc.gpsimd.memset(pad[:], 0.0)
            last.then_inc(s_const, 1)

        @block.vector
        def _(dve):
            ch = Count(dve, s_ch)
            LINKS = FINISH + 2

            def tile_stats(g, j):
                return nc.vector.bn_stats(st[:, at(g * TI + j), :], X[:, at(g * TI + j), :])

            def variance(g, u, last):
                ch = Count(dve, s_ch)
                ch.n = g * LINKS
                ch.link(last)
                finish_stats(nc.vector, ch, st[:, at(g * TI, TI), :], mean[:, u], rstd[:, u], tmp[:, u], 1e-6)
                dve.sem_inc(s_var, 1)

            def reciprocal(g, u):
                dve.wait_ge(s_sd, g + 1)
                nc.vector.reciprocal(rstd[:, u], rstd[:, u]).then_inc(s_ch, 1)
                dve.wait_ge(s_ch, (g + 1) * LINKS)

            def low(t, u, j):
                dve.wait_ge(s_hi, t + 1)
                rows = slice(1 + j * ROWS, 1 + (j + 1) * ROWS)
                a = ps_t[j % RING][:, 0:P].rearrange("p (r x) -> p r x", x=W)
                b = ps_t[j % RING][CB:P, P:2 * P].rearrange("p (r x) -> p r x", x=W)
                nc.vector.tensor_tensor(pad_lo[:, u, 1, rows], a, pad_hi[:, u, 1, rows], ALU.subtract)
                pb = pad_b[CB:P, u, 1, rows]
                nc.vector.tensor_tensor(pb, b, pb, ALU.subtract).then_inc(s_lo, 1)

            def image(g, u, nth, following=True):
                reciprocal(g, u)
                dve.wait_ge(s_tab[u], 1 + 4 * 16 * nth)
                for j in range(TI):
                    t = g * TI + j
                    nc.vector.tensor_scalar(xn[:, u * TI + j, :], X[:, at(t), :], mean[:, u, j:j + 1], rstd[:, u, j:j + 1],
                                            ALU.subtract, ALU.mult).then_inc(s_xd, 1)
                if following:
                    dve.wait_ge(s_img[1 - u], 16 * (nth + 1 + u))
                for j in range(TI):
                    if following:
                        last = tile_stats(g + 1, j)
                    low(g * TI + j, u, j)
                if following:
                    variance(g + 1, 1 - u, last)
                dve.wait_ge(s_lo, RING + (g + 1) * TI)
                for pad in (pad_lo, pad_b):
                    for kx, dst, src in SHIFTS:
                        last = nc.vector.tensor_copy(pad[:, u, kx, 1:1 + H, dst], pad[:, u, 1, 1:1 + H, src])
                last.then_inc(s_shift, 1)

            def gather_conv(g, u):
                dve.wait_ge(s_cl, g + 1)
                src = ps_c[u][:, 0:TI * 2 * NOM].rearrange("p (t s o) -> p t s o", s=2, o=NOM)[:, :, 0, :]
                nc.vector.tensor_tensor(om[:, at(g * TI, TI), :], src, omlo[:, u], ALU.add).then_inc(s_cfree, 1)

            dve.wait_ge(s_img[0], 16)
            for j in range(TI):
                first = tile_stats(0, j)
            variance(0, 0, first)
            ch = Count(dve, s_split)
            dve.wait_ge(s_w, 48)
            nc.vector.tensor_copy(w_a[:, :, 0, :], wf[:, 0])
            nc.vector.tensor_copy(w_b[:, :, 0, :], wf[:, 1])
            ch.link(nc.vector.memset(w_b[CB:P, :, 1, :], 0.0))
            nc.vector.tensor_tensor(w_a[:, :, 1, :], wf[:, 0], w_a[:, :, 0, :], ALU.subtract)
            nc.vector.tensor_tensor(w_b[0:CB, :, 1, :], wf[0:CB, 1], w_b[0:CB, :, 0, :], ALU.subtract).then_inc(s_wsplit, 1)
            image(0, 0, 0)
            with dve.Fori(0, NIMG // 2 - 1) as i:
                image(2 * i + 1, 1, i)
                gather_conv(2 * i, 0)
                image(2 * i + 2, 0, i + 1)
                gather_conv(2 * i + 1, 1)
            image(NIMG - 1, 1, NIMG // 2 - 1, following=False)
            gather_conv(NIMG - 2, 0)
            gather_conv(NIMG - 1, 1)

        @block.scalar
        def _(act):
            def root(g, u):
                act.wait_ge(s_var, g + 1)
                nc.scalar.activation(rstd[:, u], rstd[:, u], ACT.Sqrt).then_inc(s_sd, 1)

            root(0, 0)
            act.wait_ge(s_const, 2)

            def image(g, u, following=True):
                act.wait_ge(s_conv, g + 1)
                for j in range(TI):
                    act.wait_ge(s_tp, g * TI + j + 1)
                    rows = slice(1 + j * ROWS, 1 + (j + 1) * ROWS)
                    a = ps_t[j % RING][:, 0:P].rearrange("p (r x) -> p r x", x=W)
                    b = ps_t[j % RING][:, P:2 * P].rearrange("p (r x) -> p r x", x=W)
                    nc.scalar.activation(pad_hi[:, u, 1, rows], a, ACT.Copy)
                    nc.scalar.activation(pad_b[:, u, 1, rows], b, ACT.Copy).then_inc(s_hi, 1)
                if following:
                    root(g + 1, 1 - u)
                act.wait_ge(s_hi, (g + 1) * TI)
                for kx, dst, src in SHIFTS:
                    last = nc.scalar.activation(pad_hi[:, u, kx, 1:1 + H, dst], pad_hi[:, u, 1, 1:1 + H, src], ACT.Copy)
                last.then_inc(s_shift_hi, 1)

            def conv_low(g, u):
                act.wait_ge(s_conv, 2 + g + 1)
                act.wait_ge(s_cfree, g + 1)
                src = ps_c[u][:, 0:TI * 2 * NOM].rearrange("p (t s o) -> p t s o", s=2, o=NOM)[:, :, 1, :]
                nc.scalar.activation(omlo[:, u], src, ACT.Copy).then_inc(s_cl, 1)

            image(0, 0)
            with act.Fori(0, NIMG // 2 - 1) as i:
                image(2 * i + 1, 1)
                conv_low(2 * i, 0)
                image(2 * i + 2, 0)
                conv_low(2 * i + 1, 1)
            image(NIMG - 1, 1, following=False)
            conv_low(NIMG - 2, 0)
            conv_low(NIMG - 1, 1)

        @block.tensor
        def _(pe):
            pe.sem_inc(s_lo, RING)
            pe.sem_inc(s_cfree, 2)
            pe.sem_inc(s_conv, 2)
            for tab in s_tab:
                pe.sem_inc(tab, 1)
            pe.wait_ge(s_wsplit, 1)

            def image(g, u):
                for j in range(TI):
                    t = g * TI + j
                    pe.wait_ge(s_xd, t + 1)
                    pe.wait_ge(s_lo, t + 1)
                    turn_tile(nc, ps_t[j % RING], xn[:, u * TI + j, :], ident).then_inc(s_tp, 1)

            def conv(g, u):
                pe.wait_ge(s_shift_hi, g + 1)
                pe.wait_ge(s_shift, g + 1)
                pe.wait_ge(s_cfree, g + 1)
                for j in range(TI):
                    o = j * 2 * NOM
                    for tap in range(K9):
                        ky, kx = tap // 3, tap % 3
                        first = j == 0 and tap == 0
                        for n, (pad, wt, cols) in enumerate(((pad_hi, w_a, 2), (pad_b, w_b, 2), (pad_lo, w_a, 1))):
                            last = nc.tensor.matmul(ps_c[u][:, o:o + cols * NOM], pad[:, u, kx].rearrange("p y x -> p (y x)")
                                                    [:, (j * ROWS + ky) * W:(j * ROWS + ky) * W + P],
                                                    wt[:, tap, 0:cols, :], start=(first and n == 0),
                                                    stop=(tap == K9 - 1 and n == 2), skip_group_check=True)
                last.then_inc(s_conv, 1)

            image(0, 0)
            with pe.Fori(0, NIMG // 2 - 1) as i:
                image(2 * i + 1, 1)
                conv(2 * i, 0)
                image(2 * i + 2, 0)
                conv(2 * i + 1, 1)
            image(NIMG - 1, 1)
            conv(NIMG - 2, 0)
            conv(NIMG - 1, 1)


def stage_corners(nc, io, om, grid, wts, idx):
    with ExitStack() as ctx:
        k = Kit(nc, ctx, "crn")
        N = T * K9
        bias = k.sb("bias", [P, 1, NOM])
        flat = {n: k.sb(n, [P, N]) for n in ("by", "bx", "t", "y0", "y1", "x0", "x1", "m")}
        fl = k.sb("fl", [P, N], I32)
        s_in, s_ch, s_z, s_m = k.sem("loaded"), k.sem("dve_chain"), k.sem("mask_logits"), k.sem("mask_ready")
        block = ctx.enter_context(nc.Block())

        @block.sync
        def _(sp):
            sp.dma_start(bias[:, 0, :], io["om_b"].to_broadcast([P, NOM])).then_inc(s_in, 16)
            sp.dma_start(grid[:], io["grid"]).then_inc(s_in, 16)

        @block.scalar
        def _(act):
            act.wait_ge(s_z, 1)
            nc.scalar.activation(flat["m"][:], flat["m"][:], ACT.Sigmoid).then_inc(s_m, 1)

        @block.vector
        def _(dve):
            v = nc.vector
            ch = Count(dve, s_ch)
            dve.wait_ge(s_in, 32)
            ch.link(v.tensor_tensor(om[:], om[:], bias[:].to_broadcast([P, T, NOM]), ALU.add))
            tk = lambda ap: ap.rearrange("p (t k) -> p t k", k=K9)
            ch.link(v.tensor_copy(tk(flat["m"][:]), om[:, :, 2 * K9:NOM]))
            dve.sem_inc(s_z, 1)
            t = flat["t"][:]
            for d in range(2):
                w0, w1, b = ((flat["y0"], flat["y1"], flat["by"]), (flat["x0"], flat["x1"], flat["bx"]))[d]
                w0, w1, b = w0[:], w1[:], b[:]
                ch.link(v.tensor_scalar(tk(w0), om[:, :, d:2 * K9:2], -MAXOFF, MAXOFF, ALU.max, ALU.min))
                ch.link(v.tensor_tensor(w0, w0, grid[:, d], ALU.add))
                ch.link(v.tensor_copy(fl[:], w0))
                ch.link(v.tensor_copy(b, fl[:]))
                ch.link(v.tensor_tensor(t, b, w0, ALU.is_gt))
                ch.link(v.tensor_tensor(b, b, t, ALU.subtract))
                ch.link(v.tensor_scalar(b, b, 0.0, float(H - 1), ALU.max, ALU.min))
                ch.link(v.tensor_tensor(t, w0, b, ALU.subtract))
                ch.link(v.tensor_scalar(w0, t, -1.0, 1.0, ALU.mult, ALU.add))
                ch.link(v.scalar_tensor_tensor(out=w1, in0=w0, scalar=1.0, in1=t, op0=ALU.add, op1=ALU.min))
                ch.link(v.scalar_tensor_tensor(out=w0, in0=t, scalar=1.0, in1=w0, op0=ALU.add, op1=ALU.min))
                ch.link(v.tensor_scalar(w0, w0, 0.0, None, ALU.max))
                ch.link(v.tensor_scalar(t, b, float(H - 1), None, ALU.is_lt))
                ch.link(v.scalar_tensor_tensor(out=w1, in0=w1, scalar=0.0, in1=t, op0=ALU.max, op1=ALU.mult))
            ch.link(v.scalar_tensor_tensor(out=t, in0=flat["by"][:], scalar=float(W), in1=flat["bx"][:],
                                           op0=ALU.mult, op1=ALU.add))
            ch.link(v.tensor_tensor(t, t, grid[:, 2], ALU.add))
            v.tensor_copy(idx[:].rearrange("p t k -> p (t k)"), t)
            dve.wait_ge(s_m, 1)
            for y in ("y0", "y1"):
                ch.link(v.scalar_tensor_tensor(out=flat[y][:], in0=flat["m"][:], scalar=2.0, in1=flat[y][:],
                                               op0=ALU.mult, op1=ALU.mult))
            for n, (y, x) in enumerate((("y0", "x0"), ("y0", "x1"), ("y1", "x0"), ("y1", "x1"))):
                v.tensor_tensor(wts[:, :, :, n], tk(flat[y][:]), tk(flat[x][:]), ALU.mult)


def stage_deform(nc, io, table, wts, idx, Y, ones, ident, sums):
    with ExitStack() as ctx:
        k = Kit(nc, ctx, "dfm")
        gath = k.sb("gath", [P, 2, K9, 4 * C])
        samp = k.sb("samp", [P, 2, CONV_K])
        sampT = k.sb("sampT", [P, 2, CONV_M * P])
        wconv = k.sb("wconv", [P, CONV_M, C])
        wt = k.sb("wt", [P, 2, K9, 4])
        IXR = 4
        ix = k.sb("ix", [P, IXR, K9], I32)
        GROUP, PER = 3, 3 * K9
        ysq = k.sb("ysq", [P, 2, 2, C])
        ps_t = [k.ps(f"t{i}") for i in range(4)]
        ps_y = [k.ps(f"y{i}") for i in range(2)]
        ps_s = k.ps("s")
        s_w = k.sem("weights_loaded")
        s_g = [[k.sem(f"gathered{u}_{n}") for n in range(K9)] for u in range(2)]
        s_ix, s_first, s_samp = k.sem("tile_indices"), k.sem("first_corner"), k.sem("samples_ready")
        s_acc, s_sfree = k.sem("dve_accumulate"), k.sem("samples_free")
        s_wt, s_free = k.sem("tile_weights"), k.sem("gather_slots_free")
        s_turn, s_evac = k.sem("turned"), k.sem("turned_copied")
        s_conv, s_y, s_sum, s_zero, s_sums = k.sem("conv_done"), k.sem("y_ready"), k.sem("y_summed"), k.sem("sum_zeroed"), k.sem("sums")
        block = ctx.enter_context(nc.Block())
        BANKS = 4
        blocks = [list(range(4 * q, min(4 * q + 4, CONV_M))) for q in range(BANKS)]
        rows = lambda m: min(P, CONV_K - m * P)

        @block.sync
        def _(sp):
            full = (CONV_M - 1) * P
            sp.dma_start(wconv[:, 0:CONV_M - 1, :], io["conv_w"][0:full].rearrange("(m p) c -> p m c", p=P)).then_inc(s_w, 16)
            sp.dma_start(wconv[0:CONV_K - full, CONV_M - 1, :], io["conv_w"][full:CONV_K]).then_inc(s_w, 16)

        @block.gpsimd
        def _(pool):
            pool.wait_ge(s_zero, 1)
            def indices(t, r):
                nc.gpsimd.tensor_copy(ix[:, r, :], idx[:, at(t), :]).then_inc(s_ix, 1)

            def gather(t, r, first=False):
                u = r % 2
                pool.wait_ge(s_ix, t + 1)
                for n in range(K9):
                    if n % GROUP == 0:
                        if not first:
                            pool.wait_ge(s_acc, (t - 2) * PER + GROUP * (n + GROUP))
                        pool.sem_inc(s_free, 1)
                    nc.gpsimd.indirect_dma_start(
                        out=gath[:, u, n, :], out_offset=None, in_=table,
                        in_offset=bass.IndirectOffsetOnAxis(ap=ix[:, r, n:n + 1], axis=0)).then_inc(s_g[u][n], 16)
                    if n == GROUP:
                        indices((t + 1) if isinstance(t, int) else (t + 1) % T, (r + 1) % IXR)

            indices(0, 0)
            for t in range(IXR):
                gather(t, t, t < 2)
            with pool.Fori(1, T // IXR) as i:
                for r in range(IXR):
                    gather(IXR * i + r, r)

        @block.vector
        def _(dve):
            nc.vector.memset(ysq[:, 0], 0.0).then_inc(s_zero, 1)
            nc.vector.tensor_copy(wt[:, 0], wts[:, 0]).then_inc(s_wt, 1)

            with dve.Fori(0, T // 2) as i:
                for u in range(2):
                    t = 2 * i + u
                    n_acc = t * PER
                    for g0 in range(0, K9, 3):
                        dve.wait_ge(s_first, t * K9 + g0 + 3)
                        if g0 == 0:
                            dve.wait_ge(s_wt, t + 1)
                        for c in range(1, 4):
                            if c > 1:
                                dve.wait_ge(s_acc, n_acc)
                            for n in range(g0, g0 + 3):
                                s = samp[:, u, n * C:(n + 1) * C]
                                last = nc.vector.scalar_tensor_tensor(
                                    out=s, in0=gath[:, u, n, c * C:(c + 1) * C], scalar=wt[:, u, n, c:c + 1], in1=s,
                                    op0=ALU.mult, op1=ALU.add)
                                last.then_inc(s_acc, 1)
                                n_acc = n_acc + 1
                        if g0 == 0:
                            nc.vector.tensor_copy(wt[:, 1 - u], wts[:, at((t + 1) % T)]).then_inc(s_wt, 1)
                    dve.wait_ge(s_acc, n_acc)
                    dve.sem_inc(s_samp, 1)

        @block.scalar
        def _(act):
            act.sem_inc(s_sfree, 2)

            def first_corners(t, u, q):
                act.wait_ge(s_sfree, t + 1)
                act.wait_ge(s_wt, t + 1)
                for n in range(K9):
                    act.wait_ge(s_g[u][n], 16 * (q + 1))
                    nc.scalar.activation(samp[:, u, n * C:(n + 1) * C], gath[:, u, n, 0:C], ACT.Copy,
                                         scale=wt[:, u, n, 0:1]).then_inc(s_first, 1)

            def copy_turned(t, u):
                for q in range(BANKS):
                    act.wait_ge(s_turn, t * BANKS + q + 1)
                    full = [m for m in blocks[q] if rows(m) == P]
                    w = len(full) * P
                    last = nc.scalar.activation(sampT[:, u, 4 * q * P:4 * q * P + w], ps_t[q][:, 0:w], ACT.Copy)
                    for m in blocks[q]:
                        if rows(m) < P:
                            last = nc.scalar.activation(sampT[0:rows(m), u, m * P:(m + 1) * P],
                                                        ps_t[q][0:rows(m), w:w + P], ACT.Copy)
                    last.then_inc(s_evac, 1)

            def keep_y(t, u):
                act.wait_ge(s_conv, t + 1)
                act.wait_ge(s_sum, t + 1)
                nc.scalar.activation(ysq[:, u, 0], ps_y[u][:, 0:C], ACT.Copy)
                nc.scalar.activation(ysq[:, u, 1], ps_y[u][:, 0:C], ACT.Square)
                nc.scalar.activation(Y[:, at(t), :], ps_y[u][:, 0:C], ACT.Copy).then_inc(s_y, 1)

            first_corners(0, 0, 0)
            first_corners(1, 1, 0)
            copy_turned(0, 0)
            first_corners(2, 0, 1)
            copy_turned(1, 1)
            first_corners(3, 1, 1)
            keep_y(0, 0)
            copy_turned(2, 0)
            with act.Fori(2, T // 2) as i:
                for u in range(2):
                    first_corners(2 * i + u, u, i)
                    keep_y(2 * i + u - 3, 1 - u)
                    copy_turned(2 * i + u - 1, 1 - u)
            keep_y(T - 3, 1)
            copy_turned(T - 1, 1)
            keep_y(T - 2, 0)
            keep_y(T - 1, 1)
            act.wait_ge(s_sums, 1)
            nc.scalar.activation(sums[:], ps_s[:, 0:2 * C], ACT.Copy)

        @block.tensor
        def _(pe):
            pe.wait_ge(s_zero, 1)
            nc.tensor.matmul(ps_s[:, 0:2 * C], ones[:], ysq[:, 0].rearrange("p a c -> p (a c)"), start=True, stop=False,
                             skip_group_check=True).then_inc(s_sum, 1)
            pe.sem_inc(s_sum, 1)
            pe.sem_inc(s_evac, BANKS)
            pe.wait_ge(s_w, 32)

            def turn(t, u):
                pe.wait_ge(s_samp, t + 1)
                for q in range(BANKS):
                    pe.wait_ge(s_evac, t * BANKS + q + 1)
                    for j, m in enumerate(blocks[q]):
                        last = nc.tensor.transpose(ps_t[q][0:rows(m), j * P:(j + 1) * P],
                                                   samp[:, u, m * P:m * P + rows(m)], ident[:])
                    last.then_inc(s_turn, 1)
                pe.wait_ge(s_turn, (t + 1) * BANKS)
                pe.sem_inc(s_sfree, 1)

            def conv(t, u):
                pe.wait_ge(s_evac, BANKS + (t + 1) * BANKS)
                pe.wait_ge(s_y, t + 1)
                for m in range(CONV_M):
                    last = nc.tensor.matmul(ps_y[u][:, 0:C], sampT[0:rows(m), u, m * P:(m + 1) * P],
                                            wconv[0:rows(m), m, :], start=(m == 0), stop=(m == CONV_M - 1))
                last.then_inc(s_conv, 1)

            def add_sums(t, u):
                pe.wait_ge(s_y, 2 + t + 1)
                return nc.tensor.matmul(ps_s[:, 0:2 * C], ones[:], ysq[:, u].rearrange("p a c -> p (a c)"),
                                        start=False, stop=False, skip_group_check=True).then_inc(s_sum, 1)

            pe.sem_inc(s_y, 2)
            turn(0, 0)
            turn(1, 1)
            conv(0, 0)
            turn(2, 0)
            conv(1, 1)
            turn(3, 1)
            conv(2, 0)
            add_sums(0, 0)
            with pe.Fori(2, T // 2) as i:
                for u in range(2):
                    turn(2 * i + u, u)
                    conv(2 * i + u - 1, 1 - u)
                    add_sums(2 * i + u - 3, 1 - u)
            add_sums(T - 3, 1)
            conv(T - 1, 1)
            add_sums(T - 2, 0)
            add_sums(T - 1, 1)
            pe.wait_ge(s_sum, 2 + T)
            pe.sem_inc(s_sums, 1)


def stage_batchnorm(nc, io, X, Y, sums, st):
    with ExitStack() as ctx:
        k = Kit(nc, ctx, "bn")
        par = k.sb("par", [P, 3, C])
        mean, var, scale, shift = (k.sb(n, [P, 1, C]) for n in ("mean", "var", "scale", "shift"))
        s_in, s_ch, s_var, s_sd = k.sem("loaded"), k.sem("dve_chain"), k.sem("variance_ready"), k.sem("std_ready")
        s_mul, s_z, s_gelu, s_add = k.sem("scaled"), k.sem("normalised"), k.sem("gelu_done"), k.sem("added")
        s_aff = k.sem("scale_shift_ready")
        block = ctx.enter_context(nc.Block())
        GRP = 8

        @block.sync
        def _(sp):
            for n, name in enumerate(("gamma", "beta", "conv_b")):
                sp.dma_start(par[:, n, :], io[name].to_broadcast([P, C])).then_inc(s_in, 16)

        @block.vector
        def _(dve):
            v, ch = nc.vector, Count(dve, s_ch)
            m, q, sc, sh = mean[:, 0], var[:, 0], scale[:, 0], shift[:, 0]
            dve.wait_ge(s_in, 48)
            ch.link(v.tensor_scalar(m, sums[:, 0:C], 1.0 / NTOK, None, ALU.mult))
            ch.link(v.tensor_scalar(q, sums[:, C:2 * C], 1.0 / NTOK, None, ALU.mult))
            ch.link(v.tensor_tensor(sc, m, m, ALU.mult))
            ch.link(v.tensor_tensor(q, q, sc, ALU.subtract))
            ch.link(v.tensor_scalar(q, q, 0.0, 1e-5, ALU.max, ALU.add))
            dve.sem_inc(s_var, 1)
            ch.link(v.tensor_tensor(sh, m, par[:, 2], ALU.add))
            ch.link(v.tensor_tensor(sh, par[:, 2], sh, ALU.subtract))
            dve.wait_ge(s_sd, 1)
            ch.link(v.reciprocal(q, q))
            ch.link(v.tensor_tensor(sc, q, par[:, 0], ALU.mult))
            ch.link(v.tensor_tensor(sh, sh, sc, ALU.mult))
            ch.link(v.tensor_tensor(sh, sh, par[:, 1], ALU.add))

            dve.sem_inc(s_aff, 1)

            def scaled(g):
                y = Y[:, at(g * GRP, GRP), :]
                v.tensor_tensor(y, y, scale[:].to_broadcast([P, GRP, C]), ALU.mult).then_inc(s_mul, 1)

            def add_back(g):
                dve.wait_ge(s_gelu, g + 1)
                x = X[:, at(g * GRP, GRP), :]
                v.tensor_tensor(x, x, Y[:, at(g * GRP, GRP), :], ALU.add).then_inc(s_add, 1)

            def stats(g):
                dve.wait_ge(s_add, g + 1)
                for j in range(GRP):
                    v.bn_stats(st[:, at(g * GRP + j), :], X[:, at(g * GRP + j), :])

            G = T // GRP
            scaled(0)
            scaled(1)
            with dve.Fori(2, G) as g:
                scaled(g)
                add_back(g - 2)
                stats(g - 2)
            for g in (G - 2, G - 1):
                add_back(g)
                stats(g)

        @block.gpsimd
        def _(pool):
            pool.wait_ge(s_aff, 1)
            with pool.Fori(0, T // GRP) as g:
                pool.wait_ge(s_mul, g + 1)
                y = Y[:, at(g * GRP, GRP), :]
                nc.gpsimd.tensor_tensor(y, y, shift[:].to_broadcast([P, GRP, C]), ALU.add).then_inc(s_z, 1)

        @block.scalar
        def _(act):
            act.wait_ge(s_var, 1)
            nc.scalar.activation(var[:, 0], var[:, 0], ACT.Sqrt).then_inc(s_sd, 1)
            with act.Fori(0, T // GRP) as g:
                act.wait_ge(s_z, g + 1)
                y = Y[:, at(g * GRP, GRP), :]
                nc.scalar.activation(y, y, ACT.Gelu).then_inc(s_gelu, 1)


def stage_route(nc, io, tag, X, st, xh, xl, xb, comb_t, ident, eps, router, nexp, topk, shared_bias=None):
    with ExitStack() as ctx:
        k = Kit(nc, ctx, tag)
        RING = 4
        NR = router.shape[1]
        mean, rstd, tmp = k.sb("mean", [P, T]), k.sb("rstd", [P, T]), k.sb("tmp", [P, T])
        xd = k.sb("xd", [P, RING, C])
        xf = k.sb("xf", [P, RING, 2 * P])
        ra, rb = k.sb("ra", [P, NR]), k.sb("rb", [CB, NR])
        prob = k.sb("prob", [P, T, LG])
        rest = k.sb("rest", [P, T, LG])
        top = k.sb("top", [P, T, 8])
        red = k.sb("red", [P, T])
        sgb = k.sb("sgb", [P, 1])
        comb = k.sb("comb", [P, T, LG])
        combt = k.sb("combt", [LG, NTOK])
        NC = nexp + (shared_bias is not None)
        ps_t = [k.ps(f"t{i}") for i in range(RING)]
        ps_l = k.ps("logits", [P, T * LG])
        s_w, s_ch = k.sem("router_loaded"), k.sem("dve_chain")
        s_var, s_sd, s_xd = k.sem("variance_ready"), k.sem("std_ready"), k.sem("tile_normalised")
        s_tp, s_hi, s_lo, s_log = k.sem("transposed"), k.sem("hi_ready"), k.sem("lo_ready"), k.sem("logits_ready")
        s_comb, s_ct, s_cc, s_st = k.sem("comb_ready"), k.sem("comb_turned"), k.sem("comb_copied"), k.sem("comb_stored")
        s_sub, s_exp, s_sgb = k.sem("logits_shifted"), k.sem("exp_done"), k.sem("bias_loaded")
        block = ctx.enter_context(nc.Block())

        @block.sync
        def _(sp):
            sp.dma_start(ra[:], router[0:CA]).then_inc(s_w, 16)
            sp.dma_start(rb[:], router[CA:C]).then_inc(s_w, 16)
            if shared_bias is not None:
                sp.dma_start(sgb[:], shared_bias.to_broadcast([P, 1])).then_inc(s_sgb, 16)
            sp.wait_ge(s_cc, 1 + T // RING)
            sp.dma_start(comb_t[0:NC], combt[0:NC, :]).then_inc(s_st, 16)
            sp.wait_ge(s_st, 16)

        @block.vector
        def _(dve):
            v, ch = nc.vector, Count(dve, s_ch)
            finish_stats(v, ch, st, mean[:], rstd[:], tmp[:], eps)
            dve.sem_inc(s_var, 1)
            dve.wait_ge(s_sd, 1)
            ch.link(v.reciprocal(rstd[:], rstd[:]))

            def normalise(t, r):
                m, s = mean[:, at(t)], rstd[:, at(t)]
                v.tensor_scalar(xd[:, r, :], X[:, at(t), :], m, s, ALU.subtract, ALU.mult).then_inc(s_xd, 1)

            def low(t, r):
                dve.wait_ge(s_hi, t + 1)
                cols = at(t * P, P)
                v.tensor_tensor(xl[:, cols], ps_t[r][:, 0:P], xh[:, cols], ALU.subtract)
                v.tensor_tensor(xb[CB:P, cols], ps_t[r][CB:P, P:2 * P], xb[CB:P, cols], ALU.subtract).then_inc(s_lo, 1)

            SKEW = 3
            for t in range(RING):
                normalise(t, t)
                if t >= SKEW:
                    low(t - SKEW, t - SKEW)
            with dve.Fori(1, T // RING) as q:
                for r in range(RING):
                    normalise(RING * q + r, r)
                    low(RING * q + r - SKEW, (r - SKEW) % RING)
            for t in range(T - SKEW, T):
                low(t, t % RING)

            lg = ps_l[:].rearrange("p (t e) -> p t e", e=LG)
            dve.wait_ge(s_log, RING + T)
            ch.link(v.tensor_reduce(red[:], lg[:, :, 0:nexp], AX.X, ALU.max))
            ch.link(v.tensor_tensor(prob[:, :, 0:nexp], lg[:, :, 0:nexp], bc(red[:], nexp), ALU.subtract))
            if shared_bias is not None:
                dve.wait_ge(s_sgb, 16)
                ch.link(v.tensor_scalar(prob[:, :, nexp], lg[:, :, nexp], sgb[:, 0:1], -1.0, ALU.add, ALU.mult))
            dve.sem_inc(s_sub, 1)
            dve.wait_ge(s_exp, 1)
            if topk < 8:
                for j in range(8 - topk):
                    last = v.memset(prob[:, :, nexp + 1 + j:nexp + 2 + j], -2.0 - j)
                ch.link(last)
            width = nexp if topk == 8 else nexp + 1 + 8 - topk
            for t in range(T):
                last = v.max(top[:, t, :], prob[:, t, 0:nexp])
            ch.link(last)
            if topk < 8:
                for j in range(8 - topk):
                    last = v.memset(top[:, :, topk + j:topk + j + 1], -2.0 - j)
                ch.link(last)
            for t in range(T):
                last = v.match_replace(rest[:, t, 0:width], top[:, t, :], prob[:, t, 0:width], -1.0)
            ch.link(last)
            ch.link(v.scalar_tensor_tensor(out=comb[:, :, 0:nexp], in0=rest[:, :, 0:nexp], scalar=0.0,
                                           in1=prob[:, :, 0:nexp], op0=ALU.is_lt, op1=ALU.mult))
            ch.link(v.tensor_reduce(red[:], comb[:, :, 0:nexp], AX.X, ALU.add))
            ch.link(v.reciprocal(red[:], red[:]))
            if shared_bias is not None:
                ch.link(v.tensor_scalar(tmp[:], prob[:, :, nexp], 1.0, None, ALU.add))
                ch.link(v.reciprocal(tmp[:], tmp[:]))
                ch.link(v.tensor_copy(comb[:, :, nexp], tmp[:]))
                ch.link(v.tensor_scalar(tmp[:], tmp[:], -1.0, 1.0, ALU.mult, ALU.add))
                ch.link(v.tensor_tensor(red[:], red[:], tmp[:], ALU.mult))
            ch.link(v.tensor_tensor(comb[:, :, 0:nexp], comb[:, :, 0:nexp], bc(red[:], nexp), ALU.mult))
            dve.sem_inc(s_comb, 1)

        @block.scalar
        def _(act):
            act.wait_ge(s_var, 1)
            nc.scalar.activation(rstd[:], rstd[:], ACT.Sqrt).then_inc(s_sd, 1)
            with act.Fori(0, T // RING) as q:
                for r in range(RING):
                    t = RING * q + r
                    cols = at(t * P, P)
                    act.wait_ge(s_tp, t + 1)
                    act.wait_ge(s_log, t + 1)
                    nc.scalar.activation(xh[:, cols], ps_t[r][:, 0:P], ACT.Copy)
                    nc.scalar.activation(xb[:, cols], ps_t[r][:, P:2 * P], ACT.Copy)
                    nc.scalar.activation(xf[:, r, :], ps_t[r][:, 0:2 * P], ACT.Copy).then_inc(s_hi, 1)
            act.wait_ge(s_sub, 1)
            width = nexp + (shared_bias is not None)
            nc.scalar.activation(prob[:, :, 0:width], prob[:, :, 0:width], ACT.Exp).then_inc(s_exp, 1)
            for q in range(T // RING):
                act.wait_ge(s_ct, q + 1)
                nc.scalar.activation(combt[0:NC, q * RING * P:(q + 1) * RING * P], ps_t[q % RING][0:NC, :],
                                     ACT.Copy).then_inc(s_cc, 1)

        @block.tensor
        def _(pe):
            pe.sem_inc(s_lo, RING)
            pe.sem_inc(s_log, RING)
            pe.wait_ge(s_w, 32)

            def turn(t, r):
                pe.wait_ge(s_xd, t + 1)
                pe.wait_ge(s_lo, t + 1)
                turn_tile(nc, ps_t[r], xd[:, r, :], ident).then_inc(s_tp, 1)

            def logits(t, r):
                pe.wait_ge(s_hi, t + 1)
                out = ps_l[:, at(t * LG, NR)]
                nc.tensor.matmul(out, xf[:, r, 0:P], ra[:], start=True, stop=False)
                nc.tensor.matmul(out, xf[0:CB, r, P:2 * P], rb[:], start=False, stop=True).then_inc(s_log, 1)

            BEHIND = 3
            for t in range(RING):
                turn(t, t)
                if t >= BEHIND:
                    logits(t - BEHIND, t - BEHIND)
            with pe.Fori(1, T // RING) as q:
                for r in range(RING):
                    turn(RING * q + r, r)
                    logits(RING * q + r - BEHIND, (r - BEHIND) % RING)
            for t in range(T - BEHIND, T):
                logits(t, t % RING)
            pe.sem_inc(s_cc, 1)
            pe.wait_ge(s_comb, 1)
            for q in range(T // RING):
                if q >= RING:
                    pe.wait_ge(s_cc, 1 + q - RING + 1)
                for j in range(RING):
                    last = nc.tensor.transpose(ps_t[q % RING][0:NC, j * P:(j + 1) * P], comb[:, q * RING + j, 0:NC], ident[:])
                last.then_inc(s_ct, 1)


PIECE = 768


def split_parts(src, p0, hi, lo):
    n = src.shape[0]
    for c in range(0, src.shape[1], PIECE):
        d = min(c + PIECE, src.shape[1])
        yield src[:, c:d], p0, d - c, hi[p0:p0 + n, c:d], None if lo is None else lo[p0:p0 + n, c:d]


def split_up(src, wa_h, wa_l, wbb, wbl):
    yield from split_parts(src[0:CA], 0, wa_h, wa_l)
    yield from split_parts(src[CA:C], 0, wbb, wbl)
    yield from split_parts(src[CA:C], CB, wbb, None)


def split_down(src, hi, lo):
    step = PIECE // C
    for n in range(0, src.shape[0] // P, step):
        m = min(n + step, src.shape[0] // P)
        yield (src[n * P:m * P].rearrange("(n p) c -> p n c", p=P), 0, (m - n) * C,
               hi[:, n:m].rearrange("p n c -> p (n c)"), lo[:, n:m].rearrange("p n c -> p (n c)"))


def stage_split(nc, tag, parts):
    with ExitStack() as ctx:
        k = Kit(nc, ctx, tag)
        NB = 4
        buf = k.sb("buf", [P, NB, PIECE])
        s_in = [k.sem(f"loaded{i}") for i in range(NB)]
        s_hi, s_done = k.sem("hi_made"), k.sem("piece_split")
        block = ctx.enter_context(nc.Block())
        full = [n for n, part in enumerate(parts) if part[4] is not None]

        def piece(n):
            _, p0, w, hi, _ = parts[n]
            return buf[p0:p0 + hi.shape[0], n % NB, 0:w]

        @block.sync
        def _(sp):
            for n, (src, p0, w, hi, lo) in enumerate(parts):
                if n >= NB:
                    sp.wait_ge(s_done, n - NB + 1)
                dst = piece(n)
                if len(src.shape) == 3:
                    dst = dst.rearrange("p (n c) -> p n c", c=C)
                sp.dma_start(dst, src).then_inc(s_in[n % NB], 16)

        @block.scalar
        def _(act):
            for n in full:
                act.wait_ge(s_in[n % NB], 16 * (n // NB + 1))
                nc.scalar.activation(parts[n][3], piece(n), ACT.Copy).then_inc(s_hi, 1)

        @block.vector
        def _(dve):
            for n, (src, p0, w, hi, lo) in enumerate(parts):
                dve.wait_ge(s_in[n % NB], 16 * (n // NB + 1))
                if lo is None:
                    nc.vector.tensor_copy(hi, piece(n)).then_inc(s_done, 1)
                else:
                    dve.wait_ge(s_hi, full.index(n) + 1)
                    nc.vector.tensor_tensor(lo, piece(n), hi, ALU.subtract).then_inc(s_done, 1)


def stage_ffn(nc, tag, X, xh, xl, xb, comb_t, up, gate, down, loads, func, st=None, out=None):
    with ExitStack() as ctx:
        k = Kit(nc, ctx, tag)
        NH, NL = down[0].shape[1], len(loads)
        SKEW, HB = (2, 3) if gate else (3, 4)
        assert NH % HB == 0 and HB > SKEW
        hf = k.sb("hf", [P, HB, CHUNK])
        hg = k.sb("hg", [P, 2, CHUNK]) if gate else None
        hc = k.sb("hc", [P, 2, CHUNK]) if gate else None
        hh = k.sb("hh", [P, HB, CHUNK], F16)
        hl = k.sb("hl", [P, HB, CHUNK], F16)
        acc = k.sb("acc", [P, TC, C]) if out is not None else None
        coef = k.sb("coef", [P, NL, CHUNK])
        NPS = 2 if gate else 4
        ps_u = [k.ps(f"up{i}") for i in range(NPS)]
        ps_g = [k.ps(f"gate{i}") for i in range(NPS)] if gate else None
        ps_o = [k.ps(f"out{j}") for j in range(TC)]
        CG = 4
        s_coef = [k.sem(f"coefs_loaded{q}") for q in range(-(-NL // CG))]
        s_up, s_gate = k.sem("up_ready"), k.sem("gate_ready")
        s_act, s_mul, s_hf = k.sem("activated"), k.sem("up_scaled"), k.sem("hidden_ready")
        s_hh, s_hl, s_used = k.sem("hi_ready"), k.sem("lo_ready"), k.sem("hidden_used")
        s_acc, s_out = k.sem("accumulated"), k.sem("stored")
        block = ctx.enter_context(nc.Block())
        load_of = {blk: n for n, (_, blks) in enumerate(loads) for blk in blks}
        group_dmas = [sum(len(rows) for rows, _ in loads[q * CG:(q + 1) * CG]) for q in range(len(s_coef))]
        last_block = [loads[min((q + 1) * CG, NL) - 1][1][-1] for q in range(len(s_coef))]

        @block.sync
        def _(sp):
            sp.sem_inc(s_hf, HB)

            def load(i, q):
                tok = ((i % NCHUNK) if not isinstance(i, int) else i % NCHUNK) * CHUNK
                for n in range(q * CG, min((q + 1) * CG, NL)):
                    for e, r0, r1 in loads[n][0]:
                        sp.dma_start(coef[r0:r1, n, :], comb_t[e:e + 1, at(tok, CHUNK)].to_broadcast([r1 - r0, CHUNK]))\
                          .then_inc(s_coef[q], 16)

            for q in range(len(s_coef)):
                load(0, q)
            with sp.Fori(0, NCHUNK) as i:
                for q in range(len(s_coef)):
                    sp.wait_ge(s_hf, HB + i * NH + last_block[q] + 1)
                    load(i + 1, q)
                if out is not None:
                    sp.wait_ge(s_acc, (i + 2) * TC)
                    sp.dma_start(out[at(i * CHUNK, CHUNK)].rearrange("(t p) c -> p t c", p=P), acc[:]).then_inc(s_out, 16)
            if out is not None:
                sp.wait_ge(s_out, 1 + 16 * NCHUNK)
            for q in range(len(s_coef)):
                sp.wait_ge(s_coef[q], 16 * group_dmas[q] * (NCHUNK + 1))

        @block.tensor
        def _(pe):
            pe.sem_inc(s_hl, 1)
            pe.sem_inc(s_acc, TC)
            if out is not None:
                pe.sem_inc(s_out, 1)

            def product(ps, w, n, cols):
                wa_h, wa_l, wbb, wbl = w
                c = slice(n * P, (n + 1) * P)
                nc.tensor.matmul(ps[:], wa_h[:, c], xh[:, cols], start=True, stop=False)
                nc.tensor.matmul(ps[:], wa_h[:, c], xl[:, cols], start=False, stop=False)
                nc.tensor.matmul(ps[:], wa_l[:, c], xh[:, cols], start=False, stop=False)
                nc.tensor.matmul(ps[:], wbb[:, c], xb[:, cols], start=False, stop=False)
                return nc.tensor.matmul(ps[:], wbl[0:CB, c], xb[0:CB, cols], start=False, stop=True)

            def hidden(i, m, prologue=False):
                n = m % NH
                cols = at((i + 1) % NCHUNK * CHUNK if m >= NH else i * CHUNK, CHUNK)
                if not prologue or m >= NPS:
                    pe.wait_ge(s_hf, HB - NPS + i * NH + m + 1)
                if gate:
                    product(ps_g[n % NPS], gate, n, cols).then_inc(s_gate, 1)
                product(ps_u[n % NPS], up, n, cols).then_inc(s_up, 1)

            def expert(i, n):
                pe.wait_ge(s_hl, 1 + i * NH + n + 1)
                s = n % HB
                for j in range(TC):
                    tok = slice(j * P, (j + 1) * P)
                    if n == 0:
                        pe.wait_ge(s_acc, i * TC + j + 1)
                    for m, (a, b) in enumerate(((hh, down[0]), (hh, down[1]), (hl, down[0]))):
                        last = nc.tensor.matmul(ps_o[j][:, 0:C], a[:, s, tok], b[:, n, :],
                                                start=(n == 0 and m == 0), stop=(n == NH - 1 and m == 2))
                last.then_inc(s_used, 1)

            for m in range(SKEW):
                hidden(0, m, True)
            with pe.Fori(0, NCHUNK) as i:
                for n in range(NH):
                    hidden(i, n + SKEW)
                    expert(i, n)

        @block.scalar
        def _(act):
            act.sem_inc(s_used, HB)

            def activate(b, n):
                if gate:
                    act.wait_ge(s_gate, b + 1)
                    act.wait_ge(s_hf, HB - 2 + b + 1)
                    nc.scalar.activation(hg[:, n % 2], ps_g[n % NPS][:], func).then_inc(s_act, 1)
                else:
                    act.wait_ge(s_up, b + 1)
                    act.wait_ge(s_used, b + 1)
                    nc.scalar.activation(hf[:, n % HB], ps_u[n % NPS][:], func).then_inc(s_act, 1)

            def high(b, n):
                act.wait_ge(s_hf, HB + b + 1)
                act.wait_ge(s_used, b + 1)
                nc.scalar.activation(hh[:, n % HB], hf[:, n % HB], ACT.Copy).then_inc(s_hh, 1)

            activate(0, 0)
            with act.Fori(0, NCHUNK) as i:
                for n in range(NH):
                    activate(i * NH + n + 1, (n + 1) % NH)
                    high(i * NH + n, n)
            for m in range(SKEW - 1):
                activate(NCHUNK * NH + m + 1, m + 1)
                high(NCHUNK * NH + m, m)

        @block.vector
        def _(dve):
            v = nc.vector

            def scale(i, m):
                n, b = m % NH, i * NH + m
                q = load_of[n] // CG
                if n == 0 or load_of[n - 1] // CG != q:
                    dve.wait_ge(s_coef[q], 16 * group_dmas[q] * (i + 1 + m // NH))
                c = coef[:, load_of[n], :]
                if gate:
                    dve.wait_ge(s_up, b + 1)
                    v.tensor_tensor(hc[:, n % 2], c, ps_u[n % NPS][:], ALU.mult).then_inc(s_mul, 1)
                    dve.wait_ge(s_act, b + 1)
                    dve.wait_ge(s_mul, b + 1)
                    dve.wait_ge(s_used, b + 1)
                    v.tensor_tensor(hf[:, n % HB], hg[:, n % 2], hc[:, n % 2], ALU.mult).then_inc(s_hf, 1)
                else:
                    dve.wait_ge(s_act, b + 1)
                    v.tensor_tensor(hf[:, n % HB], hf[:, n % HB], c, ALU.mult).then_inc(s_hf, 1)

            def low(b, n):
                dve.wait_ge(s_hh, b + 1)
                v.tensor_tensor(hl[:, n % HB], hf[:, n % HB], hh[:, n % HB], ALU.subtract).then_inc(s_hl, 1)

            scale(0, 0)
            for m in range(1, SKEW):
                scale(0, m)
                low(m - 1, m - 1)
            with dve.Fori(0, NCHUNK) as i:
                for n in range(NH):
                    m = n + SKEW
                    scale(i, m)
                    low(i * NH + m - 1, (m - 1) % NH)
                dve.wait_ge(s_used, HB + (i + 1) * NH)
                for j in range(TC):
                    x = X[:, at(i * TC + j), :]
                    if out is not None and j == 0:
                        dve.wait_ge(s_out, 1 + 16 * i)
                    v.tensor_tensor(x if out is None else acc[:, j, :].unsqueeze(1), ps_o[j][:, 0:C].unsqueeze(1), x,
                                    ALU.add).then_inc(s_acc, 1)
                if st is not None:
                    dve.wait_ge(s_acc, TC + (i + 1) * TC)
                    for j in range(TC):
                        v.bn_stats(st[:, at(i * TC + j), :], X[:, at(i * TC + j), :])
            dve.wait_ge(s_hl, 1 + NCHUNK * NH + SKEW - 1)


def stage_attention(nc, io, X, st, ident, ones):
    with ExitStack() as ctx:
        k = Kit(nc, ctx, "att")
        RING, HALF = 4, CHUNK
        N = H * W
        HT = TI * HEADS
        mean, rstd, tmp = k.sb("mean", [P, T]), k.sb("rstd", [P, T]), k.sb("tmp", [P, T])
        xd = k.sb("xd", [P, RING, C])
        xt = k.sb("xt", [P, 2, N])
        w = k.sb("w", [P, 2, 2, N])
        w2 = k.sb("w2", [P, 2, 2, N])
        val = k.sb("val", [P, 2, N])
        scr = k.sb("scr", [P, 2, HALF])
        pib = k.sb("pi_channels", [P, 2, 2, HALF])
        wq, wo, wos = k.sb("wq", [P, 2, C]), k.sb("wo", [P, 2, C]), k.sb("wos", [P, 2, C])
        hm, rm = k.sb("headmask", [P, 2, HEADS]), k.sb("rm", [P, 2, HEADS])
        temp = k.sb("temp", [P, 1, HEADS])
        ob = k.sb("ob", [1, C])
        ssq = k.sb("ssq", [P, 2, 2, 2])
        rn = k.sb("rn", [P, 2])
        z, pi = k.sb("z", [P, TI, HEADS]), k.sb("pi", [P, TI, HEADS])
        red = k.sb("red", [P, TI])
        pe_ = k.sb("pi_spread", [P, TI, C])
        dot, psum_pi, att = k.sb("dot", [P, 2, 2]), k.sb("sum_pi", [P, 2, 2]), k.sb("attn", [P, 2, 2])
        ps_t = [k.ps("ta"), k.ps("tb")]
        ps_q = [[k.ps(f"q{h}{b}") for b in "ab"] for h in range(2)]
        ps_s, ps_o = k.ps("s"), k.ps("o")
        out_pair = (ps_o[:, 0:2 * C], ps_s[:, P:P + 2 * C])
        ROWSB = (P, CB)
        c0 = (0, CA)
        s_in, s_ch0, s_ch = k.sem("loaded"), k.sem("setup_chain"), k.sem("dve_chain")
        s_var, s_sd, s_xd = k.sem("variance_ready"), k.sem("std_ready"), k.sem("tile_normalised")
        s_turn, s_xt, s_q, s_w = k.sem("half_turned"), k.sem("half_copied"), k.sem("qkv_half"), k.sem("w_half_kept")
        s_r, s_s, s_sub, s_exp = k.sem("norms_ready"), k.sem("head_sums"), k.sem("logits_shifted"), k.sem("exp_done")
        s_pe, s_p, s_vh, s_sum = k.sem("pi_spread"), k.sem("pi_turned"), k.sem("values_half"), k.sem("pi_summed")
        s_fold, s_o, s_add = k.sem("weights_scaled"), k.sem("out_pair"), k.sem("pair_added")
        block = ctx.enter_context(nc.Block())

        def images(eng, step):
            step(0, 0, now=True)
            step(1, 1, now=True, before=True)
            with eng.Fori(1, NIMG // 2) as i:
                step(2 * i, 0, now=True, before=True, last=True)
                step(2 * i + 1, 1, now=True, before=True, last=True)
            step(NIMG, 0, before=True, last=True)
            step(NIMG + 1, 1, last=True)

        @block.sync
        def _(sp):
            for name, dst in (("qkv", wq), ("out_w", wo), ("headmask", hm)):
                for b in range(2):
                    sp.dma_start(dst[0:ROWSB[b], b, :], io[name][c0[b]:c0[b] + ROWSB[b]]).then_inc(s_in, 16)
            sp.dma_start(temp[:, 0, :], io["temp"].to_broadcast([P, HEADS])).then_inc(s_in, 16)
            sp.dma_start(ob[:], io["out_b"]).then_inc(s_in, 16)

        @block.vector
        def _(dve):
            v, c = nc.vector, Count(dve, s_ch0)
            finish_stats(v, c, st, mean[:], rstd[:], tmp[:], 1e-6)
            dve.sem_inc(s_var, 1)
            dve.wait_ge(s_sd, 1)
            c.link(v.reciprocal(rstd[:], rstd[:]))
            dve.wait_ge(s_in, 128)
            HEAD, SOFT, LINKS = 8, 6, 21

            def norm(g):
                for j in range(TI):
                    dve.wait_ge(s_turn, 1 + 2 * g + j // RING)
                    t = g * TI + j
                    v.tensor_scalar(xd[:, j % RING], X[:, at(t), :], mean[:, at(t)], rstd[:, at(t)],
                                    ALU.subtract, ALU.mult).then_inc(s_xd, 1)

            def head(g, u, ch):
                dve.wait_ge(s_w, 1 + 2 * g + 2)
                dve.wait_ge(s_s, 1 + g)
                for b in range(2):
                    r = slice(0, ROWSB[b])
                    ch.link(v.tensor_tensor(rn[r, b:b + 1], ssq[r, u, b, 0:1], ssq[r, u, b, 1:2], ALU.add))
                    ch.link(v.tensor_scalar(rn[r, b:b + 1], rn[r, b:b + 1], 1e-24, None, ALU.max))
                    ch.link(v.reciprocal(rn[r, b:b + 1], rn[r, b:b + 1]))
                    ch.link(v.tensor_scalar(rm[r, b], hm[r, b], rn[r, b:b + 1], None, ALU.mult))
                dve.sem_inc(s_r, 1)

            def softmax(g, ch):
                dve.wait_ge(s_s, 1 + g + 1)
                lg = ps_s[:, 0:HT].rearrange("p (t h) -> p t h", h=HEADS)
                ch.link(v.tensor_tensor(z[:], lg, temp[:].to_broadcast([P, TI, HEADS]), ALU.mult))
                ch.link(v.tensor_reduce(red[:], z[:], AX.X, ALU.max))
                ch.link(v.tensor_tensor(z[:], z[:], bc(red[:], HEADS), ALU.subtract))
                dve.sem_inc(s_sub, 1)
                dve.wait_ge(s_exp, g + 1)
                ch.link(v.tensor_reduce(red[:], z[:], AX.X, ALU.add))
                ch.link(v.reciprocal(red[:], red[:]))
                ch.link(v.tensor_tensor(pi[:], z[:], bc(red[:], HEADS), ALU.mult))
                dve.wait_ge(s_p, 1 + 2 * g)
                v.tensor_copy(pe_[:].rearrange("p t (h d) -> p (t h) d", d=DH),
                              bc(pi[:].rearrange("p t h -> p (t h)"), DH)).then_inc(s_pe, 1)

            def values(g, u, ch):
                dve.wait_ge(s_o, 1 + 4 * g)
                for h in range(2):
                    dve.wait_ge(s_sum, 1 + 2 * g + h + 1)
                    cols = slice(h * HALF, (h + 1) * HALF)
                    for b in range(2):
                        r = slice(0, ROWSB[b])
                        v.tensor_tensor(val[r, b, cols], w[r, u, b, cols], pib[r, h, b], ALU.mult)
                        last = v.scalar_tensor_tensor(out=scr[r, b], in0=w2[r, u, b, cols], scalar=1.0, in1=pib[r, h, b],
                                                      op0=ALU.mult, op1=ALU.mult, accum_out=dot[r, b, h:h + 1])
                    last.then_inc(s_vh, 1)
                    dve.wait_ge(s_vh, 2 * g + h + 1)
                a, s = att[:, :, 0], att[:, :, 1]
                ch.link(v.tensor_tensor(a, dot[:, :, 0], dot[:, :, 1], ALU.add))
                ch.link(v.scalar_tensor_tensor(out=s, in0=psum_pi[:, :, 0], scalar=1e-8, in1=psum_pi[:, :, 1],
                                               op0=ALU.add, op1=ALU.add))
                ch.link(v.reciprocal(s, s))
                ch.link(v.tensor_tensor(a, a, s, ALU.mult))
                ch.link(v.tensor_scalar(a, a, 1.0, None, ALU.add))
                ch.link(v.reciprocal(a, a))
                for b in range(2):
                    r = slice(0, ROWSB[b])
                    last = v.tensor_scalar(wos[r, b], wo[r, b], att[r, b, 0:1], -1.0, ALU.mult, ALU.mult)
                ch.link(last)
                dve.sem_inc(s_fold, 1)

            def add(g):
                for r in range(TI // 2):
                    dve.wait_ge(s_o, 1 + 4 * g + r + 1)
                    x = X[:, at(g * TI + 2 * r, 2), :]
                    v.tensor_tensor(x, out_pair[r % 2].rearrange("p (t c) -> p t c", c=C), x, ALU.add).then_inc(s_add, 1)

            for t_ in (dot, psum_pi):
                last = v.memset(t_[:], 0.0)
            c.link(last)
            dve.sem_inc(s_sum, 1)

            def stats(g):
                dve.wait_ge(s_add, 2 + 4 * g + 4)
                for j in range(TI):
                    v.bn_stats(st[:, at(g * TI + j), :], X[:, at(g * TI + j), :])

            def step(g, u, now=False, before=False, last=False):
                ch = Count(dve, s_ch)
                ch.n = HEAD + SOFT + (g - 2) * LINKS if last else 0
                if before:
                    head(g - 1, 1 - u, ch)
                if now:
                    norm(g)
                if last:
                    values(g - 2, u, ch)
                if before:
                    softmax(g - 1, ch)
                if last:
                    add(g - 2)
                    stats(g - 2)

            images(dve, step)

        @block.scalar
        def _(act):
            act.wait_ge(s_var, 1)
            nc.scalar.activation(rstd[:], rstd[:], ACT.Sqrt).then_inc(s_sd, 1)
            act.wait_ge(s_sum, 1)

            def copy_turned(g):
                for h in range(2):
                    act.wait_ge(s_turn, 1 + 2 * g + h + 1)
                    act.wait_ge(s_q, 1 + 2 * g)
                    for b in range(2):
                        r = slice(0, ROWSB[b])
                        last = nc.scalar.activation(xt[r, b, h * HALF:(h + 1) * HALF], ps_t[b][r, :], ACT.Copy)
                    last.then_inc(s_xt, 1)

            def keep_w(g, u):
                act.wait_ge(s_fold, g + 1)
                for h in range(2):
                    act.wait_ge(s_q, 1 + 2 * g + h + 1)
                    cols = slice(h * HALF, (h + 1) * HALF)
                    for b in range(2):
                        r = slice(0, ROWSB[b])
                        nc.scalar.activation(w[r, u, b, cols], ps_q[h][b][r, :], ACT.Copy)
                        last = nc.scalar.activation(w2[r, u, b, cols], ps_q[h][b][r, :], ACT.Square,
                                                    accum_out=ssq[r, u, b, h:h + 1])
                    last.then_inc(s_w, 1)

            def exp(g):
                act.wait_ge(s_sub, 1 + g + 1)
                nc.scalar.activation(z[:], z[:], ACT.Exp).then_inc(s_exp, 1)

            def sum_pi(g):
                for h in range(2):
                    act.wait_ge(s_p, 1 + 2 * g + h + 1)
                    act.wait_ge(s_fold, 2 + g)
                    act.wait_ge(s_sum, 1 + 2 * g + h)
                    for b in range(2):
                        r = slice(0, ROWSB[b])
                        last = nc.scalar.activation(pib[r, h, b], ps_q[h][b][r, :], ACT.Copy,
                                                    accum_out=psum_pi[r, b, h:h + 1])
                    last.then_inc(s_sum, 1)

            def step(g, u, now=False, before=False, last=False):
                if last:
                    sum_pi(g - 2)
                if now:
                    copy_turned(g)
                if before:
                    exp(g - 1)
                if now:
                    keep_w(g, u)

            images(act, step)

        @block.tensor
        def _(pe):
            pe.sem_inc(s_fold, 2)
            for one in (s_turn, s_q, s_xt, s_w, s_sub, s_s, s_p, s_o, s_add, s_add):
                pe.sem_inc(one, 1)
            pe.wait_ge(s_in, 128)

            def turn_and_project(g):
                for h in range(2):
                    pe.wait_ge(s_xt, 1 + 2 * g + h)
                    for j in range(RING):
                        pe.wait_ge(s_xd, g * TI + h * RING + j + 1)
                        for b in range(2):
                            last = nc.tensor.transpose(ps_t[b][0:ROWSB[b], j * P:(j + 1) * P],
                                                       xd[:, j, c0[b]:c0[b] + ROWSB[b]], ident[:])
                    last.then_inc(s_turn, 1)
                for h in range(2):
                    pe.wait_ge(s_xt, 1 + 2 * g + h + 1)
                    if not isinstance(g, int) or g > 0:
                        pe.wait_ge(s_w, 1 + 2 * g + h - 1)
                    if not isinstance(g, int) or g > 1:
                        pe.wait_ge(s_sum, 1 + 2 * (g - 2) + h + 1)
                    cols = slice(h * HALF, (h + 1) * HALF)
                    for b in range(2):
                        oc = slice(c0[b], c0[b] + ROWSB[b])
                        nc.tensor.matmul(ps_q[h][b][0:ROWSB[b], :], wq[:, 0, oc], xt[:, 0, cols], start=True, stop=False)
                        last = nc.tensor.matmul(ps_q[h][b][0:ROWSB[b], :], wq[0:CB, 1, oc], xt[0:CB, 1, cols],
                                                start=False, stop=True)
                    last.then_inc(s_q, 1)

            def head_sums(g, u):
                pe.wait_ge(s_r, g + 1)
                pe.wait_ge(s_sub, 1 + g)
                if not isinstance(g, int) or g > 1:
                    pe.wait_ge(s_add, 2 + 4 * (g - 2) + 4)
                for j in range(TI):
                    o = ps_s[:, j * HEADS:(j + 1) * HEADS]
                    tok = slice(j * P, (j + 1) * P)
                    nc.tensor.matmul(o, w2[:, u, 0, tok], rm[:, 0], start=True, stop=False)
                    last = nc.tensor.matmul(o, w2[0:CB, u, 1, tok], rm[0:CB, 1], start=False, stop=True)
                last.then_inc(s_s, 1)

            def turn_pi(g):
                pe.wait_ge(s_pe, g + 1)
                for h in range(2):
                    if isinstance(g, int) and g == NIMG - 1:
                        pe.wait_ge(s_sum, 1 + 2 * g + h - 1)
                    else:
                        pe.wait_ge(s_w, 1 + 2 * g + h + 3)
                    for j in range(RING):
                        for b in range(2):
                            last = nc.tensor.transpose(ps_q[h][b][0:ROWSB[b], j * P:(j + 1) * P],
                                                       pe_[:, h * RING + j, c0[b]:c0[b] + ROWSB[b]], ident[:])
                    last.then_inc(s_p, 1)

            def out_project(g):
                pe.wait_ge(s_fold, 2 + g + 1)
                for r in range(TI // 2):
                    pe.wait_ge(s_add, 4 * g + r + 1)
                    if r == 1 and not (isinstance(g, int) and g == NIMG - 1):
                        pe.wait_ge(s_sub, 1 + g + 2)
                    for j in range(2):
                        o = out_pair[r % 2][:, j * C:(j + 1) * C]
                        tok = slice((2 * r + j) * P, (2 * r + j + 1) * P)
                        nc.tensor.matmul(o, ones[0:1, :], ob[:], start=True, stop=False)
                        nc.tensor.matmul(o, val[:, 0, tok], wos[:, 0], start=False, stop=False)
                        last = nc.tensor.matmul(o, val[0:CB, 1, tok], wos[0:CB, 1], start=False, stop=True)
                    last.then_inc(s_o, 1)

            def step(g, u, now=False, before=False, last=False):
                if last:
                    turn_pi(g - 2)
                if before:
                    head_sums(g - 1, 1 - u)
                if now:
                    turn_and_project(g)
                if last:
                    out_project(g - 2)

            images(pe, step)


def program(nc, io, out, stages=99, dbg=None):
    table = nc.dram_tensor("corner_table", (NTOK + FRONT, 4 * C), F32, kind="Internal").ap()
    USED.clear()
    with ExitStack() as ctx:
        k = Kit(nc, ctx, "all")
        X = k.sb("x", [P, T, C])
        Y = k.sb("y", [P, T, C])
        sums = k.sb("sums", [P, 2 * C])
        st = k.sb("st", [P, T, 6])
        ident, ones = k.sb("ident", [P, P]), k.sb("ones", [P, P])
        setup_constants(nc, ident, ones)
        with ExitStack() as conv:
            kc = Kit(nc, conv, "conv")
            wts, idx = kc.sb("wts", [P, T, K9, 4]), kc.sb("idx", [P, T, K9], I32)
            with ExitStack() as early:
                ke = Kit(nc, early, "early")
                om = ke.sb("om", [P, T, NOM])
                stage_offsets(nc, io, X, Y, st, ident, om, table)
                if dbg is not None and stages == 1:
                    return dump(nc, om[:].rearrange("p t o -> p (t o)"), dbg)
                grid = ke.sb("grid", [P, 3, T * K9])
                stage_corners(nc, io, om, grid, wts, idx)
            stage_deform(nc, io, table, wts, idx, Y, ones, ident, sums)
            if dbg is not None and stages == 3:
                return dump(nc, Y[:].rearrange("p t o -> p (t o)"), dbg)
        stage_batchnorm(nc, io, X, Y, sums, st)
        if dbg is not None and stages == 4:
            return dump(nc, X[:].rearrange("p t o -> p (t o)"), dbg)
        turned = Y[:].rearrange("p t c -> p (t c)").bitcast(F16).rearrange("p (a n) -> p a n", a=3)
        xh, xl, xb = turned[:, 0], turned[:, 1], turned[:, 2]
        comb_t = nc.dram_tensor("comb_by_expert", (LG, NTOK), F32, kind="Internal").ap()
        stage_route(nc, io, "route0", X, st, xh, xl, xb, comb_t, ident, 1e-5, io["router0"], E0, 8)
        with ExitStack() as ffn:
            kf = Kit(nc, ffn, "w0")
            up = [kf.sb(n, [P, HID0], F16) for n in ("ah", "al", "bb")] + [kf.sb("bl", [CB, HID0], F16)]
            down = [kf.sb(n, [P, HID0 // P, C], F16) for n in ("dh", "dl")]
            stage_split(nc, "split0", list(split_up(io["w1_0"], *up)) + list(split_down(io["w2_0"], *down)))
            loads, blk = [], 0
            for e, w in enumerate(W0_WIDTHS):
                loads.append(([(e, 0, P)], [blk + j for j in range(w // P)]))
                blk += w // P
            stage_ffn(nc, "ffn0", X, xh, xl, xb, comb_t, up, None, down, loads, ACT.Gelu_apprx_tanh, st)
        if dbg is not None and stages == 5:
            return dump(nc, X[:].rearrange("p t o -> p (t o)"), dbg)
        clear_semaphores(nc)
        stage_attention(nc, io, X, st, ident, ones)
        if dbg is not None and stages == 6:
            return dump(nc, X[:].rearrange("p t o -> p (t o)"), dbg)
        stage_route(nc, io, "route1", X, st, xh, xl, xb, comb_t, ident, 1e-5, io["router1"], E1, 2, io["sg_b"])
        with ExitStack() as ffn:
            kf = Kit(nc, ffn, "w1")
            gate, up = ([kf.sb(f"{g}{n}", [P, HID1], F16) for n in ("ah", "al", "bb")] + [kf.sb(f"{g}bl", [CB, HID1], F16)]
                        for g in ("g", "u"))
            down = [kf.sb(n, [P, HID1 // P, C], F16) for n in ("dh", "dl")]
            parts = []
            for w, routed, shared in ((gate, "wg", "wsg"), (up, "wu", "wsu")):
                parts += split_up(io[routed], *(a[:, 0:HID1R] for a in w))
                parts += split_up(io[shared], *(a[:, HID1R:HID1] for a in w))
            nr = HID1R // P
            parts += split_down(io["wd"], *(a[:, 0:nr] for a in down))
            parts += split_down(io["wsd"], *(a[:, nr:HID1 // P] for a in down))
            stage_split(nc, "split1", parts)
            loads = []
            for e in range(0, E1, 2):
                b = e // 2 * 3
                loads += [([(e, 0, P)], [b]), ([(e, 0, CB), (e + 1, CB, P)], [b + 1]), ([(e + 1, 0, P)], [b + 2])]
            loads.append(([(E1, 0, P)], list(range(nr, HID1 // P))))
            stage_ffn(nc, "ffn1", X, xh, xl, xb, comb_t, up, gate, down, loads, ACT.Silu, out=out)


def setup_constants(nc, ident, ones):
    with ExitStack() as ctx:
        k = Kit(nc, ctx, "const")
        s = k.sem("set")
        block = ctx.enter_context(nc.Block())

        @block.gpsimd
        def _(pool):
            nc.gpsimd.memset(ident[:], 0.0).then_inc(s, 1)
            nc.gpsimd.memset(ones[:], 1.0)
            pool.wait_ge(s, 1)
            nc.gpsimd.affine_select(out=ident[:], in_=ident[:], compare_op=ALU.not_equal, fill=1.0, base=0,
                                    pattern=[[-1, P]], channel_multiplier=1).then_inc(s, 1)
            pool.wait_ge(s, 2)


def dump(nc, ap, dbg):
    with ExitStack() as ctx:
        s = Kit(nc, ctx, "dbg").sem("s")
        block = ctx.enter_context(nc.Block())

        @block.sync
        def _(sp):
            sp.dma_start(dbg, ap).then_inc(s, 16)
            sp.wait_ge(s, 16)


def layouts(i):
    f = np.ascontiguousarray
    ar = {k: np.asarray(v) for k, v in i.items()}
    om_w = np.concatenate([ar["L0_conv_off_w"], ar["L0_conv_mask_w"]], 0).reshape(NOM, C, K9).transpose(1, 2, 0)
    p, t, k = np.meshgrid(np.arange(P), np.arange(T), np.arange(K9), indexing="ij")
    grid = np.stack([(t % TI) * ROWS + p // W - 1 + k // 3, p % W - 1 + k % 3,
                     (t // TI) * H * W + FRONT], 1).astype(np.float32)
    return {
        "x": f(ar["x"].reshape(NIMG, C, H * W).transpose(0, 2, 1).reshape(NTOK, C)),
        "om_w": f(om_w.reshape(C, K9 * NOM)),
        "om_b": f(np.concatenate([ar["L0_conv_off_b"], ar["L0_conv_mask_b"]]).reshape(1, NOM)),
        "grid": f(grid.reshape(P, 3, T * K9)),
        "conv_w": f(ar["L0_conv_proj_w"].reshape(C, C, K9).transpose(2, 1, 0).reshape(CONV_K, C)),
        "conv_b": f(ar["L0_conv_proj_b"].reshape(1, C)),
        "gamma": f(ar["L0_conv_gamma"].reshape(1, C)),
        "beta": f(ar["L0_conv_beta"].reshape(1, C)),
        "router0": f(ar["L0_ffn_router_w"].T),
        "w1_0": f(ar["L0_ffn_w1"]),
        "w2_0": f(ar["L0_ffn_w2"]),
        "qkv": f(ar["L1_conv_qkv_w"].T),
        "temp": f(ar["L1_conv_temp"].reshape(1, HEADS)),
        "out_w": f(ar["L1_conv_out_w"].T),
        "out_b": f(ar["L1_conv_out_b"].reshape(1, C)),
        "headmask": f((np.arange(C)[:, None] // DH == np.arange(HEADS)).astype(np.float32)),
        "router1": f(np.concatenate([ar["L1_ffn_router_w"], ar["L1_ffn_sg_w"]], 1)),
        "sg_b": f(ar["L1_ffn_sg_b"].reshape(1, 1)),
        "wg": f(ar["L1_ffn_w_gate"].transpose(1, 0, 2).reshape(C, HID1R)),
        "wu": f(ar["L1_ffn_w_up"].transpose(1, 0, 2).reshape(C, HID1R)),
        "wd": f(ar["L1_ffn_w_down"].reshape(HID1R, C)),
        "wsg": f(ar["L1_ffn_ws_gate"]),
        "wsu": f(ar["L1_ffn_ws_up"]),
        "wsd": f(ar["L1_ffn_ws_down"]),
    }


def kernel(**inputs):
    import concourse.bacc as bacc
    from concourse.bass_utils import run_bass_kernel_spmd

    nc = bacc.Bacc("TRN2", target_bir_lowering=False, num_devices=1)
    arrays = {f"in_{n}": a for n, a in layouts(inputs).items()}
    io = {n[3:]: nc.dram_tensor(n, a.shape, mybir.dt.from_np(a.dtype), kind="ExternalInput").ap()
          for n, a in arrays.items()}
    out = nc.dram_tensor("out", (NTOK, C), F32, kind="ExternalOutput").ap()
    program(nc, io, out)
    got = run_bass_kernel_spmd(nc, [arrays], core_ids=[0]).results[0]["out"]
    return np.ascontiguousarray(got.reshape(NIMG, H * W, C).transpose(0, 2, 1)).reshape(NIMG, C, H, W)
```

```python
from contextlib import ExitStack

import concourse.bass as bass
from concourse import mybir
import numpy as np

ALU = mybir.AluOpType
ACT = mybir.ActivationFunctionType
AX = mybir.AxisListType
F32 = mybir.dt.float32
F16 = mybir.dt.float16
I32 = mybir.dt.int32

P = 128
NIMG, H, W, C = 8, 32, 32, 192
CA, CB = 128, 64
NTOK = NIMG * H * W
T = NTOK // P
TI = T // NIMG
ROWS = P // W
HP = H + 2
K9 = 9
NOM = 27
FRONT = W + 1
MAXOFF = float(H // 4)
CONV_K = K9 * C
CONV_M = -(-CONV_K // P)
E0, E1 = 16, 8
W0_WIDTHS = [128] * 8 + [256] * 8
HID0 = sum(W0_WIDTHS)
HID1R, HID1S = E1 * 192, 768
HID1 = HID1R + HID1S
CHUNK = 512
TC = CHUNK // P
NCHUNK = NTOK // CHUNK
HEADS, DH = 12, 16
LG = 16


class Count:

    def __init__(self, eng, sem):
        self.eng, self.sem, self.n = eng, sem, 0

    def mark(self, ins):
        ins.then_inc(self.sem, 1)
        self.n = self.n + 1

    def wait(self):
        self.eng.wait_ge(self.sem, self.n)

    def link(self, ins):
        self.mark(ins)
        self.wait()


USED = []


def clear_semaphores(nc):
    nc.clear_and_free_semaphores(USED)
    USED.clear()
    nc.all_engine_barrier()


class Kit:

    def __init__(self, nc, ctx, tag):
        self.nc, self.ctx, self.tag = nc, ctx, tag

    def sb(self, name, shape, dt=F32):
        return self.ctx.enter_context(self.nc.sbuf_tensor(f"{self.tag}_{name}", shape, dt))

    def ps(self, name, shape=(P, 512), dt=F32):
        return self.ctx.enter_context(self.nc.psum_tensor(f"{self.tag}_{name}", list(shape), dt))

    def sem(self, name):
        sem = self.nc.alloc_semaphore(f"{self.tag}_{name}")
        USED.append(sem)
        return sem


def bc(ap, n):
    return ap.unsqueeze(2).to_broadcast([ap.shape[0], ap.shape[1], n])


def at(t, n=1):
    return bass.ds(t, n)


def turn_tile(nc, ps, x, ident):
    nc.tensor.transpose(ps[:, 0:P], x[:, 0:P], ident[:])
    nc.tensor.transpose(ps[:, P:2 * P], x[:, C - P:C], ident[:])
    return nc.tensor.transpose(ps[0:CB, P:2 * P], x[:, CA:C], ident[:])


FINISH = 5


def finish_stats(dve, ch, st, mean, var, tmp, eps):
    me, qe, mo, qo = st[:, :, 1], st[:, :, 2], st[:, :, 4], st[:, :, 5]
    ch.link(dve.tensor_tensor(tmp, me, mo, ALU.subtract))
    dve.tensor_tensor(mean, me, mo, ALU.add)
    ch.link(dve.tensor_tensor(var, qe, qo, ALU.add))
    ch.link(dve.tensor_tensor(tmp, tmp, tmp, ALU.mult))
    dve.tensor_scalar(mean, mean, 0.5, None, ALU.mult)
    ch.link(dve.tensor_scalar(var, var, 1.0 / C, float(eps), ALU.mult, ALU.add))
    ch.link(dve.scalar_tensor_tensor(out=var, in0=tmp, scalar=0.25, in1=var,
                                     op0=ALU.mult, op1=ALU.add))


def stage_offsets(nc, io, X, xn, st, ident, om, bias, grid, table):
    with ExitStack() as ctx:
        k = Kit(nc, ctx, "off")
        mean, rstd, tmp = (k.sb(n, [P, 2, TI]) for n in ("mean", "rstd", "tmp"))
        RING = 4
        pad_hi = k.sb("pad_hi", [P, 2, 3, HP, W], F16)
        pad_lo = k.sb("pad_lo", [P, 2, 3, HP, W], F16)
        pad_b = k.sb("pad_b", [P, 2, 3, HP, W], F16)
        wf = k.sb("wf", [P, 2, K9, NOM])
        w_a = k.sb("w_a", [P, K9, 2, NOM], F16)
        w_b = k.sb("w_b", [P, K9, 2, NOM], F16)
        omlo = k.sb("omlo", [P, 2, TI, NOM])
        zero = k.sb("zero", [FRONT, 4 * C])
        ps_t = [k.ps(f"t{i}") for i in range(RING)]
        ps_c = [k.ps(f"c{i}") for i in range(2)]
        s_img = [k.sem(f"image_loaded{u}") for u in range(2)]
        s_w = k.sem("weights_loaded")
        s_const = k.sem("constants_set")
        s_ch, s_split = k.sem("stats_chain"), k.sem("split_chain")
        s_var, s_sd, s_xd = k.sem("variance_ready"), k.sem("std_ready"), k.sem("tile_normalised")
        s_tab = [k.sem(f"table_written{u}") for u in range(2)]
        s_border, s_next = k.sem("table_border"), k.sem("next_stage_loaded")
        s_tp, s_hi, s_lo = k.sem("transposed"), k.sem("hi_ready"), k.sem("lo_ready")
        s_shift, s_shift_hi = k.sem("shifted"), k.sem("hi_shifted")
        SHIFTS = ((0, slice(1, W), slice(0, W - 1)), (2, slice(0, W - 1), slice(1, W)))
        s_wsplit = k.sem("weights_split")
        s_conv, s_cfree, s_cl = k.sem("conv_done"), k.sem("conv_psum_free"), k.sem("conv_lo_copied")
        block = ctx.enter_context(nc.Block())

        @block.sync
        def _(sp):
            def load(g, u):
                sp.dma_start(X[:, at(g * TI, TI), :], io["x"][at(g * TI * P, TI * P)]
                             .rearrange("(t p) c -> p t c", p=P)).then_inc(s_img[u], 16)

            def store(g, u):
                sp.wait_ge(s_xd, (g + 1) * TI)
                for n in range(4):
                    row = g * TI * P + FRONT - (n // 2) * W - n % 2
                    sp.dma_start(table[at(row, TI * P), n * C:(n + 1) * C].rearrange("(t p) c -> p t c", p=P),
                                 xn[:, u * TI:(u + 1) * TI, :]).then_inc(s_tab[u], 16)

            load(0, 0)
            load(1, 1)
            ow = io["om_w"].rearrange("c (k o) -> c k o", k=K9)
            sp.dma_start(wf[:, 0], ow[0:CA]).then_inc(s_w, 16)
            sp.dma_start(wf[0:CB, 1], ow[CA:C]).then_inc(s_w, 16)
            sp.dma_start(wf[CB:P, 1], ow[CA:C]).then_inc(s_w, 16)
            sp.dma_start(bias[:, 0, :], io["om_b"].to_broadcast([P, NOM])).then_inc(s_next, 16)
            sp.dma_start(grid, io["grid"]).then_inc(s_next, 16)
            sp.wait_ge(s_const, 1)
            sp.dma_start(table[NTOK:NTOK + FRONT], zero[:]).then_inc(s_border, 16)
            sp.dma_start(table[0:FRONT], zero[:]).then_inc(s_border, 16)
            sp.wait_ge(s_border, 32)
            sp.wait_ge(s_img[0], 16)
            load(2, 0)
            with sp.Fori(0, NIMG // 2 - 2) as i:
                for u in range(2):
                    sp.wait_ge(s_img[1 - u], 16 * (i + 1 + u))
                    load(2 * i + u + 3, 1 - u)
                    store(2 * i + u, u)
            sp.wait_ge(s_img[1], 16 * (NIMG // 2 - 1))
            load(NIMG - 1, 1)
            for g in range(NIMG - 4, NIMG):
                store(g, g % 2)
            for tab in s_tab:
                sp.wait_ge(tab, 1 + 4 * 16 * (NIMG // 2))
            sp.wait_ge(s_next, 32)

        @block.gpsimd
        def _(pool):
            nc.gpsimd.memset(zero[:], 0.0).then_inc(s_const, 1)
            for pad in (pad_hi, pad_lo, pad_b):
                last = nc.gpsimd.memset(pad[:], 0.0)
            last.then_inc(s_const, 1)

        @block.vector
        def _(dve):
            ch = Count(dve, s_ch)
            LINKS = FINISH + 2

            def tile_stats(g, j):
                return nc.vector.bn_stats(st[:, at(g * TI + j), :], X[:, at(g * TI + j), :])

            def variance(g, u, last):
                ch = Count(dve, s_ch)
                ch.n = g * LINKS
                ch.link(last)
                finish_stats(nc.vector, ch, st[:, at(g * TI, TI), :], mean[:, u], rstd[:, u], tmp[:, u], 1e-6)
                dve.sem_inc(s_var, 1)

            def reciprocal(g, u):
                dve.wait_ge(s_sd, g + 1)
                nc.vector.reciprocal(rstd[:, u], rstd[:, u]).then_inc(s_ch, 1)
                dve.wait_ge(s_ch, (g + 1) * LINKS)

            def low(t, u, j):
                dve.wait_ge(s_hi, t + 1)
                rows = slice(1 + j * ROWS, 1 + (j + 1) * ROWS)
                a = ps_t[j % RING][:, 0:P].rearrange("p (r x) -> p r x", x=W)
                b = ps_t[j % RING][CB:P, P:2 * P].rearrange("p (r x) -> p r x", x=W)
                nc.vector.tensor_tensor(pad_lo[:, u, 1, rows], a, pad_hi[:, u, 1, rows], ALU.subtract)
                pb = pad_b[CB:P, u, 1, rows]
                nc.vector.tensor_tensor(pb, b, pb, ALU.subtract).then_inc(s_lo, 1)

            def image(g, u, nth, following=True):
                reciprocal(g, u)
                dve.wait_ge(s_tab[u], 1 + 4 * 16 * nth)
                for j in range(TI):
                    t = g * TI + j
                    nc.vector.tensor_scalar(xn[:, u * TI + j, :], X[:, at(t), :], mean[:, u, j:j + 1], rstd[:, u, j:j + 1],
                                            ALU.subtract, ALU.mult).then_inc(s_xd, 1)
                if following:
                    dve.wait_ge(s_img[1 - u], 16 * (nth + 1 + u))
                for j in range(TI):
                    if following:
                        last = tile_stats(g + 1, j)
                    low(g * TI + j, u, j)
                if following:
                    variance(g + 1, 1 - u, last)
                dve.wait_ge(s_lo, RING + (g + 1) * TI)
                for pad in (pad_lo, pad_b):
                    for kx, dst, src in SHIFTS:
                        last = nc.vector.tensor_copy(pad[:, u, kx, 1:1 + H, dst], pad[:, u, 1, 1:1 + H, src])
                last.then_inc(s_shift, 1)

            def gather_conv(g, u):
                dve.wait_ge(s_cl, g + 1)
                src = ps_c[u][:, 0:TI * 2 * NOM].rearrange("p (t s o) -> p t s o", s=2, o=NOM)[:, :, 0, :]
                nc.vector.tensor_tensor(om[:, at(g * TI, TI), :], src, omlo[:, u], ALU.add).then_inc(s_cfree, 1)

            dve.wait_ge(s_img[0], 16)
            for j in range(TI):
                first = tile_stats(0, j)
            variance(0, 0, first)
            ch = Count(dve, s_split)
            dve.wait_ge(s_w, 48)
            nc.vector.tensor_copy(w_a[:, :, 0, :], wf[:, 0])
            nc.vector.tensor_copy(w_b[:, :, 0, :], wf[:, 1])
            ch.link(nc.vector.memset(w_b[CB:P, :, 1, :], 0.0))
            nc.vector.tensor_tensor(w_a[:, :, 1, :], wf[:, 0], w_a[:, :, 0, :], ALU.subtract)
            nc.vector.tensor_tensor(w_b[0:CB, :, 1, :], wf[0:CB, 1], w_b[0:CB, :, 0, :], ALU.subtract).then_inc(s_wsplit, 1)
            image(0, 0, 0)
            with dve.Fori(0, NIMG // 2 - 1) as i:
                image(2 * i + 1, 1, i)
                gather_conv(2 * i, 0)
                image(2 * i + 2, 0, i + 1)
                gather_conv(2 * i + 1, 1)
            image(NIMG - 1, 1, NIMG // 2 - 1, following=False)
            gather_conv(NIMG - 2, 0)
            gather_conv(NIMG - 1, 1)

        @block.scalar
        def _(act):
            def root(g, u):
                act.wait_ge(s_var, g + 1)
                nc.scalar.activation(rstd[:, u], rstd[:, u], ACT.Sqrt).then_inc(s_sd, 1)

            root(0, 0)
            act.wait_ge(s_const, 2)

            def image(g, u, following=True):
                act.wait_ge(s_conv, g + 1)
                for j in range(TI):
                    act.wait_ge(s_tp, g * TI + j + 1)
                    rows = slice(1 + j * ROWS, 1 + (j + 1) * ROWS)
                    a = ps_t[j % RING][:, 0:P].rearrange("p (r x) -> p r x", x=W)
                    b = ps_t[j % RING][:, P:2 * P].rearrange("p (r x) -> p r x", x=W)
                    nc.scalar.activation(pad_hi[:, u, 1, rows], a, ACT.Copy)
                    nc.scalar.activation(pad_b[:, u, 1, rows], b, ACT.Copy).then_inc(s_hi, 1)
                if following:
                    root(g + 1, 1 - u)
                act.wait_ge(s_hi, (g + 1) * TI)
                for kx, dst, src in SHIFTS:
                    last = nc.scalar.activation(pad_hi[:, u, kx, 1:1 + H, dst], pad_hi[:, u, 1, 1:1 + H, src], ACT.Copy)
                last.then_inc(s_shift_hi, 1)

            def conv_low(g, u):
                act.wait_ge(s_conv, 2 + g + 1)
                act.wait_ge(s_cfree, g + 1)
                src = ps_c[u][:, 0:TI * 2 * NOM].rearrange("p (t s o) -> p t s o", s=2, o=NOM)[:, :, 1, :]
                nc.scalar.activation(omlo[:, u], src, ACT.Copy).then_inc(s_cl, 1)

            image(0, 0)
            with act.Fori(0, NIMG // 2 - 1) as i:
                image(2 * i + 1, 1)
                conv_low(2 * i, 0)
                image(2 * i + 2, 0)
                conv_low(2 * i + 1, 1)
            image(NIMG - 1, 1, following=False)
            conv_low(NIMG - 2, 0)
            conv_low(NIMG - 1, 1)

        @block.tensor
        def _(pe):
            pe.sem_inc(s_lo, RING)
            pe.sem_inc(s_cfree, 2)
            pe.sem_inc(s_conv, 2)
            for tab in s_tab:
                pe.sem_inc(tab, 1)
            pe.wait_ge(s_wsplit, 1)

            def image(g, u):
                for j in range(TI):
                    t = g * TI + j
                    pe.wait_ge(s_xd, t + 1)
                    pe.wait_ge(s_lo, t + 1)
                    turn_tile(nc, ps_t[j % RING], xn[:, u * TI + j, :], ident).then_inc(s_tp, 1)

            def conv(g, u):
                pe.wait_ge(s_shift_hi, g + 1)
                pe.wait_ge(s_shift, g + 1)
                pe.wait_ge(s_cfree, g + 1)
                for j in range(TI):
                    o = j * 2 * NOM
                    for tap in range(K9):
                        ky, kx = tap // 3, tap % 3
                        first = j == 0 and tap == 0
                        for n, (pad, wt, cols) in enumerate(((pad_hi, w_a, 2), (pad_b, w_b, 2), (pad_lo, w_a, 1))):
                            last = nc.tensor.matmul(ps_c[u][:, o:o + cols * NOM], pad[:, u, kx].rearrange("p y x -> p (y x)")
                                                    [:, (j * ROWS + ky) * W:(j * ROWS + ky) * W + P],
                                                    wt[:, tap, 0:cols, :], start=(first and n == 0),
                                                    stop=(tap == K9 - 1 and n == 2), skip_group_check=True)
                last.then_inc(s_conv, 1)

            image(0, 0)
            with pe.Fori(0, NIMG // 2 - 1) as i:
                image(2 * i + 1, 1)
                conv(2 * i, 0)
                image(2 * i + 2, 0)
                conv(2 * i + 1, 1)
            image(NIMG - 1, 1)
            conv(NIMG - 2, 0)
            conv(NIMG - 1, 1)


class Corners:
    FIRST = 4
    PARTS = ((0, FIRST), (FIRST, T))
    NAMES = ("by", "bx", "t", "y0", "y1", "x0", "x1", "m")
    SCRATCH = (len(NAMES) + 1) * T * K9

    def __init__(self, k, om, bias, grid, scratch, wts, idx):
        self.nc, self.om, self.bias, self.grid, self.wts, self.idx = k.nc, om, bias, grid, wts, idx
        N = T * K9
        self.flat = {n: scratch[:, i * N:(i + 1) * N] for i, n in enumerate(self.NAMES)}
        self.fl = scratch[:, len(self.NAMES) * N:].bitcast(I32)
        self.s_ch, self.s_z = k.sem("corners_chain"), k.sem("mask_logits")
        self.s_m, self.s_ready = k.sem("mask_ready"), k.sem("corners_ready")

    def masks(self, act, part):
        t0, t1 = self.PARTS[part]
        m = self.flat["m"][:, t0 * K9:t1 * K9]
        act.wait_ge(self.s_z, part + 1)
        self.nc.scalar.activation(m, m, ACT.Sigmoid).then_inc(self.s_m, 1)

    def rows_and_weights(self, dve, ch, part):
        v = self.nc.vector
        t0, t1 = self.PARTS[part]
        cols = slice(t0 * K9, t1 * K9)
        f = {n: a[:, cols] for n, a in self.flat.items()}
        fl, om, grid = self.fl[:, cols], self.om[:, t0:t1, :], self.grid[:, :, cols]
        tk = lambda ap: ap.rearrange("p (t k) -> p t k", k=K9)
        ch.link(v.tensor_tensor(om, om, self.bias[:].to_broadcast([P, t1 - t0, NOM]), ALU.add))
        ch.link(v.tensor_copy(tk(f["m"]), om[:, :, 2 * K9:NOM]))
        dve.sem_inc(self.s_z, 1)
        t = f["t"]
        for d in range(2):
            w0, w1, b = ((f["y0"], f["y1"], f["by"]), (f["x0"], f["x1"], f["bx"]))[d]
            ch.link(v.tensor_scalar(tk(w0), om[:, :, d:2 * K9:2], -MAXOFF, MAXOFF, ALU.max, ALU.min))
            ch.link(v.tensor_tensor(w0, w0, grid[:, d], ALU.add))
            ch.link(v.tensor_copy(fl, w0))
            ch.link(v.tensor_copy(b, fl))
            ch.link(v.tensor_tensor(t, b, w0, ALU.is_gt))
            ch.link(v.tensor_tensor(b, b, t, ALU.subtract))
            ch.link(v.tensor_scalar(b, b, 0.0, float(H - 1), ALU.max, ALU.min))
            ch.link(v.tensor_tensor(t, w0, b, ALU.subtract))
            ch.link(v.tensor_scalar(w0, t, -1.0, 1.0, ALU.mult, ALU.add))
            ch.link(v.scalar_tensor_tensor(out=w1, in0=w0, scalar=1.0, in1=t, op0=ALU.add, op1=ALU.min))
            ch.link(v.scalar_tensor_tensor(out=w0, in0=t, scalar=1.0, in1=w0, op0=ALU.add, op1=ALU.min))
            ch.link(v.tensor_scalar(w0, w0, 0.0, None, ALU.max))
            ch.link(v.tensor_scalar(t, b, float(H - 1), None, ALU.is_lt))
            ch.link(v.scalar_tensor_tensor(out=w1, in0=w1, scalar=0.0, in1=t, op0=ALU.max, op1=ALU.mult))
        ch.link(v.scalar_tensor_tensor(out=t, in0=f["by"], scalar=float(W), in1=f["bx"], op0=ALU.mult, op1=ALU.add))
        ch.link(v.tensor_tensor(t, t, grid[:, 2], ALU.add))
        ch.link(v.tensor_copy(self.idx[:, t0:t1, :], tk(t)))
        dve.sem_inc(self.s_ready, 1)
        dve.wait_ge(self.s_m, part + 1)
        for y in ("y0", "y1"):
            ch.link(v.scalar_tensor_tensor(out=f[y], in0=f["m"], scalar=2.0, in1=f[y], op0=ALU.mult, op1=ALU.mult))
        for n, (y, x) in enumerate((("y0", "x0"), ("y0", "x1"), ("y1", "x0"), ("y1", "x1"))):
            last = v.tensor_tensor(self.wts[:, t0:t1, :, n], tk(f[y]), tk(f[x]), ALU.mult)
        ch.link(last)


def stage_deform(nc, io, om, bias, grid, scratch, table, Y, ones, ident, sums):
    with ExitStack() as ctx:
        k = Kit(nc, ctx, "dfm")
        gath = k.sb("gath", [P, 2, K9, 4 * C])
        samp = k.sb("samp", [P, 2, CONV_K])
        sampT = k.sb("sampT", [P, 2, CONV_M * P])
        wconv = k.sb("wconv", [P, CONV_M, C])
        wts, idx = k.sb("wts", [P, T, K9, 4]), k.sb("idx", [P, T, K9], I32)
        corners = Corners(k, om, bias, grid, scratch, wts, idx)
        wt = k.sb("wt", [P, 2, K9, 4])
        IXR = 4
        ix = k.sb("ix", [P, IXR, K9], I32)
        GROUP, PER = 3, 3 * K9
        ysq = k.sb("ysq", [P, 2, 2, C])
        ps_t = [k.ps(f"t{i}") for i in range(4)]
        ps_y = [k.ps(f"y{i}") for i in range(2)]
        ps_s = k.ps("s")
        s_w = k.sem("weights_loaded")
        s_g = [[k.sem(f"gathered{u}_{n}") for n in range(K9)] for u in range(2)]
        s_ix, s_first = k.sem("tile_indices"), k.sem("first_corner")
        s_acc, s_sfree = k.sem("dve_accumulate"), k.sem("samples_free")
        s_wt, s_free = k.sem("tile_weights"), k.sem("gather_slots_free")
        s_turn, s_evac = k.sem("turned"), k.sem("turned_copied")
        s_conv, s_y, s_sum = k.sem("conv_done"), k.sem("y_ready"), k.sem("y_summed")
        s_zero, s_sums = k.sem("sum_zeroed"), k.sem("sums")
        block = ctx.enter_context(nc.Block())
        BANKS = 4
        blocks = [list(range(4 * q, min(4 * q + 4, CONV_M))) for q in range(BANKS)]
        rows = lambda m: min(P, CONV_K - m * P)

        @block.sync
        def _(sp):
            full = (CONV_M - 1) * P
            sp.dma_start(wconv[:, 0:CONV_M - 1, :], io["conv_w"][0:full].rearrange("(m p) c -> p m c", p=P)).then_inc(s_w, 16)
            sp.dma_start(wconv[0:CONV_K - full, CONV_M - 1, :], io["conv_w"][full:CONV_K]).then_inc(s_w, 16)

        @block.gpsimd
        def _(pool):
            def indices(t, r):
                nc.gpsimd.tensor_copy(ix[:, r, :], idx[:, at(t), :]).then_inc(s_ix, 1)

            def gather(t, r, first=False):
                u = r % 2
                pool.wait_ge(s_ix, t + 1)
                for n in range(K9):
                    if n % GROUP == 0:
                        if not first:
                            pool.wait_ge(s_acc, (t - 2) * PER + GROUP * (n + GROUP))
                        pool.sem_inc(s_free, 1)
                    nc.gpsimd.indirect_dma_start(
                        out=gath[:, u, n, :], out_offset=None, in_=table,
                        in_offset=bass.IndirectOffsetOnAxis(ap=ix[:, r, n:n + 1], axis=0)).then_inc(s_g[u][n], 16)
                    if n == GROUP:
                        indices((t + 1) % T, (r + 1) % IXR)

            pool.wait_ge(corners.s_ready, 1)
            indices(0, 0)
            for t in range(IXR):
                if t + 1 == Corners.FIRST:
                    pool.wait_ge(corners.s_ready, 2)
                gather(t, t, t < 2)
            with pool.Fori(1, T // IXR) as i:
                for r in range(IXR):
                    gather(IXR * i + r, r)

        @block.vector
        def _(dve):
            nc.vector.memset(ysq[:, 0], 0.0).then_inc(s_zero, 1)
            ch = Count(dve, corners.s_ch)
            for part in range(2):
                corners.rows_and_weights(dve, ch, part)
            nc.vector.tensor_copy(wt[:, 0], wts[:, 0]).then_inc(s_wt, 1)

            with dve.Fori(0, T // 2) as i:
                for u in range(2):
                    t = 2 * i + u
                    n_acc = t * PER
                    for g0 in range(0, K9, 3):
                        dve.wait_ge(s_first, t * K9 + g0 + 3)
                        if g0 == 0:
                            dve.wait_ge(s_wt, t + 1)
                        for c in range(1, 4):
                            if c > 1:
                                dve.wait_ge(s_acc, n_acc)
                            for n in range(g0, g0 + 3):
                                s = samp[:, u, n * C:(n + 1) * C]
                                last = nc.vector.scalar_tensor_tensor(
                                    out=s, in0=gath[:, u, n, c * C:(c + 1) * C], scalar=wt[:, u, n, c:c + 1], in1=s,
                                    op0=ALU.mult, op1=ALU.add)
                                last.then_inc(s_acc, 1)
                                n_acc = n_acc + 1
                        if g0 == 0:
                            nc.vector.tensor_copy(wt[:, 1 - u], wts[:, at((t + 1) % T)]).then_inc(s_wt, 1)

        @block.scalar
        def _(act):
            act.sem_inc(s_sfree, 2)
            for part in range(2):
                corners.masks(act, part)

            def first_corners(t, u, q, group):
                act.wait_ge(s_sfree, t + 1)
                act.wait_ge(s_wt, t + 1)
                for n in range(group * GROUP, (group + 1) * GROUP):
                    act.wait_ge(s_g[u][n], 16 * (q + 1))
                    nc.scalar.activation(samp[:, u, n * C:(n + 1) * C], gath[:, u, n, 0:C], ACT.Copy,
                                         scale=wt[:, u, n, 0:1]).then_inc(s_first, 1)

            def copy_turned(t, u, banks):
                for q in banks:
                    act.wait_ge(s_turn, t * BANKS + q + 1)
                    full = [m for m in blocks[q] if rows(m) == P]
                    w = len(full) * P
                    last = nc.scalar.activation(sampT[:, u, 4 * q * P:4 * q * P + w], ps_t[q][:, 0:w], ACT.Copy)
                    for m in blocks[q]:
                        if rows(m) < P:
                            last = nc.scalar.activation(sampT[0:rows(m), u, m * P:(m + 1) * P],
                                                        ps_t[q][0:rows(m), w:w + P], ACT.Copy)
                    last.then_inc(s_evac, 1)

            def keep_y(t, u):
                act.wait_ge(s_conv, t + 1)
                act.wait_ge(s_sum, t + 1)
                nc.scalar.activation(ysq[:, u, 0], ps_y[u][:, 0:C], ACT.Copy)
                nc.scalar.activation(ysq[:, u, 1], ps_y[u][:, 0:C], ACT.Square)
                nc.scalar.activation(Y[:, at(t), :], ps_y[u][:, 0:C], ACT.Copy).then_inc(s_y, 1)

            def tile(t, u, q, before=True, keep=True, following=True):
                first_corners(t, u, q, 1)
                if before:
                    copy_turned(t - 1, 1 - u, (2, 3))
                if keep:
                    keep_y(t - 3, 1 - u)
                first_corners(t, u, q, 2)
                copy_turned(t, u, (0,))
                if following:
                    first_corners(t + 1, 1 - u, q + u, 0)
                copy_turned(t, u, (1,))

            first_corners(0, 0, 0, 0)
            for t in range(4):
                tile(t, t % 2, t // 2, t > 0, t > 2)
            with act.Fori(2, T // 2 - 1) as i:
                for u in range(2):
                    tile(2 * i + u, u, i)
            for t in (T - 2, T - 1):
                tile(t, t % 2, t // 2, following=t + 1 < T)
            copy_turned(T - 1, 1, (2, 3))
            keep_y(T - 3, 1)
            keep_y(T - 2, 0)
            keep_y(T - 1, 1)
            act.wait_ge(s_sums, 1)
            nc.scalar.activation(sums[:], ps_s[:, 0:2 * C], ACT.Copy)

        @block.tensor
        def _(pe):
            pe.wait_ge(s_zero, 1)
            nc.tensor.matmul(ps_s[:, 0:2 * C], ones[:], ysq[:, 0].rearrange("p a c -> p (a c)"), start=True, stop=False,
                             skip_group_check=True).then_inc(s_sum, 1)
            pe.sem_inc(s_sum, 1)
            pe.sem_inc(s_evac, BANKS)
            pe.wait_ge(s_w, 32)

            def turn(t, u, banks):
                for q in banks:
                    groups = min(-(-(4 * (q + 1) * P) // (GROUP * C)), K9 // GROUP)
                    pe.wait_ge(s_acc, t * PER + groups * GROUP * GROUP)
                    pe.wait_ge(s_evac, t * BANKS + q + 1)
                    for j, m in enumerate(blocks[q]):
                        last = nc.tensor.transpose(ps_t[q][0:rows(m), j * P:(j + 1) * P],
                                                   samp[:, u, m * P:m * P + rows(m)], ident[:])
                    last.then_inc(s_turn, 1)
                if BANKS - 1 in banks:
                    pe.wait_ge(s_turn, (t + 1) * BANKS)
                    pe.sem_inc(s_sfree, 1)

            def conv(t, u):
                pe.wait_ge(s_evac, BANKS + (t + 1) * BANKS)
                pe.wait_ge(s_y, t + 1)
                for m in range(CONV_M):
                    last = nc.tensor.matmul(ps_y[u][:, 0:C], sampT[0:rows(m), u, m * P:(m + 1) * P],
                                            wconv[0:rows(m), m, :], start=(m == 0), stop=(m == CONV_M - 1))
                last.then_inc(s_conv, 1)

            def add_sums(t, u):
                pe.wait_ge(s_y, 2 + t + 1)
                return nc.tensor.matmul(ps_s[:, 0:2 * C], ones[:], ysq[:, u].rearrange("p a c -> p (a c)"),
                                        start=False, stop=False, skip_group_check=True).then_inc(s_sum, 1)

            pe.sem_inc(s_y, 2)
            def tile(t, u, before=True, keep=True):
                turn(t, u, (0,))
                if before:
                    conv(t - 1, 1 - u)
                if keep:
                    add_sums(t - 3, 1 - u)
                turn(t, u, (1, 2, 3))

            for t in range(4):
                tile(t, t % 2, t > 0, t > 2)
            with pe.Fori(2, T // 2) as i:
                for u in range(2):
                    tile(2 * i + u, u)
            add_sums(T - 3, 1)
            conv(T - 1, 1)
            add_sums(T - 2, 0)
            add_sums(T - 1, 1)
            pe.wait_ge(s_sum, 2 + T)
            pe.sem_inc(s_sums, 1)


def stage_batchnorm(nc, io, X, Y, sums, st):
    with ExitStack() as ctx:
        k = Kit(nc, ctx, "bn")
        par = k.sb("par", [P, 3, C])
        mean, var, scale, shift = (k.sb(n, [P, 1, C]) for n in ("mean", "var", "scale", "shift"))
        s_in, s_ch, s_var, s_sd = k.sem("loaded"), k.sem("dve_chain"), k.sem("variance_ready"), k.sem("std_ready")
        s_mul, s_z, s_gelu, s_add = k.sem("scaled"), k.sem("normalised"), k.sem("gelu_done"), k.sem("added")
        s_aff = k.sem("scale_shift_ready")
        block = ctx.enter_context(nc.Block())
        GRP = 8

        @block.sync
        def _(sp):
            for n, name in enumerate(("gamma", "beta", "conv_b")):
                sp.dma_start(par[:, n, :], io[name].to_broadcast([P, C])).then_inc(s_in, 16)

        @block.vector
        def _(dve):
            v, ch = nc.vector, Count(dve, s_ch)
            m, q, sc, sh = mean[:, 0], var[:, 0], scale[:, 0], shift[:, 0]
            dve.wait_ge(s_in, 48)
            ch.link(v.tensor_scalar(m, sums[:, 0:C], 1.0 / NTOK, None, ALU.mult))
            ch.link(v.tensor_scalar(q, sums[:, C:2 * C], 1.0 / NTOK, None, ALU.mult))
            ch.link(v.tensor_tensor(sc, m, m, ALU.mult))
            ch.link(v.tensor_tensor(q, q, sc, ALU.subtract))
            ch.link(v.tensor_scalar(q, q, 0.0, 1e-5, ALU.max, ALU.add))
            dve.sem_inc(s_var, 1)
            ch.link(v.tensor_tensor(sh, m, par[:, 2], ALU.add))
            ch.link(v.tensor_tensor(sh, par[:, 2], sh, ALU.subtract))
            dve.wait_ge(s_sd, 1)
            ch.link(v.reciprocal(q, q))
            ch.link(v.tensor_tensor(sc, q, par[:, 0], ALU.mult))
            ch.link(v.tensor_tensor(sh, sh, sc, ALU.mult))
            ch.link(v.tensor_tensor(sh, sh, par[:, 1], ALU.add))

            dve.sem_inc(s_aff, 1)

            def scaled(g):
                y = Y[:, at(g * GRP, GRP), :]
                v.tensor_tensor(y, y, scale[:].to_broadcast([P, GRP, C]), ALU.mult).then_inc(s_mul, 1)

            def add_back(g):
                dve.wait_ge(s_gelu, g + 1)
                x = X[:, at(g * GRP, GRP), :]
                v.tensor_tensor(x, x, Y[:, at(g * GRP, GRP), :], ALU.add).then_inc(s_add, 1)

            def stats(g):
                dve.wait_ge(s_add, g + 1)
                for j in range(GRP):
                    v.bn_stats(st[:, at(g * GRP + j), :], X[:, at(g * GRP + j), :])

            G = T // GRP
            scaled(0)
            scaled(1)
            with dve.Fori(2, G) as g:
                scaled(g)
                add_back(g - 2)
                stats(g - 2)
            for g in (G - 2, G - 1):
                add_back(g)
                stats(g)

        @block.gpsimd
        def _(pool):
            pool.wait_ge(s_aff, 1)
            with pool.Fori(0, T // GRP) as g:
                pool.wait_ge(s_mul, g + 1)
                y = Y[:, at(g * GRP, GRP), :]
                nc.gpsimd.tensor_tensor(y, y, shift[:].to_broadcast([P, GRP, C]), ALU.add).then_inc(s_z, 1)

        @block.scalar
        def _(act):
            act.wait_ge(s_var, 1)
            nc.scalar.activation(var[:, 0], var[:, 0], ACT.Sqrt).then_inc(s_sd, 1)
            with act.Fori(0, T // GRP) as g:
                act.wait_ge(s_z, g + 1)
                y = Y[:, at(g * GRP, GRP), :]
                nc.scalar.activation(y, y, ACT.Gelu).then_inc(s_gelu, 1)


PIECE = 768


def split_parts(srcs, hi, lo):
    for c in range(0, hi.shape[1], PIECE):
        d = min(c + PIECE, hi.shape[1])
        yield [(src[:, c:d], p0) for src, p0 in srcs], hi[:, c:d], lo[:, c:d]


def split_up(src, wa_h, wa_l, wbb, wbl):
    yield from split_parts([(src[0:CA], 0)], wa_h, wa_l)
    yield from split_parts([(src[CA:C], 0), (src[CA:C], CB)], wbb, wbl)


def split_down(src, hi, lo):
    step = PIECE // C
    for n in range(0, src.shape[0] // P, step):
        m = min(n + step, src.shape[0] // P)
        yield ([(src[n * P:m * P].rearrange("(n p) c -> p n c", p=P), 0)],
               hi[:, n:m].rearrange("p n c -> p (n c)"), lo[:, n:m].rearrange("p n c -> p (n c)"))


class Splitter:
    NB = 2

    def __init__(self, k, parts):
        self.nc, self.parts = k.nc, parts
        self.buf = k.sb("piece", [P, self.NB, PIECE])
        self.s_in = [k.sem(f"piece_loaded{i}") for i in range(self.NB)]
        self.s_hi, self.s_done = k.sem("piece_hi"), k.sem("piece_split")

    def load(self, sp):
        for n, (srcs, hi, lo) in enumerate(self.parts):
            if n >= self.NB:
                sp.wait_ge(self.s_done, n - self.NB + 1)
            for src, p0 in srcs:
                rows = src.shape[0]
                dst = self.buf[p0:p0 + rows, n % self.NB, 0:hi.shape[1]]
                if len(src.shape) == 3:
                    dst = dst.rearrange("p (n c) -> p n c", c=C)
                sp.dma_start(dst, src).then_inc(self.s_in[n % self.NB], 16)

    def split(self, pool):
        v, loads = self.nc.gpsimd, [0] * self.NB
        for n, (srcs, hi, lo) in enumerate(self.parts):
            r = n % self.NB
            loads[r] += len(srcs)
            pool.wait_ge(self.s_in[r], 16 * loads[r])
            w = hi.shape[1]
            v.tensor_copy(hi, self.buf[0:hi.shape[0], r, 0:w]).then_inc(self.s_hi, 1)
            pool.wait_ge(self.s_hi, n + 1)
            rows = lo.shape[0]
            v.tensor_tensor(lo, self.buf[0:rows, r, 0:w], hi[0:rows], ALU.subtract).then_inc(self.s_done, 1)


def stage_route(nc, io, tag, X, st, xh, xl, xb, comb_t, ident, eps, router, nexp, topk, parts, shared_bias=None):
    with ExitStack() as ctx:
        k = Kit(nc, ctx, tag)
        RING = 4
        NR = router.shape[1]
        mean, rstd, tmp = k.sb("mean", [P, T]), k.sb("rstd", [P, T]), k.sb("tmp", [P, T])
        xd = k.sb("xd", [P, RING, C])
        RSCALE = 64.0
        rf = k.sb("rf", [P, 2, NR])
        rs = k.sb("rs", [P, 2, 2, NR], F16)
        prob = k.sb("prob", [P, T, LG])
        rest = k.sb("rest", [P, T, LG])
        top = k.sb("top", [P, T, 8])
        red = k.sb("red", [P, T])
        sgb = k.sb("sgb", [P, 1])
        comb = rest
        combt = k.sb("combt", [LG, NTOK])
        NC = nexp + (shared_bias is not None)
        weights = Splitter(k, parts)
        ps_t = [k.ps(f"t{i}") for i in range(RING)]
        ps_l = k.ps("logits", [P, T * 2 * LG])
        s_w, s_ch = k.sem("router_loaded"), k.sem("dve_chain")
        s_var, s_sd, s_xd = k.sem("variance_ready"), k.sem("std_ready"), k.sem("tile_normalised")
        s_tp, s_hi, s_lo, s_log = k.sem("transposed"), k.sem("hi_ready"), k.sem("lo_ready"), k.sem("logits_ready")
        s_comb, s_ct, s_cc, s_st = k.sem("comb_ready"), k.sem("comb_turned"), k.sem("comb_copied"), k.sem("comb_stored")
        s_rs, s_part = k.sem("router_split"), k.sem("lo_logits_copied")
        s_sub, s_exp, s_sgb = k.sem("logits_shifted"), k.sem("exp_done"), k.sem("bias_loaded")
        block = ctx.enter_context(nc.Block())

        @block.sync
        def _(sp):
            sp.dma_start(rf[:, 0], router[0:CA]).then_inc(s_w, 16)
            sp.dma_start(rf[0:CB, 1], router[CA:C]).then_inc(s_w, 16)
            sp.dma_start(rf[CB:P, 1], router[CA:C]).then_inc(s_w, 16)
            if shared_bias is not None:
                sp.dma_start(sgb[:], shared_bias.to_broadcast([P, 1])).then_inc(s_sgb, 16)
            weights.load(sp)
            sp.wait_ge(s_cc, 1 + T // RING)
            sp.dma_start(comb_t[0:NC], combt[0:NC, :]).then_inc(s_st, 16)
            sp.wait_ge(s_st, 16)

        @block.gpsimd
        def _(pool):
            weights.split(pool)

        @block.vector
        def _(dve):
            v, ch = nc.vector, Count(dve, s_ch)
            finish_stats(v, ch, st, mean[:], rstd[:], tmp[:], eps)
            dve.sem_inc(s_var, 1)
            dve.wait_ge(s_sd, 1)
            ch.link(v.reciprocal(rstd[:], rstd[:]))

            dve.wait_ge(s_w, 48)
            ch.link(v.tensor_scalar(rf[:], rf[:], RSCALE, None, ALU.mult))
            ch.link(v.tensor_copy(rs[:, :, 0], rf[:]))
            ch.link(v.tensor_tensor(rs[:, :, 1], rf[:], rs[:, :, 0], ALU.subtract))
            dve.sem_inc(s_rs, 1)

            def normalise(t, r):
                m, s = mean[:, at(t)], rstd[:, at(t)]
                v.tensor_scalar(xd[:, r, :], X[:, at(t), :], m, s, ALU.subtract, ALU.mult).then_inc(s_xd, 1)

            def low(t, r):
                dve.wait_ge(s_hi, t + 1)
                cols = at(t * P, P)
                v.tensor_tensor(xl[:, cols], ps_t[r][:, 0:P], xh[:, cols], ALU.subtract)
                v.tensor_tensor(xb[CB:P, cols], ps_t[r][CB:P, P:2 * P], xb[CB:P, cols], ALU.subtract).then_inc(s_lo, 1)

            SKEW = 3
            for t in range(RING):
                normalise(t, t)
                if t >= SKEW:
                    low(t - SKEW, t - SKEW)
            with dve.Fori(1, T // RING) as q:
                for r in range(RING):
                    normalise(RING * q + r, r)
                    low(RING * q + r - SKEW, (r - SKEW) % RING)
            for t in range(T - SKEW, T):
                low(t, t % RING)

            lg = ps_l[:].rearrange("p (t c) -> p t c", c=2 * LG)
            dve.wait_ge(s_part, 1)
            ch.link(v.scalar_tensor_tensor(out=prob[:, :, 0:NR], in0=lg[:, :, 0:NR], scalar=1 / RSCALE,
                                           in1=rest[:, :, 0:NR], op0=ALU.mult, op1=ALU.add))
            ch.link(v.tensor_reduce(red[:], prob[:, :, 0:nexp], AX.X, ALU.max))
            ch.link(v.tensor_tensor(prob[:, :, 0:nexp], prob[:, :, 0:nexp], bc(red[:], nexp), ALU.subtract))
            if shared_bias is not None:
                dve.wait_ge(s_sgb, 16)
                ch.link(v.tensor_scalar(prob[:, :, nexp], prob[:, :, nexp], sgb[:, 0:1], -1.0, ALU.add, ALU.mult))
            dve.sem_inc(s_sub, 1)
            dve.wait_ge(s_exp, 1)
            if topk < 8:
                for j in range(8 - topk):
                    last = v.memset(prob[:, :, nexp + 1 + j:nexp + 2 + j], -2.0 - j)
                ch.link(last)
            width = nexp if topk == 8 else nexp + 1 + 8 - topk
            for t in range(T):
                last = v.max(top[:, t, :], prob[:, t, 0:nexp])
            ch.link(last)
            if topk < 8:
                for j in range(8 - topk):
                    last = v.memset(top[:, :, topk + j:topk + j + 1], -2.0 - j)
                ch.link(last)
            for t in range(T):
                last = v.match_replace(rest[:, t, 0:width], top[:, t, :], prob[:, t, 0:width], -1.0)
            ch.link(last)
            ch.link(v.scalar_tensor_tensor(out=comb[:, :, 0:nexp], in0=rest[:, :, 0:nexp], scalar=0.0,
                                           in1=prob[:, :, 0:nexp], op0=ALU.is_lt, op1=ALU.mult))
            ch.link(v.tensor_reduce(red[:], comb[:, :, 0:nexp], AX.X, ALU.add))
            ch.link(v.reciprocal(red[:], red[:]))
            if shared_bias is not None:
                ch.link(v.tensor_scalar(tmp[:], prob[:, :, nexp], 1.0, None, ALU.add))
                ch.link(v.reciprocal(tmp[:], tmp[:]))
                ch.link(v.tensor_copy(comb[:, :, nexp], tmp[:]))
                ch.link(v.tensor_scalar(tmp[:], tmp[:], -1.0, 1.0, ALU.mult, ALU.add))
                ch.link(v.tensor_tensor(red[:], red[:], tmp[:], ALU.mult))
            ch.link(v.tensor_tensor(comb[:, :, 0:nexp], comb[:, :, 0:nexp], bc(red[:], nexp), ALU.mult))
            dve.sem_inc(s_comb, 1)

        @block.scalar
        def _(act):
            act.wait_ge(s_var, 1)
            nc.scalar.activation(rstd[:], rstd[:], ACT.Sqrt).then_inc(s_sd, 1)
            with act.Fori(0, T // RING) as q:
                for r in range(RING):
                    t = RING * q + r
                    cols = at(t * P, P)
                    act.wait_ge(s_tp, t + 1)
                    nc.scalar.activation(xh[:, cols], ps_t[r][:, 0:P], ACT.Copy)
                    nc.scalar.activation(xb[:, cols], ps_t[r][:, P:2 * P], ACT.Copy).then_inc(s_hi, 1)
            act.wait_ge(s_log, T)
            lg = ps_l[:].rearrange("p (t c) -> p t c", c=2 * LG)
            nc.scalar.activation(rest[:, :, 0:NR], lg[:, :, NR:2 * NR], ACT.Copy, scale=1 / RSCALE).then_inc(s_part, 1)
            act.wait_ge(s_sub, 1)
            width = nexp + (shared_bias is not None)
            nc.scalar.activation(prob[:, :, 0:width], prob[:, :, 0:width], ACT.Exp).then_inc(s_exp, 1)
            for q in range(T // RING):
                act.wait_ge(s_ct, q + 1)
                nc.scalar.activation(combt[0:NC, q * RING * P:(q + 1) * RING * P], ps_t[q % RING][0:NC, :],
                                     ACT.Copy).then_inc(s_cc, 1)

        @block.tensor
        def _(pe):
            pe.sem_inc(s_lo, RING)

            def turn(t, r):
                pe.wait_ge(s_xd, t + 1)
                pe.wait_ge(s_lo, t + 1)
                turn_tile(nc, ps_t[r], xd[:, r, :], ident).then_inc(s_tp, 1)

            def logits(t):
                pe.wait_ge(s_lo, RING + t + 1)
                out = ps_l[:, at(t * 2 * LG, 2 * NR)]
                ra, rb = (rs[:, b].rearrange("p s e -> p (s e)") for b in range(2))
                nc.tensor.matmul(out, xh[:, at(t * P, P)], ra, start=True, stop=False)
                nc.tensor.matmul(out, xl[:, at(t * P, P)], ra, start=False, stop=False)
                nc.tensor.matmul(out, xb[:, at(t * P, P)], rb, start=False, stop=True).then_inc(s_log, 1)

            for t in range(RING):
                turn(t, t)
            pe.wait_ge(s_rs, 1)
            with pe.Fori(1, T // RING) as q:
                for r in range(RING):
                    turn(RING * q + r, r)
                    logits(RING * q + r - RING)
            for t in range(T - RING, T):
                logits(t)
            pe.sem_inc(s_cc, 1)
            pe.wait_ge(s_comb, 1)
            for q in range(T // RING):
                if q >= RING:
                    pe.wait_ge(s_cc, 1 + q - RING + 1)
                for j in range(RING):
                    last = nc.tensor.transpose(ps_t[q % RING][0:NC, j * P:(j + 1) * P], comb[:, q * RING + j, 0:NC], ident[:])
                last.then_inc(s_ct, 1)


def stage_ffn(nc, tag, X, xh, xl, xb, comb_t, up, gate, down, loads, func, st=None, out=None):
    with ExitStack() as ctx:
        k = Kit(nc, ctx, tag)
        NH, NL = down[0].shape[1], len(loads)
        SKEW, HB = (2, 3) if gate else (3, 4)
        assert NH % HB == 0 and HB > SKEW
        hf = k.sb("hf", [P, HB, CHUNK])
        hg = k.sb("hg", [P, 2, CHUNK]) if gate else None
        hc = k.sb("hc", [P, 2, CHUNK]) if gate else None
        hh = k.sb("hh", [P, HB, CHUNK], F16)
        hl = k.sb("hl", [P, HB, CHUNK], F16)
        acc = k.sb("acc", [P, TC, C]) if out is not None else None
        coef = k.sb("coef", [P, NL, CHUNK])
        NPS = 2 if gate else 4
        ps_u = [k.ps(f"up{i}") for i in range(NPS)]
        ps_g = [k.ps(f"gate{i}") for i in range(NPS)] if gate else None
        ps_o = [k.ps(f"out{j}") for j in range(TC)]
        CG = 4
        s_coef = [k.sem(f"coefs_loaded{q}") for q in range(-(-NL // CG))]
        s_up, s_gate = k.sem("up_ready"), k.sem("gate_ready")
        s_act, s_mul, s_hf = k.sem("activated"), k.sem("up_scaled"), k.sem("hidden_ready")
        s_hh, s_hl, s_used = k.sem("hi_ready"), k.sem("lo_ready"), k.sem("hidden_used")
        s_acc, s_out = k.sem("accumulated"), k.sem("stored")
        block = ctx.enter_context(nc.Block())
        load_of = {blk: n for n, (_, blks) in enumerate(loads) for blk in blks}
        group_dmas = [sum(len(rows) for rows, _ in loads[q * CG:(q + 1) * CG]) for q in range(len(s_coef))]
        last_block = [loads[min((q + 1) * CG, NL) - 1][1][-1] for q in range(len(s_coef))]

        @block.sync
        def _(sp):
            sp.sem_inc(s_hf, HB)

            def load(i, q):
                tok = i % NCHUNK * CHUNK
                for n in range(q * CG, min((q + 1) * CG, NL)):
                    for e, r0, r1 in loads[n][0]:
                        sp.dma_start(coef[r0:r1, n, :], comb_t[e:e + 1, at(tok, CHUNK)].to_broadcast([r1 - r0, CHUNK]))\
                          .then_inc(s_coef[q], 16)

            for q in range(len(s_coef)):
                load(0, q)
            with sp.Fori(0, NCHUNK) as i:
                for q in range(len(s_coef)):
                    sp.wait_ge(s_hf, HB + i * NH + last_block[q] + 1)
                    load(i + 1, q)
                if out is not None:
                    sp.wait_ge(s_acc, (i + 2) * TC)
                    sp.dma_start(out[at(i * CHUNK, CHUNK)].rearrange("(t p) c -> p t c", p=P), acc[:]).then_inc(s_out, 16)
            if out is not None:
                sp.wait_ge(s_out, 1 + 16 * NCHUNK)
            for q in range(len(s_coef)):
                sp.wait_ge(s_coef[q], 16 * group_dmas[q] * (NCHUNK + 1))

        @block.tensor
        def _(pe):
            pe.sem_inc(s_hl, 1)
            pe.sem_inc(s_acc, TC)
            if out is not None:
                pe.sem_inc(s_out, 1)

            def product(ps, w, n, cols):
                wa_h, wa_l, wbb, wbl = w
                c = slice(n * P, (n + 1) * P)
                nc.tensor.matmul(ps[:], wa_h[:, c], xh[:, cols], start=True, stop=False)
                nc.tensor.matmul(ps[:], wa_h[:, c], xl[:, cols], start=False, stop=False)
                nc.tensor.matmul(ps[:], wa_l[:, c], xh[:, cols], start=False, stop=False)
                nc.tensor.matmul(ps[:], wbb[:, c], xb[:, cols], start=False, stop=False)
                return nc.tensor.matmul(ps[:], wbl[0:CB, c], xb[0:CB, cols], start=False, stop=True)

            def hidden(i, m, prologue=False):
                n = m % NH
                cols = at((i + 1) % NCHUNK * CHUNK if m >= NH else i * CHUNK, CHUNK)
                if not prologue or m >= NPS:
                    pe.wait_ge(s_hf, HB - NPS + i * NH + m + 1)
                if gate:
                    product(ps_g[n % NPS], gate, n, cols).then_inc(s_gate, 1)
                product(ps_u[n % NPS], up, n, cols).then_inc(s_up, 1)

            def expert(i, n):
                pe.wait_ge(s_hl, 1 + i * NH + n + 1)
                s = n % HB
                for j in range(TC):
                    tok = slice(j * P, (j + 1) * P)
                    if n == 0:
                        pe.wait_ge(s_acc, i * TC + j + 1)
                    for m, (a, b) in enumerate(((hh, down[0]), (hh, down[1]), (hl, down[0]))):
                        last = nc.tensor.matmul(ps_o[j][:, 0:C], a[:, s, tok], b[:, n, :],
                                                start=(n == 0 and m == 0), stop=(n == NH - 1 and m == 2))
                last.then_inc(s_used, 1)

            for m in range(SKEW):
                hidden(0, m, True)
            with pe.Fori(0, NCHUNK) as i:
                for n in range(NH):
                    hidden(i, n + SKEW)
                    expert(i, n)

        @block.scalar
        def _(act):
            act.sem_inc(s_used, HB)

            def activate(b, n):
                if gate:
                    act.wait_ge(s_gate, b + 1)
                    act.wait_ge(s_hf, HB - 2 + b + 1)
                    nc.scalar.activation(hg[:, n % 2], ps_g[n % NPS][:], func).then_inc(s_act, 1)
                else:
                    act.wait_ge(s_up, b + 1)
                    act.wait_ge(s_used, b + 1)
                    nc.scalar.activation(hf[:, n % HB], ps_u[n % NPS][:], func).then_inc(s_act, 1)

            def high(b, n):
                act.wait_ge(s_hf, HB + b + 1)
                act.wait_ge(s_used, b + 1)
                nc.scalar.activation(hh[:, n % HB], hf[:, n % HB], ACT.Copy).then_inc(s_hh, 1)

            activate(0, 0)
            with act.Fori(0, NCHUNK) as i:
                for n in range(NH):
                    activate(i * NH + n + 1, (n + 1) % NH)
                    high(i * NH + n, n)
            for m in range(SKEW - 1):
                activate(NCHUNK * NH + m + 1, m + 1)
                high(NCHUNK * NH + m, m)

        @block.vector
        def _(dve):
            v = nc.vector

            def scale(i, m):
                n, b = m % NH, i * NH + m
                q = load_of[n] // CG
                if n == 0 or load_of[n - 1] // CG != q:
                    dve.wait_ge(s_coef[q], 16 * group_dmas[q] * (i + 1 + m // NH))
                c = coef[:, load_of[n], :]
                if gate:
                    dve.wait_ge(s_up, b + 1)
                    v.tensor_tensor(hc[:, n % 2], c, ps_u[n % NPS][:], ALU.mult).then_inc(s_mul, 1)
                    dve.wait_ge(s_act, b + 1)
                    dve.wait_ge(s_mul, b + 1)
                    dve.wait_ge(s_used, b + 1)
                    v.tensor_tensor(hf[:, n % HB], hg[:, n % 2], hc[:, n % 2], ALU.mult).then_inc(s_hf, 1)
                else:
                    dve.wait_ge(s_act, b + 1)
                    v.tensor_tensor(hf[:, n % HB], hf[:, n % HB], c, ALU.mult).then_inc(s_hf, 1)

            def low(b, n):
                dve.wait_ge(s_hh, b + 1)
                v.tensor_tensor(hl[:, n % HB], hf[:, n % HB], hh[:, n % HB], ALU.subtract).then_inc(s_hl, 1)

            scale(0, 0)
            for m in range(1, SKEW):
                scale(0, m)
                low(m - 1, m - 1)
            with dve.Fori(0, NCHUNK) as i:
                for n in range(NH):
                    m = n + SKEW
                    scale(i, m)
                    low(i * NH + m - 1, (m - 1) % NH)
                dve.wait_ge(s_used, HB + (i + 1) * NH)
                for j in range(TC):
                    x = X[:, at(i * TC + j), :]
                    if out is not None and j == 0:
                        dve.wait_ge(s_out, 1 + 16 * i)
                    v.tensor_tensor(x if out is None else acc[:, j, :].unsqueeze(1), ps_o[j][:, 0:C].unsqueeze(1), x,
                                    ALU.add).then_inc(s_acc, 1)
                if st is not None:
                    dve.wait_ge(s_acc, TC + (i + 1) * TC)
                    for j in range(TC):
                        v.bn_stats(st[:, at(i * TC + j), :], X[:, at(i * TC + j), :])
            dve.wait_ge(s_hl, 1 + NCHUNK * NH + SKEW - 1)


def stage_attention(nc, io, X, st, ident):
    with ExitStack() as ctx:
        k = Kit(nc, ctx, "att")
        RING, HALF = 4, CHUNK
        N = H * W
        HT = TI * HEADS
        mean, rstd, tmp = k.sb("mean", [P, T]), k.sb("rstd", [P, T]), k.sb("tmp", [P, T])
        xd = k.sb("xd", [P, TI, C])
        xt = k.sb("xt", [P, 2, N])
        w = k.sb("w", [P, 2, 2, N])
        w2 = k.sb("w2", [P, 2, 2, N])
        val = k.sb("val", [P, 2, N])
        scr = k.sb("scr", [P, 2, HALF])
        pib = k.sb("pi_channels", [P, 2, 2, HALF])
        wq, wo, wos = k.sb("wq", [P, 2, C]), k.sb("wo", [P, 2, C]), k.sb("wos", [P, 2, C])
        hm, rm = k.sb("headmask", [P, 2, HEADS]), k.sb("rm", [P, 2, HEADS])
        temp = k.sb("temp", [P, 1, HEADS])
        ssq = k.sb("ssq", [P, 2, 2, 2])
        rn = k.sb("rn", [P, 2])
        z, pi = k.sb("z", [P, TI, HEADS]), k.sb("pi", [P, TI, HEADS])
        red = k.sb("red", [P, TI])
        pe_ = k.sb("pi_spread", [P, TI, C])
        dot, psum_pi, att = k.sb("dot", [P, 2, 2]), k.sb("sum_pi", [P, 2, 2]), k.sb("attn", [P, 2, 2])
        ps_t = [k.ps("ta"), k.ps("tb")]
        ps_q = [[k.ps(f"q{h}{b}") for b in "ab"] for h in range(2)]
        ps_s, ps_o = k.ps("s"), k.ps("o")
        out_pair = (ps_o[:, 0:2 * C], ps_s[:, P:P + 2 * C])
        ROWSB = (P, CB)
        c0 = (0, CA)
        s_in, s_ch0, s_ch = k.sem("loaded"), k.sem("setup_chain"), k.sem("dve_chain")
        s_var, s_sd, s_xd = k.sem("variance_ready"), k.sem("std_ready"), k.sem("tile_normalised")
        s_turn, s_xt, s_q, s_w = k.sem("half_turned"), k.sem("half_copied"), k.sem("qkv_half"), k.sem("w_half_kept")
        s_r, s_s, s_sub, s_exp = k.sem("norms_ready"), k.sem("head_sums"), k.sem("logits_shifted"), k.sem("exp_done")
        s_pe, s_p, s_vh, s_sum = k.sem("pi_spread"), k.sem("pi_turned"), k.sem("values_half"), k.sem("pi_summed")
        s_fold, s_o, s_add = k.sem("weights_scaled"), k.sem("out_pair"), k.sem("pair_added")
        block = ctx.enter_context(nc.Block())

        def images(eng, step):
            step(0, 0, now=True)
            step(1, 1, now=True, before=True)
            with eng.Fori(1, NIMG // 2) as i:
                step(2 * i, 0, now=True, before=True, last=True)
                step(2 * i + 1, 1, now=True, before=True, last=True)
            step(NIMG, 0, before=True, last=True)
            step(NIMG + 1, 1, last=True)

        @block.sync
        def _(sp):
            for name, dst in (("qkv", wq), ("out_w", wo), ("headmask", hm)):
                for b in range(2):
                    sp.dma_start(dst[0:ROWSB[b], b, :], io[name][c0[b]:c0[b] + ROWSB[b]]).then_inc(s_in, 16)
            sp.dma_start(temp[:, 0, :], io["temp"].to_broadcast([P, HEADS])).then_inc(s_in, 16)
            sp.dma_start(wos[CB:CB + 1, 1, :], io["out_b"]).then_inc(s_in, 16)

        @block.vector
        def _(dve):
            v, c = nc.vector, Count(dve, s_ch0)
            finish_stats(v, c, st, mean[:], rstd[:], tmp[:], 1e-6)
            dve.sem_inc(s_var, 1)
            dve.wait_ge(s_sd, 1)
            c.link(v.reciprocal(rstd[:], rstd[:]))
            HEAD, SOFT, LINKS = 4, 6, 17

            def norm(g):
                for j in range(TI):
                    if not isinstance(g, int) or g > 0:
                        dve.wait_ge(s_turn, 2 * g + j // RING)
                    t = (g % NIMG) * TI + j
                    v.tensor_scalar(xd[:, j], X[:, at(t), :], mean[:, at(t)], rstd[:, at(t)],
                                    ALU.subtract, ALU.mult).then_inc(s_xd, 1)

            def head(g, u, ch):
                dve.wait_ge(s_w, 1 + 2 * g + 2)
                dve.wait_ge(s_s, 1 + g)
                ch.link(v.tensor_tensor(rn[:], ssq[:, u, :, 0], ssq[:, u, :, 1], ALU.add))
                ch.link(v.tensor_scalar(rn[:], rn[:], 1e-24, None, ALU.max))
                ch.link(v.reciprocal(rn[:], rn[:]))
                ch.link(v.tensor_tensor(rm[:], hm[:], bc(rn[:], HEADS), ALU.mult))
                dve.sem_inc(s_r, 1)

            def softmax(g, ch):
                dve.wait_ge(s_s, 1 + g + 1)
                lg = ps_s[:, 0:HT].rearrange("p (t h) -> p t h", h=HEADS)
                ch.link(v.tensor_tensor(z[:], lg, temp[:].to_broadcast([P, TI, HEADS]), ALU.mult))
                ch.link(v.tensor_reduce(red[:], z[:], AX.X, ALU.max))
                ch.link(v.tensor_tensor(z[:], z[:], bc(red[:], HEADS), ALU.subtract))
                dve.sem_inc(s_sub, 1)
                dve.wait_ge(s_exp, g + 1)
                ch.link(v.tensor_reduce(red[:], z[:], AX.X, ALU.add))
                ch.link(v.reciprocal(red[:], red[:]))
                ch.link(v.tensor_tensor(pi[:], z[:], bc(red[:], HEADS), ALU.mult))
                dve.wait_ge(s_p, 1 + 2 * g)
                v.tensor_copy(pe_[:].rearrange("p t (h d) -> p (t h) d", d=DH),
                              bc(pi[:].rearrange("p t h -> p (t h)"), DH)).then_inc(s_pe, 1)

            def values(g, u, ch):
                dve.wait_ge(s_o, 1 + 4 * g)
                for h in range(2):
                    dve.wait_ge(s_sum, 1 + 2 * g + h + 1)
                    cols = slice(h * HALF, (h + 1) * HALF)
                    for b in range(2):
                        r = slice(0, ROWSB[b])
                        v.tensor_tensor(val[r, b, cols], w[r, u, b, cols], pib[r, h, b], ALU.mult)
                        last = v.scalar_tensor_tensor(out=scr[r, b], in0=w2[r, u, b, cols], scalar=1.0, in1=pib[r, h, b],
                                                      op0=ALU.mult, op1=ALU.mult, accum_out=dot[r, b, h:h + 1])
                    last.then_inc(s_vh, 1)
                    dve.wait_ge(s_vh, 2 * g + h + 1)
                a, s = att[:, :, 0], att[:, :, 1]
                ch.link(v.tensor_tensor(a, dot[:, :, 0], dot[:, :, 1], ALU.add))
                ch.link(v.scalar_tensor_tensor(out=s, in0=psum_pi[:, :, 0], scalar=1e-8, in1=psum_pi[:, :, 1],
                                               op0=ALU.add, op1=ALU.add))
                ch.link(v.reciprocal(s, s))
                ch.link(v.tensor_tensor(a, a, s, ALU.mult))
                ch.link(v.tensor_scalar(a, a, 1.0, None, ALU.add))
                ch.link(v.reciprocal(a, a))
                for b in range(2):
                    r = slice(0, ROWSB[b])
                    last = v.tensor_scalar(wos[r, b], wo[r, b], att[r, b, 0:1], -1.0, ALU.mult, ALU.mult)
                ch.link(last)
                dve.sem_inc(s_fold, 1)

            def add(g):
                for r in range(TI // 2):
                    dve.wait_ge(s_o, 1 + 4 * g + r + 1)
                    x = X[:, at(g * TI + 2 * r, 2), :]
                    v.tensor_tensor(x, out_pair[r % 2].rearrange("p (t c) -> p t c", c=C), x, ALU.add).then_inc(s_add, 1)

            norm(0)
            for t_ in (dot[:], psum_pi[:], ssq[:], hm[CB:P, 1]):
                last = v.memset(t_, 0.0)
            c.link(v.memset(val[CB:CB + 1, 1], 1.0))
            dve.sem_inc(s_sum, 1)

            def stats(g):
                dve.wait_ge(s_add, 2 + 4 * g + 4)
                for j in range(TI):
                    t = (g + NIMG) % NIMG * TI + j
                    v.bn_stats(st[:, at(t), :], X[:, at(t), :])

            def step(g, u, now=False, before=False, last=False):
                ch = Count(dve, s_ch)
                ch.n = HEAD + SOFT + (g - 2) * LINKS if last else 0
                if before:
                    head(g - 1, 1 - u, ch)
                if last:
                    stats(g - 3)
                    values(g - 2, u, ch)
                if before:
                    softmax(g - 1, ch)
                if now:
                    norm(g + 1)
                if last:
                    add(g - 2)

            dve.wait_ge(s_in, 128)
            images(dve, step)
            stats(NIMG - 1)

        @block.scalar
        def _(act):
            act.wait_ge(s_var, 1)
            nc.scalar.activation(rstd[:], rstd[:], ACT.Sqrt).then_inc(s_sd, 1)
            act.wait_ge(s_sum, 1)

            def copy_turned(g):
                for h in range(2):
                    act.wait_ge(s_turn, 1 + 2 * g + h + 1)
                    act.wait_ge(s_q, 1 + 2 * g)
                    for b in range(2):
                        r = slice(0, ROWSB[b])
                        last = nc.scalar.activation(xt[r, b, h * HALF:(h + 1) * HALF], ps_t[b][r, :], ACT.Copy)
                    last.then_inc(s_xt, 1)

            def keep_w(g, u):
                act.wait_ge(s_fold, g + 1)
                for h in range(2):
                    act.wait_ge(s_q, 1 + 2 * g + h + 1)
                    cols = slice(h * HALF, (h + 1) * HALF)
                    for b in range(2):
                        r = slice(0, ROWSB[b])
                        nc.scalar.activation(w[r, u, b, cols], ps_q[h][b][r, :], ACT.Copy)
                        last = nc.scalar.activation(w2[r, u, b, cols], ps_q[h][b][r, :], ACT.Square,
                                                    accum_out=ssq[r, u, b, h:h + 1])
                    last.then_inc(s_w, 1)

            def exp(g):
                act.wait_ge(s_sub, 1 + g + 1)
                nc.scalar.activation(z[:], z[:], ACT.Exp).then_inc(s_exp, 1)

            def sum_pi(g):
                for h in range(2):
                    act.wait_ge(s_p, 1 + 2 * g + h + 1)
                    act.wait_ge(s_fold, 2 + g)
                    act.wait_ge(s_sum, 1 + 2 * g + h)
                    for b in range(2):
                        r = slice(0, ROWSB[b])
                        last = nc.scalar.activation(pib[r, h, b], ps_q[h][b][r, :], ACT.Copy,
                                                    accum_out=psum_pi[r, b, h:h + 1])
                    last.then_inc(s_sum, 1)

            def step(g, u, now=False, before=False, last=False):
                if last:
                    sum_pi(g - 2)
                if now:
                    copy_turned(g)
                if before:
                    exp(g - 1)
                if now:
                    keep_w(g, u)

            images(act, step)

        @block.tensor
        def _(pe):
            pe.sem_inc(s_fold, 2)
            for one in (s_turn, s_q, s_xt, s_w, s_sub, s_s, s_p, s_o, s_add, s_add):
                pe.sem_inc(one, 1)

            def turn(g, h):
                pe.wait_ge(s_xt, 1 + 2 * g + h)
                for j in range(RING):
                    pe.wait_ge(s_xd, g * TI + h * RING + j + 1)
                    for b in range(2):
                        last = nc.tensor.transpose(ps_t[b][0:ROWSB[b], j * P:(j + 1) * P],
                                                   xd[:, h * RING + j, c0[b]:c0[b] + ROWSB[b]], ident[:])
                last.then_inc(s_turn, 1)

            def project(g):
                if isinstance(g, int) and g == 0:
                    pe.wait_ge(s_in, 128)
                for h in range(2):
                    pe.wait_ge(s_xt, 1 + 2 * g + h + 1)
                    if not isinstance(g, int) or g > 0:
                        pe.wait_ge(s_w, 1 + 2 * g + h - 1)
                    if not isinstance(g, int) or g > 1:
                        pe.wait_ge(s_sum, 1 + 2 * (g - 2) + h + 1)
                    cols = slice(h * HALF, (h + 1) * HALF)
                    for b in range(2):
                        oc = slice(c0[b], c0[b] + ROWSB[b])
                        nc.tensor.matmul(ps_q[h][b][0:ROWSB[b], :], wq[:, 0, oc], xt[:, 0, cols], start=True, stop=False)
                        last = nc.tensor.matmul(ps_q[h][b][0:ROWSB[b], :], wq[0:CB, 1, oc], xt[0:CB, 1, cols],
                                                start=False, stop=True)
                    last.then_inc(s_q, 1)

            def head_sums(g, u):
                pe.wait_ge(s_r, g + 1)
                pe.wait_ge(s_sub, 1 + g)
                if not isinstance(g, int) or g > 1:
                    pe.wait_ge(s_add, 2 + 4 * (g - 2) + 4)
                for j in range(TI):
                    o = ps_s[:, j * HEADS:(j + 1) * HEADS]
                    tok = slice(j * P, (j + 1) * P)
                    nc.tensor.matmul(o, w2[:, u, 0, tok], rm[:, 0], start=True, stop=False)
                    last = nc.tensor.matmul(o, w2[0:CB, u, 1, tok], rm[0:CB, 1], start=False, stop=True)
                last.then_inc(s_s, 1)

            def turn_pi(g):
                pe.wait_ge(s_pe, g + 1)
                for h in range(2):
                    if isinstance(g, int) and g == NIMG - 1:
                        pe.wait_ge(s_sum, 1 + 2 * g + h - 1)
                    else:
                        pe.wait_ge(s_w, 1 + 2 * g + h + 3)
                    for j in range(RING):
                        for b in range(2):
                            last = nc.tensor.transpose(ps_q[h][b][0:ROWSB[b], j * P:(j + 1) * P],
                                                       pe_[:, h * RING + j, c0[b]:c0[b] + ROWSB[b]], ident[:])
                    last.then_inc(s_p, 1)

            def out_project(g):
                pe.wait_ge(s_fold, 2 + g + 1)
                for r in range(TI // 2):
                    pe.wait_ge(s_add, 4 * g + r + 1)
                    if r == 1 and not (isinstance(g, int) and g == NIMG - 1):
                        pe.wait_ge(s_sub, 1 + g + 2)
                    for j in range(2):
                        o = out_pair[r % 2][:, j * C:(j + 1) * C]
                        tok = slice((2 * r + j) * P, (2 * r + j + 1) * P)
                        nc.tensor.matmul(o, val[:, 0, tok], wos[:, 0], start=True, stop=False)
                        last = nc.tensor.matmul(o, val[0:CB + 1, 1, tok], wos[0:CB + 1, 1], start=False, stop=True)
                    last.then_inc(s_o, 1)

            def step(g, u, now=False, before=False, last=False):
                if last:
                    turn_pi(g - 2)
                if now:
                    turn(g, 0)
                if before:
                    head_sums(g - 1, 1 - u)
                if now:
                    turn(g, 1)
                    project(g)
                if last:
                    out_project(g - 2)

            images(pe, step)


def program(nc, io, out):
    table = nc.dram_tensor("corner_table", (NTOK + FRONT, 4 * C), F32, kind="Internal").ap()
    USED.clear()
    with ExitStack() as ctx:
        k = Kit(nc, ctx, "all")
        X = k.sb("x", [P, T, C])
        Y = k.sb("y", [P, T, C])
        sums = k.sb("sums", [P, 2 * C])
        st = k.sb("st", [P, T, 6])
        ident, ones = k.sb("ident", [P, P]), k.sb("ones", [P, P])
        setup_constants(nc, ident, ones)
        with ExitStack() as early:
            ke = Kit(nc, early, "early")
            bias = ke.sb("bias", [P, 1, NOM])
            xn, free = Y[:, 0:2 * TI, :], Y[:, 2 * TI:, :].rearrange("p t c -> p (t c)")
            n_om, n_grid = T * NOM, 3 * T * K9
            om = free[:, 0:n_om].rearrange("p (t o) -> p t o", o=NOM)
            grid = free[:, n_om:n_om + n_grid].rearrange("p (d n) -> p d n", d=3)
            scratch = free[:, n_om + n_grid:n_om + n_grid + Corners.SCRATCH]
            stage_offsets(nc, io, X, xn, st, ident, om, bias, grid, table)
            stage_deform(nc, io, om, bias, grid, scratch, table, Y, ones, ident, sums)
        stage_batchnorm(nc, io, X, Y, sums, st)
        turned = Y[:].rearrange("p t c -> p (t c)").bitcast(F16).rearrange("p (a n) -> p a n", a=3)
        xh, xl, xb = turned[:, 0], turned[:, 1], turned[:, 2]
        comb_t = nc.dram_tensor("comb_by_expert", (LG, NTOK), F32, kind="Internal").ap()
        with ExitStack() as ffn:
            kf = Kit(nc, ffn, "w0")
            up = [kf.sb(n, [P, HID0], F16) for n in ("ah", "al", "bb")] + [kf.sb("bl", [CB, HID0], F16)]
            down = [kf.sb(n, [P, HID0 // P, C], F16) for n in ("dh", "dl")]
            parts = list(split_up(io["w1_0"], *up)) + list(split_down(io["w2_0"], *down))
            stage_route(nc, io, "route0", X, st, xh, xl, xb, comb_t, ident, 1e-5, io["router0"], E0, 8, parts)
            loads, blk = [], 0
            for e, w in enumerate(W0_WIDTHS):
                loads.append(([(e, 0, P)], [blk + j for j in range(w // P)]))
                blk += w // P
            stage_ffn(nc, "ffn0", X, xh, xl, xb, comb_t, up, None, down, loads, ACT.Gelu_apprx_tanh, st)
        clear_semaphores(nc)
        stage_attention(nc, io, X, st, ident)
        with ExitStack() as ffn:
            kf = Kit(nc, ffn, "w1")
            gate, up = ([kf.sb(f"{g}{n}", [P, HID1], F16) for n in ("ah", "al", "bb")] + [kf.sb(f"{g}bl", [CB, HID1], F16)]
                        for g in ("g", "u"))
            down = [kf.sb(n, [P, HID1 // P, C], F16) for n in ("dh", "dl")]
            parts = []
            for w, routed, shared in ((gate, "wg", "wsg"), (up, "wu", "wsu")):
                parts += split_up(io[routed], *(a[:, 0:HID1R] for a in w))
                parts += split_up(io[shared], *(a[:, HID1R:HID1] for a in w))
            nr = HID1R // P
            parts += split_down(io["wd"], *(a[:, 0:nr] for a in down))
            parts += split_down(io["wsd"], *(a[:, nr:HID1 // P] for a in down))
            stage_route(nc, io, "route1", X, st, xh, xl, xb, comb_t, ident, 1e-5, io["router1"], E1, 2, parts,
                        io["sg_b"])
            loads = []
            for e in range(0, E1, 2):
                b = e // 2 * 3
                loads += [([(e, 0, P)], [b]), ([(e, 0, CB), (e + 1, CB, P)], [b + 1]), ([(e + 1, 0, P)], [b + 2])]
            loads.append(([(E1, 0, P)], list(range(nr, HID1 // P))))
            stage_ffn(nc, "ffn1", X, xh, xl, xb, comb_t, up, gate, down, loads, ACT.Silu, out=out)


def setup_constants(nc, ident, ones):
    with ExitStack() as ctx:
        k = Kit(nc, ctx, "const")
        s = k.sem("set")
        block = ctx.enter_context(nc.Block())

        @block.gpsimd
        def _(pool):
            nc.gpsimd.memset(ident[:], 0.0).then_inc(s, 1)
            nc.gpsimd.memset(ones[:], 1.0)
            pool.wait_ge(s, 1)
            nc.gpsimd.affine_select(out=ident[:], in_=ident[:], compare_op=ALU.not_equal, fill=1.0, base=0,
                                    pattern=[[-1, P]], channel_multiplier=1).then_inc(s, 1)
            pool.wait_ge(s, 2)


def layouts(i):
    f = np.ascontiguousarray
    ar = {k: np.asarray(v) for k, v in i.items()}
    om_w = np.concatenate([ar["L0_conv_off_w"], ar["L0_conv_mask_w"]], 0).reshape(NOM, C, K9).transpose(1, 2, 0)
    p, t, k = np.meshgrid(np.arange(P), np.arange(T), np.arange(K9), indexing="ij")
    grid = np.stack([(t % TI) * ROWS + p // W - 1 + k // 3, p % W - 1 + k % 3,
                     (t // TI) * H * W + FRONT], 1).astype(np.float32)
    return {
        "x": f(ar["x"].reshape(NIMG, C, H * W).transpose(0, 2, 1).reshape(NTOK, C)),
        "om_w": f(om_w.reshape(C, K9 * NOM)),
        "om_b": f(np.concatenate([ar["L0_conv_off_b"], ar["L0_conv_mask_b"]]).reshape(1, NOM)),
        "grid": f(grid.reshape(P, 3, T * K9)),
        "conv_w": f(ar["L0_conv_proj_w"].reshape(C, C, K9).transpose(2, 1, 0).reshape(CONV_K, C)),
        "conv_b": f(ar["L0_conv_proj_b"].reshape(1, C)),
        "gamma": f(ar["L0_conv_gamma"].reshape(1, C)),
        "beta": f(ar["L0_conv_beta"].reshape(1, C)),
        "router0": f(ar["L0_ffn_router_w"].T),
        "w1_0": f(ar["L0_ffn_w1"]),
        "w2_0": f(ar["L0_ffn_w2"]),
        "qkv": f(ar["L1_conv_qkv_w"].T),
        "temp": f(ar["L1_conv_temp"].reshape(1, HEADS)),
        "out_w": f(ar["L1_conv_out_w"].T),
        "out_b": f(ar["L1_conv_out_b"].reshape(1, C)),
        "headmask": f((np.arange(C)[:, None] // DH == np.arange(HEADS)).astype(np.float32)),
        "router1": f(np.concatenate([ar["L1_ffn_router_w"], ar["L1_ffn_sg_w"]], 1)),
        "sg_b": f(ar["L1_ffn_sg_b"].reshape(1, 1)),
        "wg": f(ar["L1_ffn_w_gate"].transpose(1, 0, 2).reshape(C, HID1R)),
        "wu": f(ar["L1_ffn_w_up"].transpose(1, 0, 2).reshape(C, HID1R)),
        "wd": f(ar["L1_ffn_w_down"].reshape(HID1R, C)),
        "wsg": f(ar["L1_ffn_ws_gate"]),
        "wsu": f(ar["L1_ffn_ws_up"]),
        "wsd": f(ar["L1_ffn_ws_down"]),
    }


def kernel(**inputs):
    import concourse.bacc as bacc
    from concourse.bass_utils import run_bass_kernel_spmd

    nc = bacc.Bacc("TRN2", target_bir_lowering=False, num_devices=1)
    arrays = {f"in_{n}": a for n, a in layouts(inputs).items()}
    io = {n[3:]: nc.dram_tensor(n, a.shape, mybir.dt.from_np(a.dtype), kind="ExternalInput").ap()
          for n, a in arrays.items()}
    out = nc.dram_tensor("out", (NTOK, C), F32, kind="ExternalOutput").ap()
    program(nc, io, out)
    got = run_bass_kernel_spmd(nc, [arrays], core_ids=[0]).results[0]["out"]
    return np.ascontiguousarray(got.reshape(NIMG, H * W, C).transpose(0, 2, 1)).reshape(NIMG, C, H, W)
```
